# Optimizing a Trainium2 kernel written in Bass

```python
import numpy as np
import jax
import jax.numpy as jnp

def _softmax(x, axis=-1):
    return jax.nn.softmax(x, axis=axis)

def _gelu(x):
    return jax.nn.gelu(x, approximate=True)

def _silu(x):
    return jax.nn.silu(x)

def _sigmoid(x):
    return jax.nn.sigmoid(x)

def _layernorm(x, axis=-1, eps=1e-05):
    m = jnp.mean(x, axis=axis, keepdims=True)
    v = jnp.var(x, axis=axis, keepdims=True)
    return (x - m) / jnp.sqrt(v + eps)

def _scatter_add(tgt, idx, src, axis=0):
    return tgt.at[idx].add(src)

def _segment_sum(src, seg, n):
    return jax.ops.segment_sum(src, seg, n)
kernel_name = 'mk_xattn_ffn_d2_seqx_r8_957b13'

def setup_inputs(seed: int=0):
    np.random.seed(seed)
    _w = jnp.asarray

    def _rec_inputs():
        import jax
        import jax.numpy as jnp
        _rk = jax.random.key(seed)
        x = 7.22e-05 + 1 * jax.random.normal(jax.random.fold_in(_rk, 1), (4, 256, 256), jnp.float32)
        _lenS = 256 - jax.random.randint(jax.random.fold_in(_rk, 7), (4,), 0, max(1, 256 // 4) + 1, jnp.int32)
        _lenS2 = 256 - jax.random.randint(jax.random.fold_in(_rk, 8), (4,), 0, max(1, 256 // 4) + 1, jnp.int32)
        _ctx_1024P = jax.random.normal(jax.random.fold_in(_rk, 11), (4, 16, 128), jnp.float32)
        _ctx_1024c = jax.random.dirichlet(jax.random.fold_in(_rk, 511), 0.3 * jnp.ones((16,), jnp.float32), (4, 256))
        _ctx_1024t = jnp.einsum('bsk,bkd->bsd', _ctx_1024c, _ctx_1024P)
        _ctx_1024t = _ctx_1024t * jax.lax.rsqrt(jnp.mean(jnp.square(_ctx_1024t)) + 1e-12) * 0.953939
        ctx_1024 = -1.39393e-06 + 0.999914 * (_ctx_1024t + 0.3 * jax.random.normal(jax.random.fold_in(_rk, 611), (4, 256, 128), jnp.float32))
        fside_BxSx2_0 = jax.random.uniform(jax.random.fold_in(_rk, 12), (4, 256, 2), jnp.float32, 0.0, 0.999707)
        return (x, ctx_1024, fside_BxSx2_0)
    x, ctx_1024, fside_BxSx2_0 = _rec_inputs()

    def _L0_xattn_setup():
        import jax, jax.numpy as jnp
        import numpy as np
        DIM = 256
        CTX_DIM = 128
        N_HEADS = 32
        HEAD_DIM = DIM // N_HEADS
        POS_DIM = 2
        B, N, CTXN = (2, 256, 256)
        ROPE_BASE = 10000.0

        def apply_axial_rope(x, pos):
            b, n, h, d = x.shape
            p = pos.shape[-1]
            dpa = d // p
            half = dpa // 2
            freqs = ROPE_BASE ** (-jnp.arange(half, dtype=x.dtype) / half)
            ang = pos[..., :, None] * freqs
            cos = jnp.cos(ang)[:, :, None, :, :]
            sin = jnp.sin(ang)[:, :, None, :, :]
            xr = x.reshape(b, n, h, p, half, 2)
            x1, x2 = (xr[..., 0], xr[..., 1])
            out = jnp.stack([x1 * cos - x2 * sin, x1 * sin + x2 * cos], axis=-1)
            return out.reshape(b, n, h, d)
        key = jax.random.key(seed)
        ks = jax.random.split(key, 8)
        x = jax.random.normal(ks[0], (B, N, DIM), jnp.float32)
        ctx = jax.random.normal(ks[1], (B, CTXN, CTX_DIM), jnp.float32)
        pos_map = jax.random.uniform(ks[2], (B, N, POS_DIM), jnp.float32)
        ctx_pos_map = jax.random.uniform(ks[3], (B, CTXN, POS_DIM), jnp.float32)
        Wq = jax.random.normal(ks[4], (DIM, DIM), jnp.float32) / np.sqrt(DIM)
        Wkv = jax.random.normal(ks[5], (CTX_DIM, 2 * DIM), jnp.float32) / np.sqrt(CTX_DIM)
        Wout = jax.random.normal(ks[6], (DIM, DIM), jnp.float32) / np.sqrt(DIM)
        bout = jnp.zeros((DIM,), jnp.float32)
        return {'x': x, 'ctx': ctx, 'pos_map': pos_map, 'ctx_pos_map': ctx_pos_map, 'Wq': Wq, 'Wkv': Wkv, 'Wout': Wout, 'bout': bout}
    _L0_xattn_all = _L0_xattn_setup()
    _L0_xattn_in = {k: v for k, v in _L0_xattn_all.items() if k in ('Wq', 'Wkv', 'Wout', 'bout')}
    del _L0_xattn_all

    def _L0_ffn_setup():
        import jax, jax.numpy as jnp
        import numpy as np
        HIDDEN = 256
        MOE_INTER = 128
        SHARED_INTER = 512
        N_EXPERTS = 16
        TOP_K = 2
        N_GROUP = 4
        TOPK_GROUP = 2
        NORM_TOPK_PROB = True
        ROUTED_SCALING = 1.0

        def relu2(x):
            r = jax.nn.relu(x)
            return r * r

        def _get_topk_indices(scores, e_bias):
            T, E = scores.shape
            s = scores + e_bias[None, :]
            gsz = E // N_GROUP
            group_scores = jax.lax.top_k(s.reshape(T, N_GROUP, gsz), 2)[0].sum(-1)
            group_idx = jax.lax.top_k(group_scores, TOPK_GROUP)[1]
            group_mask = jnp.zeros((T, N_GROUP), dtype=bool).at[jnp.arange(T)[:, None], group_idx].set(True)
            score_mask = jnp.repeat(group_mask, gsz, axis=1)
            masked = jnp.where(score_mask, s, 0.0)
            topk_indices = jax.lax.top_k(masked, TOP_K)[1]
            return jax.lax.stop_gradient(topk_indices)

        def _router(x_flat, router_weight, e_bias):
            logits = jnp.einsum('th,eh->te', x_flat.astype(jnp.float32), router_weight.astype(jnp.float32))
            scores = jax.nn.sigmoid(logits)
            topk_indices = _get_topk_indices(scores, e_bias)
            topk_weights = jnp.take_along_axis(scores, topk_indices, axis=1)
            if NORM_TOPK_PROB:
                topk_weights = topk_weights / (topk_weights.sum(-1, keepdims=True) + 1e-20)
            return (topk_indices, topk_weights * ROUTED_SCALING)
        key = jax.random.key(seed)
        ks = jax.random.split(key, 6)
        s = 0.02
        hidden_states = jax.random.normal(ks[0], (1, 256, HIDDEN), dtype=jnp.float32)
        router_weight = jax.random.normal(ks[1], (N_EXPERTS, HIDDEN), dtype=jnp.float32) * s
        e_bias = jnp.zeros((N_EXPERTS,), dtype=jnp.float32)
        w_up = jax.random.normal(ks[2], (N_EXPERTS, HIDDEN, MOE_INTER), dtype=jnp.float32) * s
        w_down = jax.random.normal(ks[3], (N_EXPERTS, MOE_INTER, HIDDEN), dtype=jnp.float32) * s
        shared_up = jax.random.normal(ks[4], (HIDDEN, SHARED_INTER), dtype=jnp.float32) * s
        shared_down = jax.random.normal(ks[5], (SHARED_INTER, HIDDEN), dtype=jnp.float32) * s
        return {'hidden_states': hidden_states, 'router_weight': router_weight, 'e_bias': e_bias, 'w_up': w_up, 'w_down': w_down, 'shared_up': shared_up, 'shared_down': shared_down}
    _L0_ffn_all = _L0_ffn_setup()
    _L0_ffn_in = {k: v for k, v in _L0_ffn_all.items() if k in ('router_weight', 'e_bias', 'w_up', 'w_down', 'shared_up', 'shared_down')}
    del _L0_ffn_all

    def _L1_xattn_setup():
        import jax, jax.numpy as jnp
        import numpy as np
        B, S1, S2, DCA = (2, 256, 128, 16)
        QDIM, KDIM, H = (256, 128, 16)
        HD = QDIM // H
        SCALE = HD ** (-0.5)
        EPS = 1e-06
        DCA_WEIGHT = 1.0

        def _ln(t, w, b):
            m = jnp.mean(t, axis=-1, keepdims=True)
            v = jnp.var(t, axis=-1, keepdims=True)
            return (t - m) * jax.lax.rsqrt(v + EPS) * w + b

        def _attn(q, k, v):
            s = jnp.einsum('bhqd,bhkd->bhqk', q, k) * SCALE
            p = jax.nn.softmax(s, axis=-1)
            return jnp.einsum('bhqk,bhkd->bhqd', p, v)
        key = jax.random.key(seed)
        ks = jax.random.split(key, 8)
        w = lambda k, shape: jax.random.normal(k, shape, jnp.float32) * 0.02
        return {'x': jax.random.normal(ks[0], (B, S1, QDIM), jnp.float32), 'y': jax.random.normal(ks[1], (B, S2 + DCA, KDIM), jnp.float32), 'Wq': w(ks[2], (QDIM, QDIM)), 'bq': jnp.zeros((QDIM,), jnp.float32), 'Wk': w(ks[3], (KDIM, QDIM)), 'bk': jnp.zeros((QDIM,), jnp.float32), 'Wv': w(ks[4], (KDIM, QDIM)), 'bv': jnp.zeros((QDIM,), jnp.float32), 'Wkv_dca': w(ks[5], (KDIM, 2 * QDIM)), 'bkv_dca': jnp.zeros((2 * QDIM,), jnp.float32), 'qn_w': jnp.ones((HD,), jnp.float32), 'qn_b': jnp.zeros((HD,), jnp.float32), 'kn_w': jnp.ones((HD,), jnp.float32), 'kn_b': jnp.zeros((HD,), jnp.float32), 'kn_dca_w': jnp.ones((HD,), jnp.float32), 'kn_dca_b': jnp.zeros((HD,), jnp.float32), 'Wo': w(ks[6], (QDIM, QDIM)), 'bo': jnp.zeros((QDIM,), jnp.float32)}
    _L1_xattn_all = _L1_xattn_setup()
    _L1_xattn_in = {k: v for k, v in _L1_xattn_all.items() if k in ('Wq', 'bq', 'Wk', 'bk', 'Wv', 'bv', 'Wkv_dca', 'bkv_dca', 'qn_w', 'qn_b', 'kn_w', 'kn_b', 'kn_dca_w', 'kn_dca_b', 'Wo', 'bo')}
    del _L1_xattn_all

    def _L1_ffn_setup():
        import jax, jax.numpy as jnp
        import numpy as np
        TOP_K = 4
        key = jax.random.key(seed)
        ks = jax.random.split(key, 8)
        B, S, H = (1, 128, 256)
        E, I = (60, 176)
        I_SH = 704
        s = 0.02
        return {'hidden_states': jax.random.normal(ks[0], (B, S, H), jnp.float32), 'gate_w': jax.random.normal(ks[1], (E, H), jnp.float32) * s, 'shared_gate_w': jax.random.normal(ks[2], (1, H), jnp.float32) * s, 'w13': jax.random.normal(ks[3], (E, 2 * I, H), jnp.float32) * s, 'w2': jax.random.normal(ks[4], (E, H, I), jnp.float32) * s, 'se_gate_up_w': jax.random.normal(ks[5], (2 * I_SH, H), jnp.float32) * s, 'se_down_w': jax.random.normal(ks[6], (H, I_SH), jnp.float32) * s}
    _L1_ffn_all = _L1_ffn_setup()
    _L1_ffn_in = {k: v for k, v in _L1_ffn_all.items() if k in ('gate_w', 'shared_gate_w', 'w13', 'w2', 'se_gate_up_w', 'se_down_w')}
    del _L1_ffn_all
    return {'x': x, 'ctx_1024': ctx_1024, 'fside_BxSx2_0': fside_BxSx2_0, 'L0_xattn_Wq': _L0_xattn_in['Wq'], 'L0_xattn_Wkv': _L0_xattn_in['Wkv'], 'L0_xattn_Wout': _L0_xattn_in['Wout'], 'L0_xattn_bout': _L0_xattn_in['bout'], 'L0_ffn_router_weight': _L0_ffn_in['router_weight'], 'L0_ffn_e_bias': _L0_ffn_in['e_bias'], 'L0_ffn_w_up': _L0_ffn_in['w_up'], 'L0_ffn_w_down': _L0_ffn_in['w_down'], 'L0_ffn_shared_up': _L0_ffn_in['shared_up'], 'L0_ffn_shared_down': _L0_ffn_in['shared_down'], 'L1_xattn_Wq': _L1_xattn_in['Wq'], 'L1_xattn_bq': _L1_xattn_in['bq'], 'L1_xattn_Wk': _L1_xattn_in['Wk'], 'L1_xattn_bk': _L1_xattn_in['bk'], 'L1_xattn_Wv': _L1_xattn_in['Wv'], 'L1_xattn_bv': _L1_xattn_in['bv'], 'L1_xattn_Wkv_dca': _L1_xattn_in['Wkv_dca'], 'L1_xattn_bkv_dca': _L1_xattn_in['bkv_dca'], 'L1_xattn_qn_w': _L1_xattn_in['qn_w'], 'L1_xattn_qn_b': _L1_xattn_in['qn_b'], 'L1_xattn_kn_w': _L1_xattn_in['kn_w'], 'L1_xattn_kn_b': _L1_xattn_in['kn_b'], 'L1_xattn_kn_dca_w': _L1_xattn_in['kn_dca_w'], 'L1_xattn_kn_dca_b': _L1_xattn_in['kn_dca_b'], 'L1_xattn_Wo': _L1_xattn_in['Wo'], 'L1_xattn_bo': _L1_xattn_in['bo'], 'L1_ffn_gate_w': _L1_ffn_in['gate_w'], 'L1_ffn_shared_gate_w': _L1_ffn_in['shared_gate_w'], 'L1_ffn_w13': _L1_ffn_in['w13'], 'L1_ffn_w2': _L1_ffn_in['w2'], 'L1_ffn_se_gate_up_w': _L1_ffn_in['se_gate_up_w'], 'L1_ffn_se_down_w': _L1_ffn_in['se_down_w']}

def reference(x, ctx_1024, fside_BxSx2_0, L0_xattn_Wq, L0_xattn_Wkv, L0_xattn_Wout, L0_xattn_bout, L0_ffn_router_weight, L0_ffn_e_bias, L0_ffn_w_up, L0_ffn_w_down, L0_ffn_shared_up, L0_ffn_shared_down, L1_xattn_Wq, L1_xattn_bq, L1_xattn_Wk, L1_xattn_bk, L1_xattn_Wv, L1_xattn_bv, L1_xattn_Wkv_dca, L1_xattn_bkv_dca, L1_xattn_qn_w, L1_xattn_qn_b, L1_xattn_kn_w, L1_xattn_kn_b, L1_xattn_kn_dca_w, L1_xattn_kn_dca_b, L1_xattn_Wo, L1_xattn_bo, L1_ffn_gate_w, L1_ffn_shared_gate_w, L1_ffn_w13, L1_ffn_w2, L1_ffn_se_gate_up_w, L1_ffn_se_down_w):
    import jax
    import jax.numpy as jnp

    def _L0_xattn_ref(x, ctx, pos_map, ctx_pos_map, Wq, Wkv, Wout, bout):
        import jax, jax.numpy as jnp
        import numpy as np
        DIM = 256
        CTX_DIM = 128
        N_HEADS = 32
        HEAD_DIM = DIM // N_HEADS
        POS_DIM = 2
        B, N, CTXN = (2, 256, 256)
        ROPE_BASE = 10000.0

        def apply_axial_rope(x, pos):
            b, n, h, d = x.shape
            p = pos.shape[-1]
            dpa = d // p
            half = dpa // 2
            freqs = ROPE_BASE ** (-jnp.arange(half, dtype=x.dtype) / half)
            ang = pos[..., :, None] * freqs
            cos = jnp.cos(ang)[:, :, None, :, :]
            sin = jnp.sin(ang)[:, :, None, :, :]
            xr = x.reshape(b, n, h, p, half, 2)
            x1, x2 = (xr[..., 0], xr[..., 1])
            out = jnp.stack([x1 * cos - x2 * sin, x1 * sin + x2 * cos], axis=-1)
            return out.reshape(b, n, h, d)
        b, n, _ = x.shape
        ctx_n = ctx.shape[1]
        q = (x @ Wq).reshape(b, n, N_HEADS, HEAD_DIM)
        k, v = jnp.split(ctx @ Wkv, 2, axis=-1)
        k = k.reshape(b, ctx_n, N_HEADS, HEAD_DIM)
        v = v.reshape(b, ctx_n, N_HEADS, HEAD_DIM)
        q = apply_axial_rope(q, pos_map)
        k = apply_axial_rope(k, ctx_pos_map)
        scale = 1.0 / np.sqrt(HEAD_DIM).astype(np.float32)
        logits = jnp.einsum('bqhd,bkhd->bhqk', q, k) * scale
        w = jax.nn.softmax(logits, axis=-1)
        attn = jnp.einsum('bhqk,bkhd->bqhd', w, v)
        attn = attn.reshape(b, n, N_HEADS * HEAD_DIM)
        return attn @ Wout + bout

    def _L0_ffn_ref(hidden_states, router_weight, e_bias, w_up, w_down, shared_up, shared_down):
        import jax, jax.numpy as jnp
        import numpy as np
        HIDDEN = 256
        MOE_INTER = 128
        SHARED_INTER = 512
        N_EXPERTS = 16
        TOP_K = 2
        N_GROUP = 4
        TOPK_GROUP = 2
        NORM_TOPK_PROB = True
        ROUTED_SCALING = 1.0

        def relu2(x):
            r = jax.nn.relu(x)
            return r * r

        def _get_topk_indices(scores, e_bias):
            T, E = scores.shape
            s = scores + e_bias[None, :]
            gsz = E // N_GROUP
            group_scores = jax.lax.top_k(s.reshape(T, N_GROUP, gsz), 2)[0].sum(-1)
            group_idx = jax.lax.top_k(group_scores, TOPK_GROUP)[1]
            group_mask = jnp.zeros((T, N_GROUP), dtype=bool).at[jnp.arange(T)[:, None], group_idx].set(True)
            score_mask = jnp.repeat(group_mask, gsz, axis=1)
            masked = jnp.where(score_mask, s, 0.0)
            topk_indices = jax.lax.top_k(masked, TOP_K)[1]
            return jax.lax.stop_gradient(topk_indices)

        def _router(x_flat, router_weight, e_bias):
            logits = jnp.einsum('th,eh->te', x_flat.astype(jnp.float32), router_weight.astype(jnp.float32))
            scores = jax.nn.sigmoid(logits)
            topk_indices = _get_topk_indices(scores, e_bias)
            topk_weights = jnp.take_along_axis(scores, topk_indices, axis=1)
            if NORM_TOPK_PROB:
                topk_weights = topk_weights / (topk_weights.sum(-1, keepdims=True) + 1e-20)
            return (topk_indices, topk_weights * ROUTED_SCALING)
        orig_shape = hidden_states.shape
        x = hidden_states.reshape(-1, HIDDEN)
        T = x.shape[0]
        topk_indices, topk_weights = _router(x, router_weight, e_bias)
        combine = jnp.zeros((T, N_EXPERTS), dtype=topk_weights.dtype).at[jnp.arange(T)[:, None], topk_indices].add(topk_weights)
        h1 = jnp.einsum('th,ehi->tei', x, w_up)
        a = relu2(h1) * combine[:, :, None]
        routed = jnp.einsum('tei,eih->th', a, w_down)
        shared = relu2(hidden_states @ shared_up) @ shared_down
        return routed.reshape(orig_shape) + shared

    def _L1_xattn_ref(x, y, Wq, bq, Wk, bk, Wv, bv, Wkv_dca, bkv_dca, qn_w, qn_b, kn_w, kn_b, kn_dca_w, kn_dca_b, Wo, bo):
        import jax, jax.numpy as jnp
        import numpy as np
        B, S1, S2, DCA = (2, 256, 128, 16)
        QDIM, KDIM, H = (256, 128, 16)
        HD = QDIM // H
        SCALE = HD ** (-0.5)
        EPS = 1e-06
        DCA_WEIGHT = 1.0

        def _ln(t, w, b):
            m = jnp.mean(t, axis=-1, keepdims=True)
            v = jnp.var(t, axis=-1, keepdims=True)
            return (t - m) * jax.lax.rsqrt(v + EPS) * w + b

        def _attn(q, k, v):
            s = jnp.einsum('bhqd,bhkd->bhqk', q, k) * SCALE
            p = jax.nn.softmax(s, axis=-1)
            return jnp.einsum('bhqk,bhkd->bhqd', p, v)
        b, s1, _ = x.shape
        y_dca = y[:, -DCA:, :]
        y_main = y[:, :-DCA, :]
        kv_dca = (y_dca @ Wkv_dca + bkv_dca).reshape(b, DCA, 2, H, HD)
        k_dca = _ln(kv_dca[:, :, 0], kn_dca_w, kn_dca_b)
        v_dca = kv_dca[:, :, 1]
        s2 = y_main.shape[1]
        q = _ln((x @ Wq + bq).reshape(b, s1, H, HD), qn_w, qn_b)
        kv = jnp.concatenate([y_main @ Wk + bk, y_main @ Wv + bv], axis=-1)
        kv = kv.reshape(b, s2, H, 2 * HD)
        k = _ln(kv[..., :HD], kn_w, kn_b)
        v = kv[..., HD:]
        qT = q.transpose(0, 2, 1, 3)
        ctx = _attn(qT, k.transpose(0, 2, 1, 3), v.transpose(0, 2, 1, 3))
        ctx = ctx.transpose(0, 2, 1, 3).reshape(b, s1, QDIM)
        ctx_dca = _attn(qT, k_dca.transpose(0, 2, 1, 3), v_dca.transpose(0, 2, 1, 3))
        ctx_dca = ctx_dca.transpose(0, 2, 1, 3).reshape(b, s1, QDIM)
        ctx = ctx + DCA_WEIGHT * ctx_dca
        return ctx @ Wo + bo

    def _L1_ffn_ref(hidden_states, gate_w, shared_gate_w, w13, w2, se_gate_up_w, se_down_w):
        import jax, jax.numpy as jnp
        import numpy as np
        TOP_K = 4
        orig_shape = hidden_states.shape
        E, H = gate_w.shape
        I = w2.shape[2]
        x = hidden_states.reshape(-1, H)
        M = x.shape[0]
        gu = x @ se_gate_up_w.T
        I_sh = se_down_w.shape[1]
        shared = jax.nn.silu(gu[:, :I_sh]) * gu[:, I_sh:] @ se_down_w.T
        shared = shared * jax.nn.sigmoid(x @ shared_gate_w.T)
        logits = x @ gate_w.T
        probs = jax.nn.softmax(logits.astype(jnp.float32), axis=-1)
        weights, sel = jax.lax.top_k(probs, TOP_K)
        cw = jnp.zeros((M, E), jnp.float32).at[jnp.arange(M)[:, None], sel].add(weights)

        def step(acc, ews):
            w13_e, w2_e, cw_e = ews
            gu_e = x @ w13_e.T
            h = jax.nn.silu(gu_e[:, :I]) * gu_e[:, I:]
            return (acc + cw_e[:, None] * (h @ w2_e.T), None)
        sparse, _ = jax.lax.scan(step, jnp.zeros((M, H), jnp.float32), (w13, w2, cw.T))
        return (shared + sparse).reshape(orig_shape)
    x = x + _L0_xattn_ref(_layernorm(x, axis=-1), ctx_1024, fside_BxSx2_0, fside_BxSx2_0, L0_xattn_Wq, L0_xattn_Wkv, L0_xattn_Wout, L0_xattn_bout)
    x = x + _L0_ffn_ref(_layernorm(x, axis=-1), L0_ffn_router_weight, L0_ffn_e_bias, L0_ffn_w_up, L0_ffn_w_down, L0_ffn_shared_up, L0_ffn_shared_down)
    x = x + _L1_xattn_ref(_layernorm(x, axis=-1), ctx_1024, L1_xattn_Wq, L1_xattn_bq, L1_xattn_Wk, L1_xattn_bk, L1_xattn_Wv, L1_xattn_bv, L1_xattn_Wkv_dca, L1_xattn_bkv_dca, L1_xattn_qn_w, L1_xattn_qn_b, L1_xattn_kn_w, L1_xattn_kn_b, L1_xattn_kn_dca_w, L1_xattn_kn_dca_b, L1_xattn_Wo, L1_xattn_bo)
    x = x + _L1_ffn_ref(_layernorm(x, axis=-1), L1_ffn_gate_w, L1_ffn_shared_gate_w, L1_ffn_w13, L1_ffn_w2, L1_ffn_se_gate_up_w, L1_ffn_se_down_w)
    return x

_drawn_inputs = setup_inputs


def setup_inputs(seed=0):
    import zlib

    import numpy as np

    out = dict(_drawn_inputs(seed))
    spreads = {'L0_xattn_bout': (0.0, 0.1),
     'L0_ffn_e_bias': (0.0, 0.382),
     'L1_xattn_bq': (0.0, 0.8),
     'L1_xattn_bk': (0.0, 0.399),
     'L1_xattn_bv': (0.0, 0.428),
     'L1_xattn_bkv_dca': (0.0, 0.268),
     'L1_xattn_qn_w': (1.0, 0.6),
     'L1_xattn_qn_b': (0.0, 0.8),
     'L1_xattn_kn_w': (1.0, 0.6),
     'L1_xattn_kn_b': (0.0, 0.8),
     'L1_xattn_kn_dca_w': (1.0, 0.6),
     'L1_xattn_kn_dca_b': (0.0, 0.8),
     'L1_xattn_bo': (0.0, 0.1)}
    factors = {'L0_ffn_router_weight': 4.696,
     'L0_ffn_w_up': 3.58,
     'L0_ffn_w_down': 3.218,
     'L1_xattn_Wq': 2.794,
     'L1_ffn_gate_w': 8.0,
     'L1_ffn_shared_gate_w': 8.0,
     'L1_ffn_w13': 8.0,
     'L1_ffn_w2': 8.0,
     'L1_ffn_se_gate_up_w': 4.4,
     'L1_ffn_se_down_w': 4.334}
    for name, (base, spread) in spreads.items():
        noise = np.random.default_rng([zlib.crc32(name.encode()), seed]).standard_normal(out[name].shape)
        drawn = base * np.exp(spread * noise) if base else spread * noise
        out[name] = jnp.asarray(drawn.astype(out[name].dtype))
    for name, factor in factors.items():
        out[name] = (out[name] * factor).astype(out[name].dtype)
    return out
```

```python
from contextlib import ExitStack

import numpy as np

import concourse.bass as bass
from concourse import mybir
from concourse.alu_op_type import AluOpType as ALU

ACT = mybir.ActivationFunctionType
F32 = mybir.dt.float32
BF16 = mybir.dt.bfloat16
U32 = mybir.dt.uint32
AX_X = mybir.AxisListType.X

P = 128
D = 256
KD = D // P
B = 4
S = 256
T = B * S
NT = T // P
QT = S // P
CD = 128
G = 8
PARTS = 6
Q_PART = (0, 0, 1, 0, 1, 2)
K_PART = (0, 1, 0, 2, 1, 0)
DCA = 16
MAIN = S - DCA
ROUNDER = 1.5 * 2.0 ** 23
PI_BELOW = 3.1415925


def bcast(ap, axis, n):
    a = ap.unsqueeze(axis)
    shape = list(a.shape)
    shape[axis] = n
    return a.broadcast_to(shape)


class Layer:

    def __init__(self, name, heads, shifts, scale):
        self.name = name
        self.heads = heads
        self.hd = D // heads
        self.rows = PARTS * self.hd
        self.shifts = shifts
        self.krows = self.rows + 2 * shifts
        self.vw = shifts * (self.hd + 1)
        self.scale = scale
        self.groups = heads // G
        self.units = B * self.groups

    def stack(self, m, src):
        return m.stacks[self.name, src]


L0 = Layer("l0", 32, 1, float(1.0 / np.sqrt(np.float32(8))))
L1 = Layer("l1", 16, 2, 0.25)


class Chain:

    def __init__(self, eng, sem, base=0):
        self.eng, self.sem, self.base, self.n = eng, sem, base, 0

    def link(self, ins):
        self.n += 1
        ins.then_inc(self.sem, 1)
        self.eng.wait_ge(self.sem, self.base + self.n)


class Mem:

    def __init__(self, nc, ctx):
        self.nc, self.ctx = nc, ctx
        self.stage_sems, self.old_sems = [], []

    def sb(self, name, shape, dt=F32, ctx=None):
        return (ctx or self.ctx).enter_context(self.nc.sbuf_tensor(name, shape, dt))

    def sem(self, name, ctx=None):
        s = (ctx or self.ctx).enter_context(self.nc.semaphore(name))
        if ctx is not None:
            self.stage_sems.append(s)
        return s

    def clear_sems(self, dve):
        for s in self.old_sems:
            dve.sem_clear(s)
        self.old_sems = []


def rsqrt_vector(nc, dve, chain, var, eps, work, root_in, root_out):
    v, y, r, t = work
    if eps is not None:
        chain.link(nc.vector.tensor_scalar(v, var, eps, None, ALU.add))
    nc.vector.reciprocal(t, v).then_inc(root_in, 1)
    dve.wait_ge(root_out, 1)
    chain.link(nc.vector.tensor_tensor(t, y, y, ALU.mult))
    chain.link(nc.vector.tensor_tensor(r, t, v, ALU.mult))
    chain.link(nc.vector.tensor_scalar(t, r, -0.5, 1.5, ALU.mult, ALU.add))
    chain.link(nc.vector.tensor_tensor(r, y, t, ALU.mult))


def layernorm_vector(nc, dve, chain, m, eps, root_in, root_out, xn_ready):
    for i in range(NT):
        ins = nc.vector.bn_stats(m.bn[:, i, :], m.xs[:, i, :])
    chain.link(ins)
    for i in range(NT):
        ins = nc.vector.bn_aggr(m.mv[:, i, :], m.bn[:, i, :])
    chain.link(ins)
    rsqrt_vector(nc, dve, chain, m.mv[:, :, 1], eps, [m.rstd[:, j, :] for j in range(4)], root_in, root_out)
    for i in range(NT):
        nc.vector.tensor_scalar(m.xn[:, i, :], m.xs[:, i, :], m.mv[:, i, 0:1], m.rstd[:, 2, i:i + 1],
                                ALU.subtract, ALU.mult).then_inc(xn_ready, 1)


def layernorm_scalar(nc, act, m, root_in, root_out):
    act.wait_ge(root_in, 1)
    nc.scalar.activation(m.rstd[:, 1, :], m.rstd[:, 3, :], ACT.Sqrt).then_inc(root_out, 1)


def transpose_tile(nc, m, bank, src):
    for c in range(KD):
        ins = nc.tensor.transpose(m.ps[:, bank, c * P:(c + 1) * P], src[:, c * P:(c + 1) * P], m.ident[:])
    return ins


def transposed_copy(nc, m, i, bank, dst):
    return nc.scalar.copy(dst[:, :, i * P:(i + 1) * P],
                          m.ps[:, bank, 0:D].rearrange("p (c t) -> p c t", c=KD))


def matmul_tile(nc, out, xT, i, w, bias=None, ones=None):
    for c in range(KD):
        ins = nc.tensor.matmul(out, xT[:, c, i * P:(i + 1) * P], w[:, c, :], start=(c == 0),
                               stop=(c == KD - 1 and bias is None))
    if bias is not None:
        ins = nc.tensor.matmul(out, ones, bias, start=False, stop=True)
    return ins


SPLITS = [(src, half, th) for src in ("k", "q") for half in range(KD) for th in range(2)]
SW = 4 * P
WRITES = 2 * PARTS


def split_tensor(nc, pe, m, s, tiles_ready, parts_taken):
    src, half, th = SPLITS[s]
    tile = m.k_tm if src == "k" else m.q_tm
    pe.wait_ge(tiles_ready, (0 if src == "k" else NT) + 4 * th + 4)
    if s >= 2:
        pe.wait_ge(parts_taken, s - 1)
    for j in range(4):
        ins = nc.tensor.transpose(m.ps[:, 6 + s % 2, j * P:(j + 1) * P],
                                  tile[:, 4 * th + j, half * P:(half + 1) * P], m.ident[:])
    return ins


def split_writes(sp, m, lay, s, part_dma):
    src, half, th = SPLITS[s]
    heads = P // lay.hd
    for j, part in enumerate(Q_PART if src == "q" else K_PART):
        for b in range(2):
            rows = lay.stack(m, src)[2 * th + b, j * lay.hd:(j + 1) * lay.hd, half * heads:(half + 1) * heads, :]
            sp.dma_start(rows.rearrange("d h t -> h d t"),
                         m.part[:, s % 2, part, b * S:(b + 1) * S]).then_inc(part_dma[s % 2], 16)


def prep_l0(nc, m, io):
    lay = L0
    with ExitStack() as ctx:
        def sem(n):
            return m.sem("p0_" + n, ctx)
        wq = m.sb("p0_wq", [P, KD, D], ctx=ctx)
        wkv = m.sb("p0_wkv", [P, 2 * D], ctx=ctx)
        ang = m.sb("p0_ang", [P, 2, NT, 4], ctx=ctx)
        trig = m.sb("p0_trig", [P, 2, NT, 4], ctx=ctx)
        turns = m.sb("p0_turns", [P, 2, NT, 4], ctx=ctx)
        pos = m.sb("p0_pos", [P, NT, 2], ctx=ctx)
        rot = m.sb("p0_rot", [P, 2, 2, D], ctx=ctx)
        ld_const, ld_x, ld_ctx, ld_wkv, ld_wq, ld_pos = (sem(n) for n in (
            "ld_const", "ld_x", "ld_ctx", "ld_wkv", "ld_wq", "ld_pos"))
        step, xn_ready, xt_ps, xt_ready = sem("step"), sem("xn_ready"), sem("xt_ps"), sem("xt_ready")
        kv_ps, v_copied, q_ps, rot_ready, rot_done = (sem(n) for n in (
            "kv_ps", "v_copied", "q_ps", "rot_ready", "rot_done"))
        ang_ready, trig_ready, root_in, root_out = (sem(n) for n in ("ang_ready", "trig_ready", "root_in", "root_out"))
        split_ps, hi_ready, rest_ready, mid_ready, lo_ready, ones_set = (sem(n) for n in (
            "split_ps", "hi_ready", "rest_ready", "mid_ready", "lo_ready", "ones_set"))
        part_dma = [sem("part_dma0"), sem("part_dma1")]
        ps = m.ps
        block = ctx.enter_context(nc.Block())

        @block.sync
        def _(sp):
            sp.dma_start(m.xs[:], io["x"].rearrange("b (i p) d -> p (b i) d", p=P)).then_inc(ld_x, 16)
            for dst, name in ((m.ident, "ident"), (m.ones_row, "ones_row")):
                sp.dma_start(dst[:], io[name]).then_inc(ld_const, 16)
            sp.dma_start(m.ctxT[:], io["ctxT"]).then_inc(ld_ctx, 16)
            sp.dma_start(wkv[:], io["L0_xattn_Wkv"]).then_inc(ld_wkv, 16)
            sp.dma_start(pos[:], io["fside_BxSx2_0"].rearrange("b (i p) c -> p (b i) c", p=P)).then_inc(ld_pos, 16)
            sp.dma_start(wq[:], io["L0_xattn_Wq"].rearrange("(c p) n -> p c n", p=P)).then_inc(ld_wq, 16)
            for s in range(len(SPLITS)):
                sp.wait_ge(lo_ready, s + 1)
                sp.wait_ge(mid_ready, s + 1)
                split_writes(sp, m, lay, s, part_dma)
            for b in range(2):
                sp.wait_ge(part_dma[b], 16 * WRITES * len(SPLITS) // 2)

        @block.tensor
        def _(pe):
            pe.wait_ge(ld_ctx, 16)
            pe.wait_ge(ld_wkv, 16)
            for i in range(NT):
                if i >= 2:
                    pe.wait_ge(v_copied, i - 1)
                    pe.wait_ge(rot_ready, i - 1)
                for side in range(2):
                    ins = nc.tensor.matmul(ps[:, 2 * side + i % 2, 0:D], m.ctxT[:, i * P:(i + 1) * P],
                                           wkv[:, side * D:(side + 1) * D], start=True, stop=True)
                ins.then_inc(kv_ps, 1)
            pe.wait_ge(v_copied, NT)
            pe.wait_ge(ld_const, 32)
            pe.wait_ge(ld_wq, 16)
            for i in range(NT + 1):
                if i < NT:
                    pe.wait_ge(xn_ready, i + 1)
                    if i >= 2:
                        pe.wait_ge(xt_ready, i - 1)
                    transpose_tile(nc, m, 2 + i % 2, m.xn[:, i, :]).then_inc(xt_ps, 1)
                if i >= 1:
                    t = i - 1
                    pe.wait_ge(xt_ready, t + 1)
                    if t >= 2:
                        pe.wait_ge(rot_ready, NT + t - 1)
                    matmul_tile(nc, ps[:, 4 + t % 2, 0:D], m.xT, t, wq).then_inc(q_ps, 1)
            for s in range(len(SPLITS)):
                split_tensor(nc, pe, m, s, rot_done, rest_ready).then_inc(split_ps, 1)

        @block.vector
        def _(dve):
            chain = Chain(dve, step)
            dve.wait_ge(ld_pos, 16)
            for f, freq in enumerate((1.0, 10000.0 ** -0.5)):
                for k, phase in enumerate((0.0, np.pi / 2)):
                    ins = nc.vector.tensor_scalar(ang[:, k, :, f::2], pos[:], float(np.float32(freq)),
                                                  float(phase), ALU.mult, ALU.add)
            chain.link(ins)
            chain.link(nc.vector.tensor_scalar(turns[:], ang[:], float(0.5 / np.pi), ROUNDER, ALU.mult, ALU.add))
            chain.link(nc.vector.tensor_scalar(trig[:], turns[:], ROUNDER, float(-2 * np.pi), ALU.subtract, ALU.mult))
            chain.link(nc.vector.tensor_tensor(turns[:], trig[:], ang[:], ALU.add))
            nc.vector.tensor_scalar(ang[:], turns[:], PI_BELOW, -PI_BELOW, ALU.min, ALU.max).then_inc(ang_ready, 1)
            nc.vector.memset(m.v0[:, :, :, lay.hd:lay.hd + 1], 1.0).then_inc(ones_set, 1)
            dve.wait_ge(ld_x, 16)
            layernorm_vector(nc, dve, chain, m, 1e-5, root_in, root_out, xn_ready)
            dve.wait_ge(trig_ready, 1)
            for n in range(2 * NT):
                i, k_side = n % NT, n < NT
                dve.wait_ge(kv_ps if k_side else q_ps, i + 1)
                if n >= 2:
                    dve.wait_ge(rot_done, n - 1)
                src = ps[:, (0 if k_side else 4) + i % 2, 0:D].rearrange("p (h a e) -> p h (a e)", h=32, a=4)
                src = src.rearrange("p h (a e) -> p h a e", a=4)
                for k in range(2):
                    w = trig[:, k, i, :]
                    wb = w.unsqueeze(1).unsqueeze(3).broadcast_to([P, 32, 4, 2])
                    ins = nc.vector.tensor_tensor(rot[:, n % 2, k, :].rearrange("p (h a e) -> p h a e", h=32, a=4),
                                                  src, wb, ALU.mult)
                ins.then_inc(rot_ready, 1)
            for s in range(len(SPLITS)):
                dve.wait_ge(hi_ready, s + 1)
                if s >= 2:
                    dve.wait_ge(lo_ready, s - 1)
                nc.vector.tensor_tensor(m.rest[:, s % 2, :], ps[:, 6 + s % 2, :], m.part[:, s % 2, 0, :],
                                        ALU.subtract).then_inc(rest_ready, 1)

        @block.scalar
        def _(act):
            act.wait_ge(ang_ready, 1)
            nc.scalar.activation(trig[:], ang[:], ACT.Sin).then_inc(trig_ready, 1)
            layernorm_scalar(nc, act, m, root_in, root_out)
            act.wait_ge(ones_set, 1)
            for i in range(NT):
                act.wait_ge(kv_ps, i + 1)
                nc.scalar.copy(m.v0[:, i, :, 0:lay.hd],
                               ps[:, 2 + i % 2, 0:D].rearrange("p (h e) -> p h e", h=32)).then_inc(v_copied, 1)
            for i in range(NT):
                act.wait_ge(xt_ps, i + 1)
                transposed_copy(nc, m, i, 2 + i % 2, m.xT).then_inc(xt_ready, 1)
            split_scalar(nc, act, m, split_ps, part_dma, hi_ready, rest_ready, mid_ready)

        @block.gpsimd
        def _(pool):
            pool.wait_ge(ld_const, 32)
            nc.gpsimd.tensor_copy(m.ident_bf[:], m.ident[:])
            for n in range(2 * NT):
                i = n % NT
                dst = (m.k_tm if n < NT else m.q_tm)[:, i, :].rearrange("p (a e) -> p a e", e=2)
                sin = rot[:, n % 2, 0, :].rearrange("p (a e) -> p a e", e=2)
                cos = rot[:, n % 2, 1, :].rearrange("p (a e) -> p a e", e=2)
                pool.wait_ge(rot_ready, n + 1)
                nc.gpsimd.tensor_tensor(dst[:, :, 0], cos[:, :, 0], sin[:, :, 1], ALU.subtract)
                nc.gpsimd.tensor_tensor(dst[:, :, 1], sin[:, :, 0], cos[:, :, 1], ALU.add).then_inc(rot_done, 1)
            split_gpsimd(nc, pool, m, mid_ready, rest_ready, part_dma, lo_ready)


def split_scalar(nc, act, m, split_ps, part_dma, hi_ready, rest_ready, mid_ready):
    for s in range(len(SPLITS)):
        act.wait_ge(split_ps, s + 1)
        if s >= 2:
            act.wait_ge(part_dma[s % 2], 16 * WRITES * (s // 2))
        nc.scalar.copy(m.part[:, s % 2, 0, :], m.ps[:, 6 + s % 2, :]).then_inc(hi_ready, 1)
        act.wait_ge(rest_ready, s + 1)
        nc.scalar.copy(m.part[:, s % 2, 1, :], m.rest[:, s % 2, :]).then_inc(mid_ready, 1)


def split_gpsimd(nc, pool, m, mid_ready, rest_ready, part_dma, lo_ready):
    for s in range(len(SPLITS)):
        pool.wait_ge(rest_ready, s + 1)
        pool.wait_ge(mid_ready, s + 1)
        if s >= 2:
            pool.wait_ge(part_dma[s % 2], 16 * WRITES * (s // 2))
        nc.gpsimd.tensor_tensor(m.part[:, s % 2, 2, :], m.rest[:, s % 2, :], m.part[:, s % 2, 1, :],
                                ALU.subtract).then_inc(lo_ready, 1)


def zero_slots(nc, pool, m, zeros, zero_set):
    nc.gpsimd.memset(zeros[:], 0.0).then_inc(zero_set, 1)
    pool.wait_ge(zero_set, 1)
    for r in range(BLOCKS // ROUND):
        rows = m.x_slots[r * ROUND * P:(r + 1) * ROUND * P, :].rearrange("(b p) d -> p b d", p=P)
        pool.dma_start(rows, bcast(zeros[:], 1, ROUND)).then_inc(m.zeroed, 16)
    for r in range(E1 // ROUND, BLOCKS // ROUND):
        rows = m.y_slots[r * ROUND * P:(r + 1) * ROUND * P, :].rearrange("(b p) d -> p b d", p=P)
        pool.dma_start(rows, bcast(zeros[:], 1, ROUND)).then_inc(m.zeroed, 16)


NBUF = 4
AHEAD = 2
PROBS = 4
LAG = 2
TURN_LAG = 4


def attention(nc, m, lay, io):
    U, GR, R, SH, W, hd = lay.units, lay.groups, lay.rows, lay.shifts, lay.vw, lay.hd
    cuts = ((0, S),) if SH == 1 else ((0, MAIN), (MAIN, S))
    v = m.v0 if lay is L0 else m.v1
    ps = m.ps
    CT = 4 // SH
    HG = 2 * CT
    NG = G // HG
    HEADS = U * G
    with ExitStack() as ctx:
        def sem(n):
            return m.sem(lay.name + "a_" + n, ctx)
        qs = m.sb(lay.name + "_qs", [lay.krows, NBUF, G, S], BF16, ctx)
        ks = m.sb(lay.name + "_ks", [lay.krows, NBUF, G, S], BF16, ctx)
        prob = m.sb(lay.name + "_prob", [P, PROBS, 2, QT, S], ctx=ctx)
        mx = m.sb(lay.name + "_mx", [P, 2, QT, SH, G], ctx=ctx)
        neg = m.sb(lay.name + "_neg", [P, 2, QT, SH, 2, G], BF16, ctx)
        negT = m.sb(lay.name + "_negT", [2 * SH * G, 2, S], BF16, ctx)
        sumsT = m.sb(lay.name + "_sumsT", [P, 2, 2 * S], ctx=ctx)
        sel = m.sb(lay.name + "_sel", [P, CT * W], ctx=ctx)
        zero_row = m.sb(lay.name + "_zero_row", [1, 2 * S], ctx=ctx)
        rec = m.sb(lay.name + "_rec", [P, 2, QT, CT * SH], ctx=ctx)
        ctxv = m.sb(lay.name + "_ctxv", [P, QT, HG * SH, hd], ctx=ctx)
        if lay is L0:
            zeros, zero_set = m.sb("zeros", [P, D], ctx=ctx), sem("zero_set")
        loaded = [sem(f"loaded{b}") for b in range(NBUF)]
        shifted = [sem(f"shifted{b}") for b in range(NBUF)]
        ones_ld, sel_ld, zero_row_set = sem("ones_ld"), sem("sel_ld"), sem("zero_row_set")
        s_ps, s_max, step, neg_ready = sem("s_ps"), sem("s_max"), sem("step"), sem("neg_ready")
        negT_ps, negT_ready, t_ps, t_exp = sem("negT_ps"), sem("negT_ready"), sem("t_ps"), sem("t_exp")
        weighed, sums_copied, tok_ps, tok_used = sem("weighed"), sem("sums_copied"), sem("tok_ps"), sem("tok_used")
        block = ctx.enter_context(nc.Block())

        @block.sync
        def _(sp):
            def load(u, b):
                bt, g = u // GR, u % GR
                for dst, src in ((qs, "q"), (ks, "k")):
                    sp.dma_start(dst[0:R, b, :, :], lay.stack(m, src)[bt, :, g * G:(g + 1) * G, :]
                                 ).then_inc(loaded[b], 16)

            def shift_rows(u, b):
                sp.wait_ge(negT_ready, u + 1)
                for r in range(2 * SH):
                    sp.dma_start(qs[R + r:R + r + 1, b, :, :], negT[r * G:(r + 1) * G, b % 2, :]
                                 ).then_inc(shifted[b], 16)

            load(0, 0)
            sp.dma_start(sel[:], io[lay.name + "_sel"]).then_inc(sel_ld, 16)
            for u in range(1, NBUF):
                load(u, u)
            for u in range(U):
                shift_rows(u, u % NBUF)
                if u >= AHEAD and u + NBUF - AHEAD < U:
                    n = u - AHEAD
                    sp.wait_ge(t_ps, G // 2 * (n + 1))
                    load(n + NBUF, n % NBUF)

        @block.gpsimd
        def _(pool):
            nc.gpsimd.memset(zero_row[:], 0.0).then_inc(zero_row_set, 1)
            for b in range(NBUF):
                pool.dma_start(ks[R:R + 2 * SH, b, :, :], io[lay.name + "_ones"]).then_inc(ones_ld, 16)
            if lay is L0:
                zero_slots(nc, pool, m, zeros, zero_set)

        @block.tensor
        def _(pe):
            turned = [0]
            maxed = [0]

            def scores(n):
                u, h = n // G, n % G
                if h == 0:
                    pe.wait_ge(loaded[u % NBUF], 32 * (u // NBUF + 1))
                if n >= 2:
                    pe.wait_ge(s_max, n - 1)
                for qt in range(QT):
                    ins = nc.tensor.matmul(ps[:, n % 2, qt * S:(qt + 1) * S],
                                           qs[0:R, u % NBUF, h, qt * P:(qt + 1) * P], ks[0:R, u % NBUF, h, :],
                                           start=True, stop=True)
                ins.then_inc(s_ps, 1)

            def transposed_maxima(u):
                pe.wait_ge(neg_ready, u + 1)
                if u >= 1:
                    pe.wait_ge(negT_ready, u)
                if turned[0]:
                    pe.wait_ge(tok_used, turned[0])
                out = ps[0:2 * SH * G, 7, 384:512].bitcast(BF16)
                for qt in range(QT):
                    ins = nc.tensor.transpose(out[:, qt * P:(qt + 1) * P],
                                              neg[:, u % 2, qt, :, :, :].rearrange("p s k g -> p (s k g)"),
                                              m.ident_bf[:])
                ins.then_inc(negT_ps, 1)
                maxed[0] += 1

            def shifted_scores(n):
                u, h = n // G, n % G
                b = u % NBUF
                if h == 0:
                    pe.wait_ge(shifted[b], 32 * SH * (u // NBUF + 1))
                if h % 2 == 0 and n >= 4:
                    pe.wait_ge(t_exp, n // 2 - 1)
                for kt in range(QT):
                    ins = nc.tensor.matmul(ps[:, 2 + n % 4, kt * S:(kt + 1) * S],
                                           ks[:, b, h, kt * P:(kt + 1) * P], qs[:, b, h, :],
                                           start=True, stop=True)
                if h % 2 == 1:
                    ins.then_inc(t_ps, 1)

            def values(c):
                pe.wait_ge(t_exp, CT * (c + 1) // 2)
                if c % 2 == 0 and c >= 2:
                    pe.wait_ge(sums_copied, c // 2)
                for kt in range(QT):
                    for j in range(CT):
                        n = CT * c + j
                        bt, head = n // lay.heads, n % lay.heads
                        row = j * P // CT
                        ins = nc.tensor.matmul(ps[row:row + W, 6, (c % 2) * S:(c % 2 + 1) * S],
                                               v[:, bt * QT + kt, head, :], prob[:, n // 2 % PROBS, n % 2, kt, :],
                                               start=(kt == 0), stop=(kt == QT - 1))
                ins.then_inc(weighed, 1)

            def token_sums(gi):
                pe.wait_ge(sums_copied, gi + 1)
                if gi >= 1:
                    pe.wait_ge(tok_used, gi)
                pe.wait_ge(negT_ready, maxed[0])
                for j in range(2 * QT):
                    ins = nc.tensor.matmul(ps[:, 7, j * CT * W:(j + 1) * CT * W],
                                           sumsT[:, gi % 2, j * P:(j + 1) * P], sel[:], start=True, stop=True)
                ins.then_inc(tok_ps, 1)
                turned[0] += 1

            pe.wait_ge(zero_row_set, 1)
            nc.tensor.matmul(ps[:, 6, :], m.ones_row[:], zero_row[:], start=True, stop=True)
            for n in range(AHEAD * G):
                scores(n)
                if n == G + 1:
                    transposed_maxima(0)
            pe.wait_ge(ones_ld, 16 * NBUF)
            pe.wait_ge(sel_ld, 16)
            for n in range(HEADS + TURN_LAG):
                if n + AHEAD * G < HEADS:
                    scores(n + AHEAD * G)
                if n < HEADS:
                    shifted_scores(n)
                    if n % G == 1 and n // G + 1 < U:
                        transposed_maxima(n // G + 1)
                if n >= LAG + CT - 1 and (n - LAG + 1) % CT == 0 and n - LAG < HEADS:
                    values((n - LAG) // CT)
                if n >= TURN_LAG and (n - TURN_LAG + 1) % HG == 0:
                    token_sums((n - TURN_LAG) // HG)

        @block.vector
        def _(dve):
            m.clear_sems(dve)
            chain = Chain(dve, step)

            def maxima(n):
                u, h = n // G, n % G
                dve.wait_ge(s_ps, n + 1)
                for s, (lo, hi) in enumerate(cuts):
                    ins = nc.vector.reduce_max(mx[:, u % 2, :, s, h],
                                               ps[:, n % 2, :].rearrange("p (q k) -> p q k", q=QT)[:, :, lo:hi],
                                               AX_X)
                ins.then_inc(s_max, 1)

            def negated(u):
                dve.wait_ge(s_max, G * (u + 1))
                if u >= 2:
                    dve.wait_ge(negT_ps, u - 1)
                chain.link(nc.vector.tensor_scalar(neg[:, u % 2, :, :, 0, :], mx[:, u % 2, :, :, :],
                                                   -1.0, None, ALU.mult))
                for q in range(QT):
                    ins = nc.vector.scalar_tensor_tensor(neg[:, u % 2, q, :, 1, :], mx[:, u % 2, q, :, :], -1.0,
                                                         neg[:, u % 2, q, :, 0, :], ALU.mult, ALU.subtract)
                ins.then_inc(neg_ready, 1)

            def normalise(gi):
                u = gi // NG
                bt, col = u // GR, (u % GR * G + gi % NG * HG) * hd
                sums = ps[:, 7, 0:2 * QT * CT * W].rearrange("p (c q n e) -> p c q n e", c=2, q=QT, e=hd + 1)
                dve.wait_ge(tok_ps, gi + 1)
                chain.link(nc.vector.reciprocal(rec[:], sums[:, :, :, :, hd]))
                for q in range(QT):
                    dst = m.attn[:, bt * QT + q, col:col + HG * hd]
                    out = dst.rearrange("p (c n e) -> p c n e", c=2, e=hd) if SH == 1 else \
                        ctxv[:, q, :, :].rearrange("p (c n) e -> p c n e", c=2)
                    ins = nc.vector.tensor_tensor(out, sums[:, :, q, :, 0:hd], bcast(rec[:, :, q, :], 3, hd),
                                                  ALU.mult)
                ins.then_inc(tok_used, 1)
                if SH == 2:
                    dve.wait_ge(tok_used, gi + 1)
                    for q in range(QT):
                        halves = ctxv[:, q, :, :].rearrange("p (n s) e -> p n s e", s=SH)
                        nc.vector.tensor_tensor(m.attn[:, bt * QT + q, col:col + HG * hd]
                                                .rearrange("p (n e) -> p n e", e=hd),
                                                halves[:, :, 0, :], halves[:, :, 1, :], ALU.add)

            for n in range(AHEAD * G):
                maxima(n)
                if n % G == G - 1:
                    negated(n // G)
            for n in range(HEADS + TURN_LAG):
                if n + AHEAD * G < HEADS:
                    maxima(n + AHEAD * G)
                    if n % G == G - 1:
                        negated(n // G + AHEAD)
                if n >= TURN_LAG and (n - TURN_LAG + 1) % HG == 0:
                    normalise((n - TURN_LAG) // HG)

        @block.scalar
        def _(act):
            def maxima_rows(u):
                act.wait_ge(negT_ps, u + 1)
                if u >= 2:
                    act.wait_ge(shifted[(u - 2) % NBUF], 32 * SH * ((u - 2) // NBUF + 1))
                nc.scalar.copy(negT[:, u % 2, :], ps[0:2 * SH * G, 7, 384:512].bitcast(BF16)
                               ).then_inc(negT_ready, 1)

            def exponentials(n):
                act.wait_ge(t_ps, n + 1)
                if n >= PROBS:
                    act.wait_ge(weighed, 2 * (n - PROBS) // CT + 1)
                nc.scalar.activation(prob[:, n % PROBS, :, :, :].rearrange("p h k q -> p (h k q)"),
                                     ps[:, 2 + 2 * (n % 2):4 + 2 * (n % 2), :].rearrange("p b n -> p (b n)"),
                                     ACT.Exp, scale=lay.scale).then_inc(t_exp, 1)

            def copied_sums(gi):
                act.wait_ge(weighed, 2 * (gi + 1))
                if gi >= 2:
                    act.wait_ge(tok_ps, gi - 1)
                nc.scalar.copy(sumsT[:, gi % 2, :], ps[:, 6, :]).then_inc(sums_copied, 1)

            maxima_rows(0)
            for n in range(HEADS // 2 + 1):
                if n < HEADS // 2:
                    exponentials(n)
                    if n % (G // 2) == 0 and n // (G // 2) + 1 < U:
                        maxima_rows(n // (G // 2) + 1)
                if n >= CT and n % CT == 0:
                    copied_sums(n // CT - 1)


def attention_output(nc, m, name, w_dram, b_dram):
    with ExitStack() as ctx:
        def sem(n):
            return m.sem(name + n, ctx)
        w = m.sb(name + "w", [P, KD, D], ctx=ctx)
        b = m.sb(name + "b", [1, D], ctx=ctx)
        ld, at_ps, at_ready, out_ps, out_used = (sem(n) for n in ("ld", "at_ps", "at_ready", "out_ps", "out_used"))
        block = ctx.enter_context(nc.Block())

        @block.sync
        def _(sp):
            sp.dma_start(w[:], w_dram.rearrange("(c p) n -> p c n", p=P)).then_inc(ld, 16)
            sp.dma_start(b[:], b_dram.rearrange("(a n) -> a n", a=1)).then_inc(ld, 16)

        @block.tensor
        def _(pe):
            for i in range(NT + 1):
                if i < NT:
                    if i >= 2:
                        pe.wait_ge(at_ready, i - 1)
                    transpose_tile(nc, m, i % 2, m.attn[:, i, :]).then_inc(at_ps, 1)
                if i == 1:
                    pe.wait_ge(ld, 32)
                if i >= 1:
                    t = i - 1
                    pe.wait_ge(at_ready, t + 1)
                    if t >= 2:
                        pe.wait_ge(out_used, t - 1)
                    matmul_tile(nc, m.ps[:, 2 + t % 2, 0:D], m.xT, t, w, b[:], m.ones_row[:]).then_inc(out_ps, 1)

        @block.scalar
        def _(act):
            for i in range(NT):
                act.wait_ge(at_ps, i + 1)
                transposed_copy(nc, m, i, i % 2, m.xT).then_inc(at_ready, 1)

        @block.vector
        def _(dve):
            for i in range(NT):
                dve.wait_ge(out_ps, i + 1)
                nc.vector.tensor_tensor(m.xs[:, i, :], m.xs[:, i, :], m.ps[:, 2 + i % 2, 0:D],
                                        ALU.add).then_inc(out_used, 1)


def rounds(eng, n, body):
    body(0, True, n == 1)
    if n == 3:
        body(1, False, False)
    elif n > 3:
        with eng.Fori(1, n - 1) as g:
            body(g, False, False)
    if n > 1:
        body(n - 1, False, True)


E0, I0 = 16, 128
SH0 = 512 // I0
X0 = E0 + SH0
GRP, GSZ = 4, 4


def route_l0(nc, m, io):
    with ExitStack() as ctx:
        def sem(n):
            return m.sem("r0_" + n, ctx)

        def sb(n, shape, dt=F32):
            return m.sb("r0_" + n, [P] + shape, dt, ctx)
        rw, bias, iota = sb("rw", [KD, E0]), sb("bias", [E0]), sb("iota", [E0])
        score, biased = sb("score", [NT, E0]), sb("biased", [NT, E0])
        hi, lo = sb("hi", [NT * GRP, 2]), sb("lo", [NT * GRP, 2])
        top, second, t0, gsum = (sb(n, [NT * GRP]) for n in ("top", "second", "t0", "gsum"))
        later = sb("later", [GRP, GRP])
        more, same = sb("more", [NT, GRP, GRP]), sb("same", [NT, GRP, GRP])
        rank, masked = sb("rank", [NT, GRP]), sb("masked", [NT, E0])
        top8, idx8, idxf = sb("top8", [NT, 8]), sb("idx8", [NT, 8], U32), sb("idxf", [NT, 8])
        hot, den = sb("hot", [2, NT, E0]), sb("den", [NT])
        ld, step, root_in, root_out, xn_ready, xt_ps, xt_ready, logit_ps, score_ready = (sem(n) for n in (
            "ld", "step", "root_in", "root_out", "xn_ready", "xt_ps", "xt_ready", "logit_ps", "score_ready"))
        block = ctx.enter_context(nc.Block())

        @block.sync
        def _(sp):
            sp.dma_start(rw[:], io["L0_router_T"].rearrange("(c p) n -> p c n", p=P)).then_inc(ld, 16)
            sp.dma_start(bias[:], io["L0_ffn_e_bias"].partition_broadcast(P)).then_inc(ld, 16)
            sp.dma_start(iota[:], io["iota"][0:E0].partition_broadcast(P)).then_inc(ld, 16)
            sp.dma_start(later[:], io["later"].partition_broadcast(P)).then_inc(ld, 16)
            for q in range(PAIRS):
                load_weights(sp, m, io, 2 * q, 2, q)

        @block.tensor
        def _(pe):
            pe.wait_ge(ld, 64)
            transpose_and_project(nc, pe, m, xn_ready, xt_ps, xt_ready, rw, E0, logit_ps)

        @block.scalar
        def _(act):
            layernorm_scalar(nc, act, m, root_in, root_out)
            for i in range(NT):
                act.wait_ge(xt_ps, i + 1)
                transposed_copy(nc, m, i, i % 2, m.xT).then_inc(xt_ready, 1)
            act.wait_ge(logit_ps, 1)
            nc.scalar.activation(score[:].rearrange("p i e -> p (i e)"), m.ps[:, 2, 0:NT * E0], ACT.Sigmoid
                                 ).then_inc(score_ready, 1)

        @block.vector
        def _(dve):
            chain = Chain(dve, step)
            link, v = chain.link, nc.vector
            layernorm_vector(nc, dve, chain, m, 1e-5, root_in, root_out, xn_ready)
            v.memset(m.comb[:, :, E0:X0], 1.0)
            dve.wait_ge(ld, 64)
            dve.wait_ge(score_ready, 1)
            link(v.tensor_tensor(biased[:], score[:], bcast(bias[:], 1, NT), ALU.add))
            pairs = biased[:].rearrange("p i (g a b) -> p (i g) a b", g=GRP, b=2)
            v.tensor_tensor(hi[:], pairs[:, :, :, 0], pairs[:, :, :, 1], ALU.max)
            link(v.tensor_tensor(lo[:], pairs[:, :, :, 0], pairs[:, :, :, 1], ALU.min))
            v.tensor_tensor(top[:], hi[:, :, 0], hi[:, :, 1], ALU.max)
            v.tensor_tensor(second[:], hi[:, :, 0], hi[:, :, 1], ALU.min)
            link(v.tensor_tensor(t0[:], lo[:, :, 0], lo[:, :, 1], ALU.max))
            link(v.tensor_tensor(gsum[:], second[:], t0[:], ALU.max))
            link(v.tensor_tensor(second[:], gsum[:], top[:], ALU.add))
            gs = second[:].rearrange("p (i g) -> p i g", g=GRP)
            mine, other = bcast(gs, 3, GRP), bcast(gs, 2, GRP)
            v.tensor_tensor(more[:], other, mine, ALU.is_gt)
            link(v.tensor_tensor(same[:], other, mine, ALU.is_equal))
            same_earlier = hot[:, 0, :, :].rearrange("p i (g h) -> p i g h", g=GRP)
            link(v.tensor_tensor(same_earlier, same[:], bcast(later[:], 1, NT), ALU.mult))
            link(v.tensor_tensor(same[:], more[:], same_earlier, ALU.add))
            link(v.tensor_reduce(rank[:], same[:], AX_X, ALU.add))
            link(v.tensor_scalar(gsum[:].rearrange("p (i g) -> p i g", g=GRP), rank[:], 1.5, None, ALU.is_lt))
            link(v.tensor_tensor(hot[:, 0, :, :].rearrange("p i (g h) -> p (i g) h", g=GRP),
                                 biased[:].rearrange("p i (g h) -> p (i g) h", g=GRP),
                                 bcast(gsum[:], 2, GSZ), ALU.mult))
            link(v.tensor_scalar(masked[:], hot[:, 0, :, :], 0.0, None, ALU.add))
            top_indices(nc, link, masked, top8, idx8, idxf)
            for j in range(2):
                ins = v.tensor_tensor(hot[:, j, :, :], bcast(iota[:], 1, NT), bcast(idxf[:, :, j], 2, E0), ALU.is_equal)
            link(ins)
            link(v.tensor_tensor(masked[:], hot[:, 0, :, :], hot[:, 1, :, :], ALU.add))
            link(v.tensor_tensor(biased[:], masked[:], score[:], ALU.mult))
            link(v.tensor_reduce(den[:], biased[:], AX_X, ALU.add))
            link(v.tensor_scalar(m.rstd[:, 0, :], den[:], 1e-20, None, ALU.add))
            link(v.reciprocal(den[:], m.rstd[:, 0, :]))
            v.tensor_tensor(m.comb[:, :, 0:E0], biased[:], bcast(den[:], 2, E0), ALU.mult)


def transpose_and_project(nc, pe, m, xn_ready, xt_ps, xt_ready, w, n, logit_ps):
    for i in range(NT):
        pe.wait_ge(xn_ready, i + 1)
        if i >= 2:
            pe.wait_ge(xt_ready, i - 1)
        transpose_tile(nc, m, i % 2, m.xn[:, i, :]).then_inc(xt_ps, 1)
    pe.wait_ge(xt_ready, NT)
    for i in range(NT):
        ins = matmul_tile(nc, m.ps[:, 2, i * n:(i + 1) * n], m.xT, i, w)
    ins.then_inc(logit_ps, 1)


def top_indices(nc, link, values, top8, idx8, idxf):
    for i in range(NT):
        ins = nc.vector.max(top8[:, i, :], values[:, i, :])
    link(ins)
    for i in range(NT):
        ins = nc.vector.max_index(idx8[:, i, :], top8[:, i, :], values[:, i, :])
    link(ins)
    link(nc.vector.tensor_copy(idxf[:], idx8[:]))


def experts_l0(nc, m, io):
    with ExitStack() as ctx:
        def sem(n):
            return m.sem("f0_" + n, ctx)
        HT = T // 2
        up = m.sb("f0_up", [P, 2, KD, I0], ctx=ctx)
        down = m.sb("f0_down", [P, 2, D], ctx=ctx)
        relu = m.sb("f0_relu", [P, 2, HT], ctx=ctx)
        hid = m.sb("f0_hid", [P, 2, HT], ctx=ctx)
        loaded = [sem("loaded0"), sem("loaded1")]
        up_ps, relu_done, hid_done, down_ps, added = (sem(n) for n in (
            "up_ps", "relu_done", "hid_done", "down_ps", "added"))
        block = ctx.enter_context(nc.Block())
        NG = X0 // 2

        @block.sync
        def _(sp):
            def body(g, first, last):
                for j in range(2):
                    e = 2 * g + j
                    if not first:
                        sp.wait_ge(down_ps, 8 * (e - 1))
                    sp.dma_start(up[:, j, :, :],
                                 io["L0_up"][bass.ds(e, 1), :, :].rearrange("a (c p) n -> p (a c) n", p=P)
                                 ).then_inc(loaded[j], 16)
                    sp.dma_start(down[:, j, :], io["L0_down"][bass.ds(e, 1), :, :].rearrange("a p n -> p (a n)")
                                 ).then_inc(loaded[j], 16)
            rounds(sp, NG, body)

        @block.tensor
        def _(pe):
            def hidden(n, slot, half, loads, first):
                if half == 0:
                    pe.wait_ge(loaded[slot], 32 * loads)
                if not first:
                    pe.wait_ge(relu_done, n - 1)
                for c in range(KD):
                    ins = nc.tensor.matmul(m.ps[:, half, :], up[:, slot, c, :], m.xT[:, c, half * HT:(half + 1) * HT],
                                           start=(c == 0), stop=(c == KD - 1))
                ins.then_inc(up_ps, 1)

            def outputs(n, slot, half, first):
                pe.wait_ge(hid_done, n + 1)
                for t in range(4):
                    if not first:
                        pe.wait_ge(added, 4 * n + t - 3)
                    nc.tensor.matmul(m.ps[:, 2 + t, 0:D], hid[:, half, t * P:(t + 1) * P], down[:, slot, :],
                                     start=True, stop=True).then_inc(down_ps, 1)

            hidden(0, 0, 0, 1, True)

            def body(g, first, last):
                for k in range(4):
                    n = 4 * g + k
                    if not (last and k == 3):
                        hidden(n + 1, ((k + 1) // 2) % 2, (k + 1) % 2, g + 1 + (k == 3), first and k == 0)
                    outputs(n, k // 2, k % 2, first and k == 0)
            rounds(pe, NG, body)

        @block.scalar
        def _(act):
            def body(g, first, last):
                for k in range(4):
                    n = 4 * g + k
                    act.wait_ge(up_ps, n + 1)
                    if not (first and k < 2):
                        act.wait_ge(hid_done, n - 1)
                    nc.scalar.activation(relu[:, k % 2, :], m.ps[:, k % 2, :], ACT.Relu).then_inc(relu_done, 1)
            rounds(act, NG, body)

        @block.gpsimd
        def _(pool):
            def body(g, first, last):
                for k in range(4):
                    n = 4 * g + k
                    pool.wait_ge(relu_done, n + 1)
                    if not (first and k < 2):
                        pool.wait_ge(down_ps, 4 * (n - 1))
                    nc.gpsimd.tensor_tensor(hid[:, k % 2, :], relu[:, k % 2, :], relu[:, k % 2, :], ALU.mult
                                            ).then_inc(hid_done, 1)
            rounds(pool, NG, body)

        @block.vector
        def _(dve):
            def body(g, first, last):
                for k in range(4):
                    for t in range(4):
                        i = 4 * (k % 2) + t
                        dve.wait_ge(down_ps, 16 * g + 4 * k + t + 1)
                        nc.vector.scalar_tensor_tensor(
                            m.xs[:, i, :], m.ps[:, 2 + t, 0:D], m.comb[:, i, bass.ds(2 * g + k // 2, 1)], m.xs[:, i, :],
                            ALU.mult, ALU.add).then_inc(added, 1)
            rounds(dve, NG, body)


def prep_l1(nc, m, io):
    lay, H, hd = L1, L1.heads, L1.hd
    with ExitStack() as ctx:
        def sem(n):
            return m.sem("p1_" + n, ctx)

        def sb(n, shape, parts=P):
            return m.sb("p1_" + n, [parts] + shape, F32, ctx)
        wq, wmain, wdca = sb("wq", [KD, D]), sb("wmain", [2 * D]), sb("wdca", [2 * D])
        bq, bmain, bdca = sb("bq", [D], 1), sb("bmain", [2 * D], 1), sb("bdca", [2 * D], 1)
        tmask = sb("tmask", [2, S], 1)
        pmask = sb("pmask", [QT, 2])
        ctxT_dca = sb("ctxT_dca", [B, P])
        nw, nb = sb("nw", [3, hd]), sb("nb", [3, hd])
        hmean, hvar = sb("hmean", [2, NT, H]), sb("hvar", [2, NT, H])
        hwork = sb("hwork", [4, 2 * NT * H])
        sq = sb("sq", [2, D])
        scaled = sb("scaled", [2, 2, D])
        ld, ld_norm, step, root_in, root_out, xn_ready, xt_ps, xt_ready = (sem(n) for n in (
            "ld", "ld_norm", "step", "root_in", "root_out", "xn_ready", "xt_ps", "xt_ready"))
        ctx_ready, v_set, k_ps, v_copied, q_ps, cent, squared, hroot_in, hroot_out, scaled_done, tm_done = (
            sem(n) for n in ("ctx_ready", "v_set", "k_ps", "v_copied", "q_ps", "cent", "squared", "hroot_in",
                             "hroot_out", "scaled_done", "tm_done"))
        pool_step, squares_summed = sem("pool_step"), sem("squares_summed")
        split_ps, hi_ready, rest_ready, mid_ready, lo_ready = (sem(n) for n in (
            "split_ps", "hi_ready", "rest_ready", "mid_ready", "lo_ready"))
        part_dma = [sem("part_dma0"), sem("part_dma1")]
        ps = m.ps
        block = ctx.enter_context(nc.Block())

        @block.sync
        def _(sp):
            loads = [(wq[:], io["L1_xattn_Wq"].rearrange("(c p) n -> p c n", p=P)),
                     (wmain[:], io["L1_wmain"]), (wdca[:], io["L1_xattn_Wkv_dca"]),
                     (bq[:], io["L1_xattn_bq"].rearrange("(a n) -> a n", a=1)),
                     (bmain[:], io["L1_bmain"]), (bdca[:], io["L1_xattn_bkv_dca"].rearrange("(a n) -> a n", a=1)),
                     (tmask[:], io["tmask"]), (pmask[:], io["pmask"])]
            for dst, src in loads:
                sp.dma_start(dst, src).then_inc(ld, 16)
            for dst, which in ((nw, "w"), (nb, "b")):
                sp.dma_start(dst[:, 0, :], io["L1_xattn_qn_" + which].partition_broadcast(P)).then_inc(ld_norm, 16)
                for j in (1, 2):
                    sp.dma_start(dst[0:P - DCA * (j - 1), j, :],
                                 io["L1_xattn_kn_" + which].partition_broadcast(P - DCA * (j - 1))).then_inc(ld_norm, 16)
                sp.dma_start(dst[P - DCA:P, 2, :],
                             io["L1_xattn_kn_dca_" + which].partition_broadcast(DCA)).then_inc(ld_norm, 16)
            for s in range(len(SPLITS)):
                sp.wait_ge(lo_ready, s + 1)
                sp.wait_ge(mid_ready, s + 1)
                split_writes(sp, m, lay, s, part_dma)
            for b in range(2):
                sp.wait_ge(part_dma[b], 16 * WRITES * len(SPLITS) // 2)

        @block.tensor
        def _(pe):
            pe.wait_ge(ld, 8 * 16)
            pe.wait_ge(ctx_ready, 1)
            for i in range(NT):
                odd = i % 2
                if i >= 2:
                    pe.wait_ge(cent, i - 1)
                if i >= 2:
                    pe.wait_ge(v_copied, i - 1)
                main = m.ctxT[:, i * P:(i + 1) * P]
                dca = ctxT_dca[:, i // 2, :]
                mmask, dmask = (tmask[:, a, odd * P:(odd + 1) * P] for a in range(2))
                k_out, v_out, vd_out = ps[:, odd, 0:D], ps[:, 2 + odd, 0:D], ps[:, 2 + odd, D:2 * D]
                for out, col in ((k_out, 0), (v_out, D)):
                    both = odd and col == 0
                    nc.tensor.matmul(out, main, wmain[:, col:col + D], start=True, stop=False)
                    ins = nc.tensor.matmul(out, mmask, bmain[:, col:col + D], start=False, stop=not both)
                    if both:
                        nc.tensor.matmul(out, dca, wdca[:, 0:D], start=False, stop=False)
                        ins = nc.tensor.matmul(out, dmask, bdca[:, 0:D], start=False, stop=True)
                if odd:
                    nc.tensor.matmul(vd_out, dca, wdca[:, D:2 * D], start=True, stop=False)
                    ins = nc.tensor.matmul(vd_out, dmask, bdca[:, D:2 * D], start=False, stop=True)
                ins.then_inc(k_ps, 1)
            pe.wait_ge(v_copied, NT)
            for i in range(NT + 1):
                if i < NT:
                    pe.wait_ge(xn_ready, i + 1)
                    if i >= 2:
                        pe.wait_ge(xt_ready, i - 1)
                    transpose_tile(nc, m, 2 + i % 2, m.xn[:, i, :]).then_inc(xt_ps, 1)
                if i >= 1:
                    t = i - 1
                    pe.wait_ge(xt_ready, t + 1)
                    if t >= 2:
                        pe.wait_ge(cent, NT + t - 1)
                    matmul_tile(nc, ps[:, 4 + t % 2, 0:D], m.xT, t, wq, bq[:], m.ones_row[:]).then_inc(q_ps, 1)
            for s in range(len(SPLITS)):
                split_tensor(nc, pe, m, s, tm_done, rest_ready).then_inc(split_ps, 1)

        def token_major(n):
            return (m.k_tm if n < NT else m.q_tm)[:, n % NT, :]

        @block.vector
        def _(dve):
            chain = Chain(dve, step)
            link, v = chain.link, nc.vector
            def sum_squares(n):
                dve.wait_ge(squared, n + 1)
                nc.vector.tensor_reduce(hvar[:, n // NT, n % NT, :], sq[:, n % 2, :].rearrange("p (h e) -> p h e", h=H),
                                        AX_X, ALU.add).then_inc(squares_summed, 1)

            layernorm_vector(nc, dve, chain, m, 1e-5, root_in, root_out, xn_ready)
            v.memset(ctxT_dca[:], 0.0)
            link(v.memset(m.v1[:], 0.0))
            dve.wait_ge(ld, 8 * 16)
            tail = m.ctxT[:].rearrange("p (b s) -> p b s", b=B)[:, :, MAIN:S]
            link(v.tensor_copy(ctxT_dca[:, :, P - DCA:P], tail))
            v.memset(tail, 0.0).then_inc(ctx_ready, 1)
            for i in range(NT):
                for a in range(2):
                    col = (a + 1) * (hd + 1) - 1
                    ins = v.tensor_copy(m.v1[:, i, :, col], pmask[:, i % 2, a:a + 1].broadcast_to([P, H]))
            ins.then_inc(v_set, 1)
            for n in range(2 * NT):
                i = n % NT
                dve.wait_ge(k_ps if n < NT else q_ps, i + 1)
                src = ps[:, (0 if n < NT else 4) + i % 2, 0:D].rearrange("p (h e) -> p h e", h=H)
                side = n // NT
                link(v.tensor_reduce(hvar[:, side, i, :], src, AX_X, ALU.add))
                link(v.tensor_scalar(hmean[:, side, i, :], hvar[:, side, i, :], 1.0 / hd, None, ALU.mult))
                v.tensor_tensor(token_major(n).rearrange("p (h e) -> p h e", h=H), src,
                                bcast(hmean[:, side, i, :], 2, hd), ALU.subtract).then_inc(cent, 1)
                if n >= 1:
                    sum_squares(n - 1)
            sum_squares(2 * NT - 1)
            dve.wait_ge(squares_summed, 2 * NT)
            flat = hvar[:].rearrange("p a i h -> p (a i h)")
            link(v.tensor_scalar(hwork[:, 0, :], flat, 1.0 / hd, 1e-6, ALU.mult, ALU.add))
            rsqrt_vector(nc, dve, chain, hwork[:, 0, :], None, [hwork[:, j, :] for j in range(4)], hroot_in, hroot_out)
            for n in range(2 * NT):
                if n >= 2:
                    dve.wait_ge(tm_done, n - 1)
                r = hwork[:, 2, n * H:(n + 1) * H]
                v.tensor_tensor(scaled[:, n % 2, 0, :].rearrange("p (h e) -> p h e", h=H),
                                token_major(n).rearrange("p (h e) -> p h e", h=H), bcast(r, 2, hd),
                                ALU.mult).then_inc(scaled_done, 1)
            for s in range(len(SPLITS)):
                dve.wait_ge(hi_ready, s + 1)
                if s >= 2:
                    dve.wait_ge(lo_ready, s - 1)
                v.tensor_tensor(m.rest[:, s % 2, :], ps[:, 6 + s % 2, :], m.part[:, s % 2, 0, :],
                                ALU.subtract).then_inc(rest_ready, 1)

        @block.scalar
        def _(act):
            layernorm_scalar(nc, act, m, root_in, root_out)
            act.wait_ge(v_set, 1)

            def square(n):
                act.wait_ge(cent, n + 1)
                if n >= 2:
                    act.wait_ge(squares_summed, n - 1)
                nc.scalar.activation(sq[:, n % 2, :], token_major(n), ACT.Square).then_inc(squared, 1)

            for i in range(NT):
                act.wait_ge(k_ps, i + 1)
                for a in range(1 + i % 2):
                    ins = nc.scalar.copy(m.v1[:, i, :, a * (hd + 1):a * (hd + 1) + hd],
                                         ps[:, 2 + i % 2, a * D:(a + 1) * D].rearrange("p (h e) -> p h e", h=H))
                ins.then_inc(v_copied, 1)
                square(i)
            for i in range(NT + 1):
                if i < NT:
                    act.wait_ge(xt_ps, i + 1)
                    transposed_copy(nc, m, i, 2 + i % 2, m.xT).then_inc(xt_ready, 1)
                if i >= 1:
                    square(NT + i - 1)
            act.wait_ge(hroot_in, 1)
            nc.scalar.activation(hwork[:, 1, :], hwork[:, 3, :], ACT.Sqrt).then_inc(hroot_out, 1)
            split_scalar(nc, act, m, split_ps, part_dma, hi_ready, rest_ready, mid_ready)

        @block.gpsimd
        def _(pool):
            pool.wait_ge(ld_norm, 8 * 16)
            for n in range(2 * NT):
                pool.wait_ge(scaled_done, n + 1)
                row = 0 if n >= NT else 1 + n % 2

                def heads(ap):
                    return ap.rearrange("p (h e) -> p h e", h=H)
                nc.gpsimd.tensor_tensor(heads(scaled[:, n % 2, 1, :]), heads(scaled[:, n % 2, 0, :]),
                                        bcast(nw[:, row, :], 1, H), ALU.mult).then_inc(pool_step, 1)
                pool.wait_ge(pool_step, n + 1)
                nc.gpsimd.tensor_tensor(heads(token_major(n)), heads(scaled[:, n % 2, 1, :]),
                                        bcast(nb[:, row, :], 1, H), ALU.add).then_inc(tm_done, 1)
            split_gpsimd(nc, pool, m, mid_ready, rest_ready, part_dma, lo_ready)


E1, I1, TOP1 = 60, 176, 4
SH1 = 704 // I1
HC = I1 // 2
ROUND = 12
OVER = -(-(T * TOP1 // P) // ROUND) * ROUND
BLOCKS = E1 + OVER
RING = ROUND
PAIRS = ROUND // 2
ZEROED = (BLOCKS + OVER) // ROUND


def route_l1(nc, m, io):
    with ExitStack() as ctx:
        def sem(n):
            return m.sem("r1_" + n, ctx)

        def sb(n, shape, dt=F32):
            return m.sb("r1_" + n, [P] + shape, dt, ctx)
        NC = E1 + 1
        gw, iota = sb("gw", [KD, NC]), sb("iota", [P])
        logit, prob = sb("logit", [NT, NC]), sb("prob", [NT, E1])
        top, total = sb("top", [NT]), sb("total", [NT])
        top8, idx8, idxf = m.topw, sb("idx8", [NT, 8], U32), sb("idxf", [NT, 8])
        hot = sb("hot", [TOP1, NT, E1])
        mask_bf = sb("mask_bf", [NT, E1], BF16)
        upper, upper_bf, ones_bf = sb("upper", [P]), sb("upper_bf", [P], BF16), sb("ones_bf", [P], BF16)
        count, marks, extra, incl = sb("count", [E1]), sb("marks", [NT]), sb("extra", [E1]), sb("incl", [E1])
        shift, slot_of, picked = sb("shift", [E1]), sb("slot_of", [NT, E1]), sb("picked", [TOP1, NT])
        over_cmp, over_f, ones_e = sb("over_cmp", [OVER, E1]), sb("over_f", [1 + OVER]), sb("ones_e", [E1])
        mask_ready, rank_ps = sem("mask_ready"), sem("rank_ps")
        ld, step, root_in, root_out, xn_ready, xt_ps, xt_ready, logit_ps, logit_ready, exp_in, exp_out = (
            sem(n) for n in ("ld", "step", "root_in", "root_out", "xn_ready", "xt_ps", "xt_ready", "logit_ps",
                             "logit_ready", "exp_in", "exp_out"))
        block = ctx.enter_context(nc.Block())

        @block.sync
        def _(sp):
            sp.dma_start(gw[:], io["L1_gates_T"].rearrange("(c p) n -> p c n", p=P)).then_inc(ld, 16)
            sp.dma_start(iota[:], io["iota"].partition_broadcast(P)).then_inc(ld, 16)
            sp.dma_start(upper[:], io["upper"]).then_inc(ld, 16)

        @block.tensor
        def _(pe):
            pe.wait_ge(ld, 48)
            transpose_and_project(nc, pe, m, xn_ready, xt_ps, xt_ready, gw, NC, logit_ps)
            pe.wait_ge(mask_ready, 1)
            for i in range(NT):
                for j in range(i + 1):
                    nc.tensor.matmul(m.ps[:, 3, i * E1:(i + 1) * E1], (upper_bf if j == i else ones_bf)[:],
                                     mask_bf[:, j, :], start=(j == 0), stop=(j == i))
            for j in range(NT):
                ins = nc.tensor.matmul(m.ps[:, 4, 0:E1], ones_bf[:], mask_bf[:, j, :],
                                       start=(j == 0), stop=(j == NT - 1))
            ins.then_inc(rank_ps, 1)

        @block.scalar
        def _(act):
            layernorm_scalar(nc, act, m, root_in, root_out)
            for i in range(NT):
                act.wait_ge(xt_ps, i + 1)
                transposed_copy(nc, m, i, i % 2, m.xT).then_inc(xt_ready, 1)
            act.wait_ge(logit_ready, 1)
            nc.scalar.activation(m.gate[:], logit[:, :, E1], ACT.Sigmoid)
            act.wait_ge(exp_in, 1)
            nc.scalar.activation(hot[:, 1, :, :], hot[:, 0, :, :], ACT.Exp).then_inc(exp_out, 1)

        @block.vector
        def _(dve):
            chain = Chain(dve, step)
            link, v = chain.link, nc.vector
            layernorm_vector(nc, dve, chain, m, 1e-5, root_in, root_out, xn_ready)
            dve.wait_ge(ld, 48)
            dve.wait_ge(logit_ps, 1)
            v.tensor_copy(logit[:].rearrange("p i e -> p (i e)"), m.ps[:, 2, 0:NT * NC]).then_inc(logit_ready, 1)
            dve.wait_ge(logit_ready, 1)
            lg = logit[:, :, 0:E1]
            link(v.tensor_reduce(top[:], lg, AX_X, ALU.max))
            v.tensor_tensor(hot[:, 0, :, :], lg, bcast(top[:], 2, E1), ALU.subtract).then_inc(exp_in, 1)
            dve.wait_ge(exp_out, 1)
            link(v.tensor_reduce(total[:], hot[:, 1, :, :], AX_X, ALU.add))
            link(v.reciprocal(top[:], total[:]))
            link(v.tensor_tensor(prob[:], hot[:, 1, :, :], bcast(top[:], 2, E1), ALU.mult))
            top_indices(nc, link, prob, top8, idx8, idxf)
            for j in range(TOP1):
                ins = v.tensor_tensor(hot[:, j, :, :], bcast(iota[:, 0:E1], 1, NT), bcast(idxf[:, :, j], 2, E1), ALU.is_equal)
            link(ins)
            v.tensor_copy(upper_bf[:], upper[:])
            v.memset(ones_bf[:], 1.0)
            v.memset(ones_e[:], 1.0)
            v.tensor_scalar(marks[:], iota[:, 1:1 + NT], float(P), None, ALU.mult)
            v.tensor_tensor(slot_of[:], hot[:, 0, :, :], hot[:, 1, :, :], ALU.add)
            link(v.tensor_tensor(prob[:], hot[:, 2, :, :], hot[:, 3, :, :], ALU.add))
            v.tensor_tensor(mask_bf[:], slot_of[:], prob[:], ALU.add).then_inc(mask_ready, 1)
            dve.wait_ge(rank_ps, 1)
            link(v.tensor_copy(count[:], m.ps[:, 4, 0:E1]))
            many = over_cmp[:].rearrange("p o e -> p (o e)")[:, 0:E1 * (NT - 1)].rearrange("p (e k) -> p e k", e=E1)
            link(v.tensor_tensor(many, bcast(count[:], 2, NT - 1), bcast(marks[:, 0:NT - 1], 1, E1), ALU.is_gt))
            link(v.tensor_reduce(extra[:], many, AX_X, ALU.add))
            link(v.tensor_tensor_scan(incl[:], ones_e[:], extra[:], 0.0, ALU.mult, ALU.add))
            link(v.tensor_tensor(count[:], incl[:], extra[:], ALU.subtract))
            link(v.tensor_tensor(extra[:], count[:], iota[:, 0:E1], ALU.subtract))
            link(v.tensor_scalar(shift[:], extra[:], float(E1 - 1), float(P), ALU.add, ALU.mult))
            rank = m.ps[:, 3, 0:NT * E1].rearrange("p (i e) -> p i e", i=NT)
            link(v.tensor_scalar(prob[:], rank, float(P), None, ALU.is_ge))
            link(v.tensor_tensor(slot_of[:], prob[:], bcast(shift[:], 1, NT), ALU.mult))
            link(v.tensor_tensor(prob[:], slot_of[:], rank, ALU.add))
            link(v.scalar_tensor_tensor(slot_of[:], bcast(iota[:, 0:E1], 1, NT), float(P), prob[:], ALU.mult, ALU.add))
            link(v.tensor_tensor(hot[:], hot[:], bcast(slot_of[:], 1, TOP1), ALU.mult))
            link(v.tensor_reduce(picked[:], hot[:], AX_X, ALU.add))
            link(v.tensor_copy(m.slot[:], picked[:]))
            link(v.tensor_tensor(over_cmp[:], bcast(incl[:], 1, OVER), bcast(iota[:, 0:OVER], 2, E1), ALU.is_le))
            link(v.tensor_reduce(over_f[:, 1:1 + OVER], over_cmp[:], AX_X, ALU.add))
            v.tensor_copy(over_f[:, 0:1], incl[:, E1 - 1:E1])
            link(v.tensor_scalar(over_cmp[:, 0, 0:OVER], over_f[:, 1:1 + OVER], float(E1 - 1), None, ALU.min))
            v.tensor_copy(m.over[:, 0:1], over_f[0:1, 0:1])
            v.tensor_copy(m.over[:, 1:1 + OVER], over_cmp[0:1, 0, 0:OVER])


def load_weights(eng, m, io, e, n, pair):
    eng.dma_start(m.ew13[:, 2 * pair:2 * pair + n, :, :],
                  io["L1_w13"][bass.ds(e, n), :, :].rearrange("a (c p) n -> p a c n", p=P)
                  ).then_inc(m.ew_loaded[pair], 16)
    eng.dma_start(m.ew2[:, 2 * pair:2 * pair + n, :, :],
                  io["L1_w2"][bass.ds(e, n), :, :].rearrange("a (c p) n -> p a c n", p=HC)
                  ).then_inc(m.ew_loaded[pair], 16)


def shared_l1(nc, m, io):
    with ExitStack() as ctx:
        def sem(n):
            return m.sem("f1_" + n, ctx)
        w13 = m.sb("f1_w13", [P, 2, KD, 2 * I1], ctx=ctx)
        w2 = m.sb("f1_w2", [HC, 2, 2, D], ctx=ctx)
        act_g = m.sb("f1_act_g", [P, 2, I1], ctx=ctx)
        hid = m.sb("f1_hid", [P, 2, I1], ctx=ctx)
        hidT = m.sb("f1_hidT", [HC, 2, 2 * P], ctx=ctx)
        loaded = [sem("loaded0"), sem("loaded1")]
        sent = sem("sent")
        gu_ps, silu_done, hid_done, ht_ps, ht_done, y_ps, added = (sem(n) for n in (
            "gu_ps", "silu_done", "hid_done", "ht_ps", "ht_done", "y_ps", "added"))
        block = ctx.enter_context(nc.Block())
        NG = SH1 // 2
        ps = m.ps

        @block.gpsimd
        def _(pool):
            pool.wait_ge(m.zeroed, 16 * ZEROED)
            for i in range(NT):
                for j in range(TOP1):
                    nc.gpsimd.indirect_dma_start(m.x_slots, bass.IndirectOffsetOnAxis(m.slot[:, j, i:i + 1], 0),
                                                 m.xn[:, i, :], None).then_inc(sent, 16)
            pool.wait_ge(sent, 16 * NT * TOP1)

        @block.sync
        def _(sp):
            def body(g, first, last):
                for j in range(2):
                    e = 2 * g + j
                    if not first:
                        sp.wait_ge(y_ps, NT * (e - 1))
                    sp.dma_start(w13[:, j, :, :],
                                 io["L1_shared_w13"][bass.ds(e, 1), :, :].rearrange("a (c p) n -> p (a c) n", p=P)
                                 ).then_inc(loaded[j], 16)
                    sp.dma_start(w2[:, j, :, :],
                                 io["L1_shared_w2"][bass.ds(e, 1), :, :].rearrange("a (c p) n -> p (a c) n", p=HC)
                                 ).then_inc(loaded[j], 16)
            rounds(sp, NG, body)

        @block.tensor
        def _(pe):
            def gate_up(n, k, g, first):
                slot, i = (k // NT) % 2, k % NT
                if i == 0:
                    pe.wait_ge(loaded[slot], 32 * (g + 1 + k // (2 * NT)))
                if not first:
                    pe.wait_ge(hid_done, n - 1)
                for c in range(KD):
                    ins = nc.tensor.matmul(ps[:, k % 2, 0:2 * I1], m.xT[:, c, i * P:(i + 1) * P], w13[:, slot, c, :],
                                           start=(c == 0), stop=(c == KD - 1))
                ins.then_inc(gu_ps, 1)

            def turn(n, k, first):
                pe.wait_ge(hid_done, n + 1)
                if not first:
                    pe.wait_ge(ht_done, n - 1)
                for c in range(2):
                    ins = nc.tensor.transpose(ps[0:HC, 2 + k % 2, c * P:(c + 1) * P],
                                              hid[:, k % 2, c * HC:(c + 1) * HC], m.ident[:])
                ins.then_inc(ht_ps, 1)

            def outputs(n, k, first):
                pe.wait_ge(ht_done, n + 1)
                if not first:
                    pe.wait_ge(added, n - 1)
                for c in range(2):
                    ins = nc.tensor.matmul(ps[:, 4 + k % 2, 0:D], hidT[:, k % 2, c * P:(c + 1) * P],
                                           w2[:, (k // NT) % 2, c, :], start=(c == 0), stop=(c == 1))
                ins.then_inc(y_ps, 1)

            gate_up(0, 0, 0, True)
            gate_up(1, 1, 0, True)
            turn(0, 0, True)

            def body(g, first, last):
                for k in range(2 * NT):
                    n = 2 * NT * g + k
                    if not (last and k >= 2 * NT - 2):
                        gate_up(n + 2, k + 2, g, False)
                    if not (last and k == 2 * NT - 1):
                        turn(n + 1, k + 1, first and k < 1)
                    outputs(n, k, first and k < 2)
            rounds(pe, NG, body)

        @block.scalar
        def _(act):
            def silu(n, k, first):
                act.wait_ge(gu_ps, n + 1)
                if not first:
                    act.wait_ge(hid_done, n - 1)
                nc.scalar.activation(act_g[:, k % 2, :], ps[:, k % 2, 0:I1], ACT.Silu).then_inc(silu_done, 1)

            silu(0, 0, True)

            def body(g, first, last):
                for k in range(2 * NT):
                    n = 2 * NT * g + k
                    if not (last and k == 2 * NT - 1):
                        silu(n + 1, k + 1, first and k < 1)
                    act.wait_ge(ht_ps, n + 1)
                    if not (first and k < 2):
                        act.wait_ge(y_ps, n - 1)
                    nc.scalar.copy(hidT[:, k % 2, :], ps[0:HC, 2 + k % 2, 0:2 * P]).then_inc(ht_done, 1)
            rounds(act, NG, body)

        @block.vector
        def _(dve):
            def multiply(n, k, first):
                dve.wait_ge(silu_done, n + 1)
                if not first:
                    dve.wait_ge(ht_ps, n - 1)
                nc.vector.tensor_tensor(hid[:, k % 2, :], act_g[:, k % 2, :], ps[:, k % 2, I1:2 * I1], ALU.mult
                                        ).then_inc(hid_done, 1)

            multiply(0, 0, True)

            def body(g, first, last):
                for k in range(2 * NT):
                    n = 2 * NT * g + k
                    if not (last and k == 2 * NT - 1):
                        multiply(n + 1, k + 1, first and k < 1)
                    i = k % NT
                    dve.wait_ge(y_ps, n + 1)
                    nc.vector.scalar_tensor_tensor(
                        m.xs[:, i, :], ps[:, 4 + k % 2, 0:D], m.gate[:, i:i + 1],
                        m.xs[:, i, :], ALU.mult, ALU.add).then_inc(added, 1)
            rounds(dve, NG, body)


def routed_l1(nc, m, io):
    with ExitStack() as ctx:
        def sem(n):
            return m.sem("f2_" + n, ctx)
        xg = m.sb("f2_xg", [P, 6, D], ctx=ctx)
        xgT = m.sb("f2_xgT", [P, 4, D], ctx=ctx)
        act_g = m.sb("f2_act_g", [P, 2, I1], ctx=ctx)
        hid = m.sb("f2_hid", [P, 2, I1], ctx=ctx)
        hidT = m.sb("f2_hidT", [HC, 2, 2 * P], ctx=ctx)
        yb = m.sb("f2_yb", [P, 4, D], ctx=ctx)
        x_loaded = [sem(f"x_loaded{j}") for j in range(3)]
        y_stored = [sem("y_stored0"), sem("y_stored1")]
        over_loaded = [sem(f"over_loaded{j}") for j in range(PAIRS)]
        xt_ps, xt_done, gu_ps, silu_done, hid_done, ht_ps, ht_done, y_ps, y_done = (sem(n) for n in (
            "xt_ps", "xt_done", "gu_ps", "silu_done", "hid_done", "ht_ps", "ht_done", "y_ps", "y_done"))
        block = ctx.enter_context(nc.Block())
        ps = m.ps
        FIXED, FURTHER = E1 // ROUND, OVER // ROUND

        def all_rounds(eng, prologue, body):
            prologue(0)
            rounds(eng, FIXED, body)
            blocks = eng.value_load(m.over[0:1, 0:1], min_val=0, max_val=OVER)
            for r in range(FURTHER):
                with eng.If(blocks > r * ROUND):
                    prologue(FIXED + r)
                    body(FIXED + r, False, True)

        @block.sync
        def _(sp):
            def load_x(g, h):
                rows = m.x_slots[bass.ds((ROUND * g + 2 * h) * P, 2 * P), :]
                sp.dma_start(xg[:, 2 * (h % 3):2 * (h % 3) + 2, :], rows.rearrange("(b p) d -> p b d", p=P)
                             ).then_inc(x_loaded[h % 3], 16)

            def store_y(g, h):
                sp.wait_ge(y_done, ROUND * g + 2 * h + 2)
                rows = m.y_slots[bass.ds((ROUND * g + 2 * h) * P, 2 * P), :]
                sp.dma_start(rows.rearrange("(b p) d -> p b d", p=P), yb[:, 2 * (h % 2):2 * (h % 2) + 2, :]
                             ).then_inc(y_stored[h % 2], 16)

            def prologue(g):
                load_x(g, 0)
                load_x(g, 1)
                if g >= FIXED:
                    for h in range(PAIRS):
                        sp.wait_ge(y_ps, ROUND * (g - 1) + 2 * h + 2)
                        for b in range(2):
                            o = ROUND * (g - FIXED) + 2 * h + b
                            e = sp.value_load(m.over[0:1, 1 + o:2 + o], min_val=0, max_val=E1 - 1)
                            for w, dram, pp in ((m.ew13, "L1_w13", P), (m.ew2, "L1_w2", HC)):
                                sp.dma_start(w[:, 2 * h + b, :, :],
                                             io[dram][bass.ds(e, 1), :, :].rearrange("a (c p) n -> p (a c) n", p=pp)
                                             ).then_inc(over_loaded[h], 16)

            def body(g, first, last):
                for h in range(PAIRS):
                    if not (first and h == 0):
                        sp.wait_ge(xt_ps, ROUND * g + 2 * h)
                    if h < PAIRS - 2:
                        load_x(g, h + 2)
                    elif not last:
                        load_x(g + 1, h + 2 - PAIRS)
                    if not (first and h == 0):
                        sp.wait_ge(y_ps, ROUND * g + 2 * h)
                    if not isinstance(g, int) or g < FIXED:
                        if h >= 1:
                            if not last:
                                load_weights(sp, m, io, ROUND * (g + 1) + 2 * (h - 1), 2, h - 1)
                        elif not first:
                            load_weights(sp, m, io, ROUND * g + 2 * (PAIRS - 1), 2, PAIRS - 1)
                    if h >= 1:
                        store_y(g, h - 1)
                    elif not first and not (isinstance(g, int) and g >= FIXED):
                        store_y(g - 1, PAIRS - 1)
                if last:
                    store_y(g, PAIRS - 1)
                    for a in range(2):
                        sp.wait_ge(y_stored[a], 16 * (PAIRS // 2) * (g + 1))
            all_rounds(sp, prologue, body)

        @block.tensor
        def _(pe):
            def turn_x(g, k, first):
                n, h = ROUND * g + k, (k // 2) % PAIRS
                gg, kk = (g, k) if k < ROUND else (g + 1, k - ROUND)
                if kk % 2 == 0:
                    pe.wait_ge(x_loaded[h % 3], 16 * ((PAIRS // 3) * gg + kk // 6 + 1))
                if not (first and k < 2):
                    pe.wait_ge(xt_done, n - 1)
                for c in range(KD):
                    ins = nc.tensor.transpose(ps[:, 6 + k % 2, c * P:(c + 1) * P], xg[:, k % 6, c * P:(c + 1) * P],
                                              m.ident[:])
                ins.then_inc(xt_ps, 1)

            def gate_up(g, k, first):
                n, slot = ROUND * g + k, k % ROUND
                gg, kk = (g, k) if k < ROUND else (g + 1, k - ROUND)
                if kk % 2 == 0:
                    if isinstance(gg, int) and gg >= FIXED:
                        pe.wait_ge(over_loaded[slot // 2], 64 * (gg - FIXED + 1))
                    else:
                        pe.wait_ge(m.ew_loaded[slot // 2], 32 * (gg + 1))
                pe.wait_ge(xt_done, n + 1)
                if not (first and k < 2):
                    pe.wait_ge(hid_done, n - 1)
                for c in range(KD):
                    ins = nc.tensor.matmul(ps[:, k % 2, 0:2 * I1], xgT[:, k % 4, c * P:(c + 1) * P],
                                           m.ew13[:, slot, c, :], start=(c == 0), stop=(c == KD - 1))
                ins.then_inc(gu_ps, 1)

            def turn_hid(g, k, first):
                n = ROUND * g + k
                pe.wait_ge(hid_done, n + 1)
                if not (first and k < 2):
                    pe.wait_ge(ht_done, n - 1)
                for c in range(2):
                    ins = nc.tensor.transpose(ps[0:HC, 2 + k % 2, c * P:(c + 1) * P],
                                              hid[:, k % 2, c * HC:(c + 1) * HC], m.ident[:])
                ins.then_inc(ht_ps, 1)

            def outputs(g, k, first):
                n = ROUND * g + k
                pe.wait_ge(ht_done, n + 1)
                if not (first and k < 2):
                    pe.wait_ge(y_done, n - 1)
                for c in range(2):
                    ins = nc.tensor.matmul(ps[:, 4 + k % 2, 0:D], hidT[:, k % 2, c * P:(c + 1) * P],
                                           m.ew2[:, k, c, :], start=(c == 0), stop=(c == 1))
                ins.then_inc(y_ps, 1)

            def prologue(g):
                first = g == 0
                for k in range(3):
                    turn_x(g, k, first)
                gate_up(g, 0, first)
                gate_up(g, 1, first)
                turn_hid(g, 0, first)

            def body(g, first, last):
                for k in range(ROUND):
                    if not (last and k + 3 >= ROUND):
                        turn_x(g, k + 3, first)
                    if not (last and k + 2 >= ROUND):
                        gate_up(g, k + 2, first)
                    if not (last and k + 1 >= ROUND):
                        turn_hid(g, k + 1, first)
                    outputs(g, k, first)
            all_rounds(pe, prologue, body)

        @block.scalar
        def _(act):
            def copy_x(g, k, first):
                n = ROUND * g + k
                act.wait_ge(xt_ps, n + 1)
                if not (first and k < 4):
                    act.wait_ge(gu_ps, n - 3)
                nc.scalar.copy(xgT[:, k % 4, :], ps[:, 6 + k % 2, 0:D]).then_inc(xt_done, 1)

            def silu(g, k, first):
                n = ROUND * g + k
                act.wait_ge(gu_ps, n + 1)
                if not (first and k < 2):
                    act.wait_ge(hid_done, n - 1)
                nc.scalar.activation(act_g[:, k % 2, :], ps[:, k % 2, 0:I1], ACT.Silu).then_inc(silu_done, 1)

            def prologue(g):
                first = g == 0
                for k in range(3):
                    copy_x(g, k, first)
                silu(g, 0, first)

            def body(g, first, last):
                for k in range(ROUND):
                    n = ROUND * g + k
                    if not (last and k + 3 >= ROUND):
                        copy_x(g, k + 3, first)
                    if not (last and k + 1 >= ROUND):
                        silu(g, k + 1, first)
                    act.wait_ge(ht_ps, n + 1)
                    if not (first and k < 2):
                        act.wait_ge(y_ps, n - 1)
                    nc.scalar.copy(hidT[:, k % 2, :], ps[0:HC, 2 + k % 2, 0:2 * P]).then_inc(ht_done, 1)
            all_rounds(act, prologue, body)

        @block.vector
        def _(dve):
            def multiply(g, k, first):
                n = ROUND * g + k
                dve.wait_ge(silu_done, n + 1)
                if not (first and k < 2):
                    dve.wait_ge(ht_ps, n - 1)
                nc.vector.tensor_tensor(hid[:, k % 2, :], act_g[:, k % 2, :], ps[:, k % 2, I1:2 * I1], ALU.mult
                                        ).then_inc(hid_done, 1)

            def prologue(g):
                multiply(g, 0, g == 0)

            def body(g, first, last):
                for k in range(ROUND):
                    if not (last and k + 1 >= ROUND):
                        multiply(g, k + 1, first)
                    dve.wait_ge(y_ps, ROUND * g + k + 1)
                    if k % 2 == 0 and not (first and k < 4):
                        dve.wait_ge(y_stored[(k // 2) % 2], 16 * ((PAIRS // 2) * g + k // 4))
                    nc.vector.tensor_copy(yb[:, k % 4, :], ps[:, 4 + k % 2, 0:D]).then_inc(y_done, 1)
            all_rounds(dve, prologue, body)


def combine_l1(nc, m):
    with ExitStack() as ctx:
        NB = 8
        yg = m.sb("yg", [P, NB, D], ctx=ctx)
        fetched = [m.sem(f"fetched{b}", ctx) for b in range(NB)]
        added = m.sem("c1_added", ctx)
        block = ctx.enter_context(nc.Block())
        picks = [(i, j) for i in range(NT) for j in range(TOP1)]

        @block.gpsimd
        def _(pool):
            for n, (i, j) in enumerate(picks):
                if n >= NB:
                    pool.wait_ge(added, n - NB + 1)
                nc.gpsimd.indirect_dma_start(yg[:, n % NB, :], None, m.y_slots,
                                             bass.IndirectOffsetOnAxis(m.slot[:, j, i:i + 1], 0)
                                             ).then_inc(fetched[n % NB], 16)

        @block.vector
        def _(dve):
            for n, (i, j) in enumerate(picks):
                dve.wait_ge(fetched[n % NB], 16 * (n // NB + 1))
                if j >= 1:
                    dve.wait_ge(added, n)
                nc.vector.scalar_tensor_tensor(m.xs[:, i, :], yg[:, n % NB, :], m.topw[:, i, j:j + 1], m.xs[:, i, :],
                                               ALU.mult, ALU.add).then_inc(added, 1)


def store(nc, m, out):
    with ExitStack() as ctx:
        stored = m.sem("stored", ctx)
        block = ctx.enter_context(nc.Block())

        @block.sync
        def _(sp):
            sp.dma_start(out.rearrange("b (i p) d -> p (b i) d", p=P), m.xs[:]).then_inc(stored, 16)
            sp.wait_ge(stored, 16)


def build(nc, io, out):
    with ExitStack() as ctx:
        m = Mem(nc, ctx)
        m.xs = m.sb("xs", [P, NT, D])
        m.xn = m.sb("xn", [P, NT, D])
        m.xT = m.sb("xT", [P, KD, T])
        m.bn = m.sb("bn", [P, NT, 6])
        m.mv = m.sb("mv", [P, NT, 2])
        m.rstd = m.sb("rstd", [P, 4, NT])
        m.ident = m.sb("ident", [P, P])
        m.ident_bf = m.sb("ident_bf", [P, P], BF16)
        m.ones_row = m.sb("ones_row", [1, P])
        m.comb = m.sb("comb", [P, NT, X0])
        m.gate = m.sb("gate", [P, NT])
        m.ew13 = m.sb("ew13", [P, RING, KD, 2 * I1])
        m.ew2 = m.sb("ew2", [HC, RING, 2, D])
        m.ew_loaded = [m.sem(f"ew_loaded{j}") for j in range(RING // 2)]
        m.zeroed = m.sem("zeroed")
        m.slot = m.sb("slot", [P, TOP1, NT], U32)
        m.topw = m.sb("topw", [P, NT, 8])
        m.over = m.sb("over", [1, 1 + OVER], U32)
        m.x_slots = nc.dram_tensor("x_slots", [BLOCKS * P, D], F32, kind="Internal").ap()
        m.y_slots = nc.dram_tensor("y_slots", [BLOCKS * P, D], F32, kind="Internal").ap()
        m.ps = ctx.enter_context(nc.psum_tensor("ps", [P, 8, 512], F32))
        m.stacks = {(lay.name, n): nc.dram_tensor(f"{lay.name}_{n}_stack", [B, lay.rows, lay.heads, S], BF16,
                                                  kind="Internal").ap() for lay in (L0, L1) for n in ("q", "k")}
        with ExitStack() as scope:
            m.ctxT = m.sb("ctxT_sb", [CD, T], ctx=scope)
            m.k_tm = m.sb("k_tm", [P, NT, D], ctx=scope)
            m.q_tm = m.sb("q_tm", [P, NT, D], ctx=scope)
            m.attn = m.sb("attn", [P, NT, D], ctx=scope)
            m.rest = m.sb("rest", [P, 2, SW], ctx=scope)
            m.part = m.sb("part", [P, 2, 3, SW], BF16, ctx=scope)
            with ExitStack() as layer:
                m.v0 = m.sb("v0", [P, NT, L0.heads, L0.hd + 1], ctx=layer)
                prep_l0(nc, m, io)
                m.old_sems, m.stage_sems = m.stage_sems, []
                attention(nc, m, L0, io)
                m.old_sems, m.stage_sems = m.stage_sems, []
            attention_output(nc, m, "o0_", io["L0_xattn_Wout"], io["L0_xattn_bout"])
            route_l0(nc, m, io)
            experts_l0(nc, m, io)
            with ExitStack() as layer:
                m.v1 = m.sb("v1", [P, NT, L1.heads, L1.vw], ctx=layer)
                prep_l1(nc, m, io)
                attention(nc, m, L1, io)
            attention_output(nc, m, "o1_", io["L1_xattn_Wo"], io["L1_xattn_bo"])
        route_l1(nc, m, io)
        shared_l1(nc, m, io)
        routed_l1(nc, m, io)
        combine_l1(nc, m)
        store(nc, m, out)


def host_layout(inputs):
    io = {n: np.ascontiguousarray(a) for n, a in inputs.items()}
    io["ctxT"] = np.ascontiguousarray(np.asarray(io.pop("ctx_1024")).reshape(T, CD).T)
    io["ident"] = np.eye(P, dtype=np.float32)
    io["ones_row"] = np.ones((1, P), np.float32)
    io["l0_ones"] = np.ones((2, G, S), np.float32)
    keys = np.arange(S) < MAIN
    io["l1_ones"] = np.broadcast_to(np.stack([keys, keys, ~keys, ~keys])[:, None, :], (4, G, S)).astype(np.float32)
    for lay in (L0, L1):
        tiles = 4 // lay.shifts
        sel = np.zeros((tiles, P // tiles, tiles, lay.vw), np.float32)
        for j in range(tiles):
            sel[j, :lay.vw, j] = np.eye(lay.vw)
        io[lay.name + "_sel"] = sel.reshape(P, tiles * lay.vw)
    io["tmask"] = np.stack([keys, ~keys]).astype(np.float32)[None]
    io["pmask"] = np.ascontiguousarray(io["tmask"].reshape(2, QT, P).transpose(2, 1, 0))
    io["iota"] = np.arange(P, dtype=np.float32)
    io["later"] = np.tril(np.ones((GRP, GRP), np.float32), -1)
    io["L0_router_T"] = np.ascontiguousarray(io["L0_ffn_router_weight"].T)
    up, down = io.pop("L0_ffn_shared_up"), io.pop("L0_ffn_shared_down")
    io["L0_up"] = np.concatenate([io.pop("L0_ffn_w_up"), up.reshape(D, SH0, I0).transpose(1, 0, 2)])
    io["L0_down"] = np.concatenate([io.pop("L0_ffn_w_down"), down.reshape(SH0, I0, D)])
    wmain = np.concatenate([io.pop("L1_xattn_Wk"), io.pop("L1_xattn_Wv")], axis=1)
    bmain = np.concatenate([io.pop("L1_xattn_bk"), io.pop("L1_xattn_bv")])[None]
    io["L1_wmain"], io["L1_bmain"] = (
        np.ascontiguousarray(a.reshape(-1, L1.heads, 2, L1.hd).transpose(0, 2, 1, 3).reshape(-1, 2 * D))
        for a in (wmain, bmain))
    io["L1_gates_T"] = np.concatenate([io.pop("L1_ffn_gate_w"), io.pop("L1_ffn_shared_gate_w")]).T.copy()
    gate_up, down = io.pop("L1_ffn_se_gate_up_w"), io.pop("L1_ffn_se_down_w")
    w13 = gate_up.reshape(2, SH1, I1, D).transpose(1, 0, 2, 3).reshape(SH1, 2 * I1, D)
    io["L1_shared_w13"] = w13.transpose(0, 2, 1).copy()
    io["L1_shared_w2"] = down.T.reshape(SH1, I1, D).copy()
    io["L1_w13"] = io.pop("L1_ffn_w13").transpose(0, 2, 1).copy()
    io["L1_w2"] = io.pop("L1_ffn_w2").transpose(0, 2, 1).copy()
    io["upper"] = np.triu(np.ones((P, P), np.float32), 1)
    return io


def kernel(**inputs):
    import concourse.bacc as bacc
    from concourse.bass_utils import run_bass_kernel_spmd

    arrays = host_layout(inputs)
    nc = bacc.Bacc("TRN2", target_bir_lowering=False, num_devices=1)
    io = {n: nc.dram_tensor("in_" + n, a.shape, mybir.dt.from_np(a.dtype), kind="ExternalInput").ap()
          for n, a in arrays.items()}
    out = nc.dram_tensor("out_x", (B, S, D), F32, kind="ExternalOutput").ap()
    build(nc, io, out)
    r = run_bass_kernel_spmd(nc, [{"in_" + n: a for n, a in arrays.items()}], core_ids=[0])
    return r.results[0]["out_x"]
```

```python
from contextlib import ExitStack

import numpy as np

import concourse.bass as bass
from concourse import mybir
from concourse.alu_op_type import AluOpType as ALU

ACT = mybir.ActivationFunctionType
F32 = mybir.dt.float32
BF16 = mybir.dt.bfloat16
U32 = mybir.dt.uint32
AX_X = mybir.AxisListType.X

P = 128
D = 256
KD = D // P
B = 4
S = 256
T = B * S
NT = T // P
QT = S // P
CD = 128
G = 8
PARTS = 6
Q_ROWS = (slice(0, 3), slice(3, 6, 2), slice(4, 5))
K_ROWS = (slice(2, 5), slice(0, 6, 5), slice(1, 2))
DCA = 16
MAIN = S - DCA
ROUNDER = 1.5 * 2.0 ** 23
PI_BELOW = 3.1415925


def bcast(ap, axis, n):
    a = ap.unsqueeze(axis)
    shape = list(a.shape)
    shape[axis] = n
    return a.broadcast_to(shape)


class Layer:

    def __init__(self, name, heads, shifts, scale):
        self.name = name
        self.heads = heads
        self.hd = D // heads
        self.rows = PARTS * self.hd
        self.shifts = shifts
        self.krows = self.rows + 2 * shifts
        self.vw = shifts * (self.hd + 1)
        self.scale = scale
        self.groups = heads // G
        self.units = B * self.groups
        self.row_tiles = 2 if self.krows <= P // 2 else 1

    def place(self, i, k):
        return (i + k * G // 2, k * P // 2, i) if self.row_tiles == 2 else (2 * i + k, 0, 2 * i + k)


L0 = Layer("l0", 32, 1, float(1.0 / np.sqrt(np.float32(8))))
L1 = Layer("l1", 16, 2, 0.25)


class Chain:

    def __init__(self, eng, sem, base=0):
        self.eng, self.sem, self.base, self.n = eng, sem, base, 0

    def link(self, ins):
        self.n += 1
        ins.then_inc(self.sem, 1)
        self.eng.wait_ge(self.sem, self.base + self.n)


class Mem:

    def __init__(self, nc, ctx):
        self.nc, self.ctx = nc, ctx
        self.stage_sems, self.old_sems = [], []

    def sb(self, name, shape, dt=F32, ctx=None):
        return (ctx or self.ctx).enter_context(self.nc.sbuf_tensor(name, shape, dt))

    def sem(self, name, ctx=None):
        s = (ctx or self.ctx).enter_context(self.nc.semaphore(name))
        if ctx is not None:
            self.stage_sems.append(s)
        return s

    def clear_sems(self, dve):
        for s in self.old_sems:
            dve.sem_clear(s)
        self.old_sems = []


def rsqrt_vector(nc, dve, chain, var, eps, work, root_in, root_out):
    v, y, r, t = work
    if eps is not None:
        chain.link(nc.vector.tensor_scalar(v, var, eps, None, ALU.add))
    nc.vector.reciprocal(t, v).then_inc(root_in, 1)
    dve.wait_ge(root_out, 1)
    chain.link(nc.vector.tensor_tensor(t, y, y, ALU.mult))
    chain.link(nc.vector.tensor_tensor(r, t, v, ALU.mult))
    chain.link(nc.vector.tensor_scalar(t, r, -0.5, 1.5, ALU.mult, ALU.add))
    chain.link(nc.vector.tensor_tensor(r, y, t, ALU.mult))


def layernorm_vector(nc, dve, chain, m, eps, root_in, root_out, xn_ready):
    for i in range(NT):
        ins = nc.vector.bn_stats(m.bn[:, i, :], m.xs[:, i, :])
    chain.link(ins)
    for i in range(NT):
        ins = nc.vector.bn_aggr(m.mv[:, i, :], m.bn[:, i, :])
    chain.link(ins)
    rsqrt_vector(nc, dve, chain, m.mv[:, :, 1], eps, [m.rstd[:, j, :] for j in range(4)], root_in, root_out)
    for i in range(NT):
        nc.vector.tensor_scalar(m.xn[:, i, :], m.xs[:, i, :], m.mv[:, i, 0:1], m.rstd[:, 2, i:i + 1],
                                ALU.subtract, ALU.mult).then_inc(xn_ready, 1)


def layernorm_scalar(nc, act, m, root_in, root_out):
    act.wait_ge(root_in, 1)
    nc.scalar.activation(m.rstd[:, 1, :], m.rstd[:, 3, :], ACT.Sqrt).then_inc(root_out, 1)


def transpose_tile(nc, m, bank, src):
    for c in range(KD):
        ins = nc.tensor.transpose(m.ps[:, bank, c * P:(c + 1) * P], src[:, c * P:(c + 1) * P], m.ident[:])
    return ins


def transposed_copy(nc, m, i, bank, dst):
    return nc.scalar.copy(dst[:, :, i * P:(i + 1) * P],
                          m.ps[:, bank, 0:D].rearrange("p (c t) -> p c t", c=KD))


def matmul_tile(nc, out, xT, i, w, bias=None, ones=None):
    for c in range(KD):
        ins = nc.tensor.matmul(out, xT[:, c, i * P:(i + 1) * P], w[:, c, :], start=(c == 0),
                               stop=(c == KD - 1 and bias is None))
    if bias is not None:
        ins = nc.tensor.matmul(out, ones, bias, start=False, stop=True)
    return ins


SPLITS = [(src, half, th) for src in ("k", "q") for half in range(KD) for th in range(2)]
SW = 4 * P
WRITES = 3


def split_tensor(nc, pe, m, s, tiles_ready, parts_taken):
    src, half, th = SPLITS[s]
    tile = m.k_tm if src == "k" else m.q_tm
    pe.wait_ge(tiles_ready, (0 if src == "k" else NT) + 4 * th + 4)
    if s >= 2:
        pe.wait_ge(parts_taken, s - 1)
    for j in range(4):
        ins = nc.tensor.transpose(m.ps[:, 6 + s % 2, j * P:(j + 1) * P],
                                  tile[:, 4 * th + j, half * P:(half + 1) * P], m.ident[:])
    return ins


def split_writes(sp, m, s, part_dma):
    src, half, th = SPLITS[s]
    for part, rows in enumerate(Q_ROWS if src == "q" else K_ROWS):
        dst = m.stacks[src][half * P:(half + 1) * P, rows, th * SW:(th + 1) * SW]
        sp.dma_start(dst, bcast(m.part[:, s % 2, part, :], 1, dst.shape[1])
                     ).then_inc(part_dma[s % 2], 16)


def prep_l0(nc, m, io):
    lay = L0
    with ExitStack() as ctx:
        def sem(n):
            return m.sem("p0_" + n, ctx)
        wq = m.sb("p0_wq", [P, KD, D], ctx=ctx)
        wkv = m.sb("p0_wkv", [P, 2 * D], ctx=ctx)
        ang = m.sb("p0_ang", [P, 2, NT, 4], ctx=ctx)
        trig = m.sb("p0_trig", [P, 2, NT, 4], ctx=ctx)
        turns = m.sb("p0_turns", [P, 2, NT, 4], ctx=ctx)
        pos = m.sb("p0_pos", [P, NT, 2], ctx=ctx)
        rot = m.sb("p0_rot", [P, 2, 2, D], ctx=ctx)
        ld_const, ld_x, ld_ctx, ld_wkv, ld_wq, ld_pos = (sem(n) for n in (
            "ld_const", "ld_x", "ld_ctx", "ld_wkv", "ld_wq", "ld_pos"))
        step, xn_ready, xt_ps, xt_ready = sem("step"), sem("xn_ready"), sem("xt_ps"), sem("xt_ready")
        kv_ps, v_copied, q_ps, rot_ready, rot_done = (sem(n) for n in (
            "kv_ps", "v_copied", "q_ps", "rot_ready", "rot_done"))
        ang_ready, trig_ready, root_in, root_out = (sem(n) for n in ("ang_ready", "trig_ready", "root_in", "root_out"))
        split_ps, hi_ready, rest_ready, mid_ready, lo_ready, ones_set = (sem(n) for n in (
            "split_ps", "hi_ready", "rest_ready", "mid_ready", "lo_ready", "ones_set"))
        part_dma = [sem("part_dma0"), sem("part_dma1")]
        ps = m.ps
        block = ctx.enter_context(nc.Block())

        @block.sync
        def _(sp):
            sp.dma_start(m.xs[:], io["x"].rearrange("b (i p) d -> p (b i) d", p=P)).then_inc(ld_x, 16)
            for dst, name in ((m.ident, "ident"), (m.ones_row, "ones_row")):
                sp.dma_start(dst[:], io[name]).then_inc(ld_const, 16)
            sp.dma_start(m.ctxT[:], io["ctxT"]).then_inc(ld_ctx, 16)
            sp.dma_start(wkv[:], io["L0_xattn_Wkv"]).then_inc(ld_wkv, 16)
            sp.dma_start(pos[:], io["fside_BxSx2_0"].rearrange("b (i p) c -> p (b i) c", p=P)).then_inc(ld_pos, 16)
            sp.dma_start(wq[:], io["L0_xattn_Wq"].rearrange("(c p) n -> p c n", p=P)).then_inc(ld_wq, 16)
            for s in range(len(SPLITS)):
                sp.wait_ge(lo_ready, s + 1)
                sp.wait_ge(mid_ready, s + 1)
                split_writes(sp, m, s, part_dma)
            for b in range(2):
                sp.wait_ge(part_dma[b], 16 * WRITES * len(SPLITS) // 2)

        @block.tensor
        def _(pe):
            pe.wait_ge(ld_ctx, 16)
            pe.wait_ge(ld_wkv, 16)
            for i in range(NT):
                if i >= 2:
                    pe.wait_ge(v_copied, i - 1)
                    pe.wait_ge(rot_ready, i - 1)
                for side in range(2):
                    ins = nc.tensor.matmul(ps[:, 2 * side + i % 2, 0:D], m.ctxT[:, i * P:(i + 1) * P],
                                           wkv[:, side * D:(side + 1) * D], start=True, stop=True)
                ins.then_inc(kv_ps, 1)
            pe.wait_ge(v_copied, NT)
            pe.wait_ge(ld_const, 32)
            pe.wait_ge(ld_wq, 16)
            for i in range(NT + 1):
                if i < NT:
                    pe.wait_ge(xn_ready, i + 1)
                    if i >= 2:
                        pe.wait_ge(xt_ready, i - 1)
                    transpose_tile(nc, m, 2 + i % 2, m.xn[:, i, :]).then_inc(xt_ps, 1)
                if i >= 1:
                    t = i - 1
                    pe.wait_ge(xt_ready, t + 1)
                    if t >= 2:
                        pe.wait_ge(rot_ready, NT + t - 1)
                    matmul_tile(nc, ps[:, 4 + t % 2, 0:D], m.xT, t, wq).then_inc(q_ps, 1)
            for s in range(len(SPLITS)):
                split_tensor(nc, pe, m, s, rot_done, rest_ready).then_inc(split_ps, 1)

        @block.vector
        def _(dve):
            chain = Chain(dve, step)
            dve.wait_ge(ld_pos, 16)
            for f, freq in enumerate((1.0, 10000.0 ** -0.5)):
                for k, phase in enumerate((0.0, np.pi / 2)):
                    ins = nc.vector.tensor_scalar(ang[:, k, :, f::2], pos[:], float(np.float32(freq)),
                                                  float(phase), ALU.mult, ALU.add)
            chain.link(ins)
            chain.link(nc.vector.tensor_scalar(turns[:], ang[:], float(0.5 / np.pi), ROUNDER, ALU.mult, ALU.add))
            chain.link(nc.vector.tensor_scalar(trig[:], turns[:], ROUNDER, float(-2 * np.pi), ALU.subtract, ALU.mult))
            chain.link(nc.vector.tensor_tensor(turns[:], trig[:], ang[:], ALU.add))
            nc.vector.tensor_scalar(ang[:], turns[:], PI_BELOW, -PI_BELOW, ALU.min, ALU.max).then_inc(ang_ready, 1)
            nc.vector.memset(m.v0[:, :, :, lay.hd:lay.hd + 1], 1.0).then_inc(ones_set, 1)
            dve.wait_ge(ld_x, 16)
            layernorm_vector(nc, dve, chain, m, 1e-5, root_in, root_out, xn_ready)
            dve.wait_ge(trig_ready, 1)
            for n in range(2 * NT):
                i, k_side = n % NT, n < NT
                dve.wait_ge(kv_ps if k_side else q_ps, i + 1)
                if n >= 2:
                    dve.wait_ge(rot_done, n - 1)
                src = ps[:, (0 if k_side else 4) + i % 2, 0:D].rearrange("p (h a e) -> p h (a e)", h=32, a=4)
                src = src.rearrange("p h (a e) -> p h a e", a=4)
                for k in range(2):
                    w = trig[:, k, i, :]
                    wb = w.unsqueeze(1).unsqueeze(3).broadcast_to([P, 32, 4, 2])
                    ins = nc.vector.tensor_tensor(rot[:, n % 2, k, :].rearrange("p (h a e) -> p h a e", h=32, a=4),
                                                  src, wb, ALU.mult)
                ins.then_inc(rot_ready, 1)
            for s in range(len(SPLITS)):
                dve.wait_ge(hi_ready, s + 1)
                if s >= 2:
                    dve.wait_ge(lo_ready, s - 1)
                nc.vector.tensor_tensor(m.rest[:, s % 2, :], ps[:, 6 + s % 2, :], m.part[:, s % 2, 0, :],
                                        ALU.subtract).then_inc(rest_ready, 1)

        @block.scalar
        def _(act):
            act.wait_ge(ang_ready, 1)
            nc.scalar.activation(trig[:], ang[:], ACT.Sin).then_inc(trig_ready, 1)
            layernorm_scalar(nc, act, m, root_in, root_out)
            act.wait_ge(ones_set, 1)
            for i in range(NT):
                act.wait_ge(kv_ps, i + 1)
                nc.scalar.copy(m.v0[:, i, :, 0:lay.hd],
                               ps[:, 2 + i % 2, 0:D].rearrange("p (h e) -> p h e", h=32)).then_inc(v_copied, 1)
            for i in range(NT):
                act.wait_ge(xt_ps, i + 1)
                transposed_copy(nc, m, i, 2 + i % 2, m.xT).then_inc(xt_ready, 1)
            split_scalar(nc, act, m, split_ps, part_dma, hi_ready, rest_ready, mid_ready)

        @block.gpsimd
        def _(pool):
            pool.wait_ge(ld_const, 32)
            nc.gpsimd.tensor_copy(m.ident_bf[:], m.ident[:])
            for n in range(2 * NT):
                i = n % NT
                dst = (m.k_tm if n < NT else m.q_tm)[:, i, :].rearrange("p (a e) -> p a e", e=2)
                sin = rot[:, n % 2, 0, :].rearrange("p (a e) -> p a e", e=2)
                cos = rot[:, n % 2, 1, :].rearrange("p (a e) -> p a e", e=2)
                pool.wait_ge(rot_ready, n + 1)
                nc.gpsimd.tensor_tensor(dst[:, :, 0], cos[:, :, 0], sin[:, :, 1], ALU.subtract)
                nc.gpsimd.tensor_tensor(dst[:, :, 1], sin[:, :, 0], cos[:, :, 1], ALU.add).then_inc(rot_done, 1)
            split_gpsimd(nc, pool, m, mid_ready, rest_ready, part_dma, lo_ready)


def split_scalar(nc, act, m, split_ps, part_dma, hi_ready, rest_ready, mid_ready):
    for s in range(len(SPLITS)):
        act.wait_ge(split_ps, s + 1)
        if s >= 2:
            act.wait_ge(part_dma[s % 2], 16 * WRITES * (s // 2))
        nc.scalar.copy(m.part[:, s % 2, 0, :], m.ps[:, 6 + s % 2, :]).then_inc(hi_ready, 1)
        act.wait_ge(rest_ready, s + 1)
        nc.scalar.copy(m.part[:, s % 2, 1, :], m.rest[:, s % 2, :]).then_inc(mid_ready, 1)


def split_gpsimd(nc, pool, m, mid_ready, rest_ready, part_dma, lo_ready):
    for s in range(len(SPLITS)):
        pool.wait_ge(rest_ready, s + 1)
        pool.wait_ge(mid_ready, s + 1)
        if s >= 2:
            pool.wait_ge(part_dma[s % 2], 16 * WRITES * (s // 2))
        nc.gpsimd.tensor_tensor(m.part[:, s % 2, 2, :], m.rest[:, s % 2, :], m.part[:, s % 2, 1, :],
                                ALU.subtract).then_inc(lo_ready, 1)


def zero_slots(nc, pool, m, zeros, zero_set, t_ps, unit):
    nc.gpsimd.memset(zeros[:], 0.0).then_inc(zero_set, 1)
    pool.wait_ge(zero_set, 1)
    writes = [(m.x_slots, r) for r in range(BLOCKS // ROUND)] + \
             [(m.y_slots, r) for r in range(E1 // ROUND, BLOCKS // ROUND)]
    for n, (slots, r) in enumerate(writes):
        pool.wait_ge(t_ps, unit * (n + 1))
        rows = slots[r * ROUND * P:(r + 1) * ROUND * P, :].rearrange("(b p) d -> p b d", p=P)
        pool.dma_start(rows, bcast(zeros[:], 1, ROUND)).then_inc(m.zeroed, 16)


NBUF = 4
AHEAD = 2
PROBS = 4
LAG = 1
TURN_LAG = 2


def attention(nc, m, lay, io):
    U, GR, R, SH, W, hd = lay.units, lay.groups, lay.rows, lay.shifts, lay.vw, lay.hd
    cuts = ((0, S),) if SH == 1 else ((0, MAIN), (MAIN, S))
    v = m.v0 if lay is L0 else m.v1
    ps = m.ps
    CT = 4 // SH
    HG = 2 * CT
    NG = G // HG
    UP = G // 2
    PAIRS = U * UP
    RT = lay.row_tiles
    tiles = [k * P // 2 for k in range(RT)]
    GT = G // RT
    with ExitStack() as ctx:
        def sem(n):
            return m.sem(lay.name + "a_" + n, ctx)
        qs = m.sb(lay.name + "_qs", [tiles[-1] + lay.krows, NBUF, GT, S], BF16, ctx)
        ks = m.sb(lay.name + "_ks", [tiles[-1] + lay.krows, NBUF, GT, S], BF16, ctx)
        prob = m.sb(lay.name + "_prob", [P, PROBS, 2, QT, S], ctx=ctx)
        mx = m.sb(lay.name + "_mx", [P, 2, QT, SH, G], ctx=ctx)
        neg = m.sb(lay.name + "_neg", [P, 2, QT, SH, 2, G], BF16, ctx)
        negT = m.sb(lay.name + "_negT", [2 * SH * G, 2, S], BF16, ctx)
        sumsT = m.sb(lay.name + "_sumsT", [P, 2, 2 * S], ctx=ctx)
        zero_row = m.sb(lay.name + "_zero_row", [1, 2 * S], ctx=ctx)
        rec = m.sb(lay.name + "_rec", [P, QT, CT * SH], ctx=ctx)
        ctxv = m.sb(lay.name + "_ctxv", [P, QT, CT * SH, hd], ctx=ctx)
        if lay is L0:
            zeros, zero_set = m.sb("zeros", [P, D], ctx=ctx), sem("zero_set")
        loaded = [sem(f"loaded{b}") for b in range(NBUF)]
        shifted = [sem(f"shifted{b}") for b in range(NBUF)]
        ones_ld, zero_row_set = sem("ones_ld"), sem("zero_row_set")
        s_ps, s_max, step, neg_ready = sem("s_ps"), sem("s_max"), sem("step"), sem("neg_ready")
        negT_ps, negT_ready, t_ps, t_exp = sem("negT_ps"), sem("negT_ready"), sem("t_ps"), sem("t_exp")
        weighed, sums_copied, tok_ps, tok_used = sem("weighed"), sem("sums_copied"), sem("tok_ps"), sem("tok_used")
        block = ctx.enter_context(nc.Block())

        def turn_at(n):
            past = n - TURN_LAG - (CT - 1)
            return past // CT * 2 + past % CT if past >= 0 and past % CT < 2 and past // CT * CT < PAIRS else None

        @block.sync
        def _(sp):
            def load(u, b):
                bt, g = u // GR, u % GR
                for dst, src in ((qs, "q"), (ks, "k")):
                    for k, row in enumerate(tiles):
                        dims = (g * G + k * GT) * hd
                        stack = m.stacks[src][dims:dims + GT * hd, :, bt * S:(bt + 1) * S]
                        sp.dma_start(dst[row:row + R, b, :, :], stack.rearrange("(h d) j t -> (d j) h t", d=hd)
                                     ).then_inc(loaded[b], 16)

            def shift_rows(u, b):
                sp.wait_ge(negT_ready, u + 1)
                for k, row in enumerate(tiles):
                    for r in range(2 * SH):
                        sp.dma_start(qs[row + R + r:row + R + r + 1, b, :, :],
                                     negT[r * G + k * GT:r * G + (k + 1) * GT, b % 2, :]).then_inc(shifted[b], 16)

            for u in range(NBUF):
                load(u, u)
            for u in range(U):
                shift_rows(u, u % NBUF)
                if u >= AHEAD and u + NBUF - AHEAD < U:
                    n = u - AHEAD
                    sp.wait_ge(t_ps, UP * (n + 1))
                    load(n + NBUF, n % NBUF)

        @block.gpsimd
        def _(pool):
            nc.gpsimd.memset(zero_row[:], 0.0).then_inc(zero_row_set, 1)
            for b in range(NBUF):
                for row in tiles:
                    pool.dma_start(ks[row + R:row + lay.krows, b, :, :], io[lay.name + "_ones"][:, 0:GT, :]
                                   ).then_inc(ones_ld, 16)
            if lay is L0:
                zero_slots(nc, pool, m, zeros, zero_set, t_ps, UP)

        @block.tensor
        def _(pe):
            turned = [0]
            maxed = [0]

            def scores(n):
                u, i = n // UP, n % UP
                if i == 0:
                    pe.wait_ge(loaded[u % NBUF], 32 * RT * (u // NBUF + 1))
                if n >= 1:
                    pe.wait_ge(s_max, n)
                for qt in range(QT):
                    for k in range(2):
                        _, row, col = lay.place(i, k)
                        ins = nc.tensor.matmul(ps[:, k, qt * S:(qt + 1) * S],
                                               qs[row:row + R, u % NBUF, col, qt * P:(qt + 1) * P],
                                               ks[row:row + R, u % NBUF, col, :], start=True, stop=True)
                ins.then_inc(s_ps, 1)

            def transposed_maxima(u):
                pe.wait_ge(neg_ready, u + 1)
                if u >= 1:
                    pe.wait_ge(negT_ready, u)
                if turned[0]:
                    pe.wait_ge(tok_used, turned[0])
                out = ps[0:2 * SH * G, 7, 384:512].bitcast(BF16)
                for qt in range(QT):
                    ins = nc.tensor.transpose(out[:, qt * P:(qt + 1) * P],
                                              neg[:, u % 2, qt, :, :, :].rearrange("p s k g -> p (s k g)"),
                                              m.ident_bf[:])
                ins.then_inc(negT_ps, 1)
                maxed[0] += 1

            def shifted_scores(n):
                u, i = n // UP, n % UP
                b = u % NBUF
                if i == 0:
                    pe.wait_ge(shifted[b], 32 * SH * RT * (u // NBUF + 1))
                if n >= 2:
                    pe.wait_ge(t_exp, n - 1)
                for kt in range(QT):
                    for k in range(2):
                        _, row, col = lay.place(i, k)
                        ins = nc.tensor.matmul(ps[:, 2 + 2 * (n % 2) + k, kt * S:(kt + 1) * S],
                                               ks[row:row + lay.krows, b, col, kt * P:(kt + 1) * P],
                                               qs[row:row + lay.krows, b, col, :], start=True, stop=True)
                ins.then_inc(t_ps, 1)

            def values(c):
                pe.wait_ge(t_exp, CT * (c + 1) // 2)
                if c % 2 == 0 and c >= 2:
                    pe.wait_ge(sums_copied, c // 2)
                for kt in range(QT):
                    for j in range(CT):
                        n, k = CT // 2 * c + j % (CT // 2), j // (CT // 2)
                        head = n // UP % GR * G + lay.place(n % UP, k)[0]
                        row = j * P // CT
                        ins = nc.tensor.matmul(ps[row:row + W, 6, (c % 2) * S:(c % 2 + 1) * S],
                                               v[:, n // UP // GR * QT + kt, head, :], prob[:, n % PROBS, k, kt, :],
                                               start=(kt == 0), stop=(kt == QT - 1))
                ins.then_inc(weighed, 1)

            def token_sums(c):
                gi = c // 2
                pe.wait_ge(sums_copied, gi + 1)
                if c >= 1:
                    pe.wait_ge(tok_used, c)
                pe.wait_ge(negT_ready, maxed[0])
                for q in range(QT):
                    ins = nc.tensor.transpose(ps[:, 7, q * P:(q + 1) * P],
                                              sumsT[:, gi % 2, (c % 2) * S + q * P:(c % 2) * S + (q + 1) * P],
                                              m.ident[:])
                ins.then_inc(tok_ps, 1)
                turned[0] += 1

            pe.wait_ge(zero_row_set, 1)
            nc.tensor.matmul(ps[:, 6, :], m.ones_row[:], zero_row[:], start=True, stop=True)
            for n in range(AHEAD * UP):
                scores(n)
                if n == UP:
                    transposed_maxima(0)
            pe.wait_ge(ones_ld, 16 * RT * NBUF)
            for n in range(PAIRS + TURN_LAG + 1):
                if n + AHEAD * UP < PAIRS:
                    scores(n + AHEAD * UP)
                if n < PAIRS:
                    shifted_scores(n)
                    if n % UP == 0 and n // UP + 1 < U:
                        transposed_maxima(n // UP + 1)
                if n >= LAG and (n - LAG + 1) % (CT // 2) == 0 and n - LAG < PAIRS:
                    values((n - LAG + 1) // (CT // 2) - 1)
                if turn_at(n) is not None:
                    token_sums(turn_at(n))

        @block.vector
        def _(dve):
            m.clear_sems(dve)
            chain = Chain(dve, step)

            def maxima(n):
                u, i = n // UP, n % UP
                first, second = (lay.place(i, k)[0] for k in range(2))
                dve.wait_ge(s_ps, n + 1)
                for s, (lo, hi) in enumerate(cuts):
                    ins = nc.vector.reduce_max(
                        mx[:, u % 2, :, s, first:second + 1:second - first].rearrange("p q k -> p k q"),
                        ps[:, 0:2, :].rearrange("p k (q t) -> p k q t", q=QT)[:, :, :, lo:hi], AX_X)
                ins.then_inc(s_max, 1)

            def negated(u):
                dve.wait_ge(s_max, UP * (u + 1))
                if u >= 2:
                    dve.wait_ge(negT_ps, u - 1)
                chain.link(nc.vector.tensor_scalar(neg[:, u % 2, :, :, 0, :], mx[:, u % 2, :, :, :],
                                                   -1.0, None, ALU.mult))
                for q in range(QT):
                    ins = nc.vector.scalar_tensor_tensor(neg[:, u % 2, q, :, 1, :], mx[:, u % 2, q, :, :], -1.0,
                                                         neg[:, u % 2, q, :, 0, :], ALU.mult, ALU.subtract)
                ins.then_inc(neg_ready, 1)

            def normalise(c):
                gi = c // 2
                u = gi // NG
                bt, col = u // GR, (u % GR * G + gi % NG * HG) * hd
                sums = ps[:, 7, 0:QT * P].rearrange("p (q n r) -> p q n r", q=QT, n=CT)[:, :, :, 0:W]
                sums = sums.rearrange("p q n (s e) -> p q n s e", s=SH)
                dve.wait_ge(tok_ps, c + 1)
                chain.link(nc.vector.reciprocal(rec[:].rearrange("p q (n s) -> p q n s", s=SH),
                                                sums[:, :, :, :, hd]))
                for q in range(QT):
                    dst = m.attn[:, bt * QT + q, col:col + HG * hd]
                    weight = bcast(rec[:, q, :], 2, hd)
                    if SH == 1:
                        out = dst.rearrange("p (k c n e) -> p k c n e", k=2, c=2, n=2)[:, :, c % 2, :, :]
                        src = sums[:, q, :, 0, 0:hd].rearrange("p (k n) e -> p k n e", k=2)
                        weight = weight.rearrange("p (k n) e -> p k n e", k=2)
                    else:
                        out = ctxv[:, q, :, :].rearrange("p (n s) e -> p n s e", s=SH)
                        src = sums[:, q, :, :, 0:hd]
                        weight = weight.rearrange("p (n s) e -> p n s e", s=SH)
                    ins = nc.vector.tensor_tensor(out, src, weight, ALU.mult)
                ins.then_inc(tok_used, 1)
                if SH == 2:
                    dve.wait_ge(tok_used, c + 1)
                    parts = ctxv[:].rearrange("p q (n s) e -> p q n s e", s=SH)
                    dst = m.attn[:, bt * QT:(bt + 1) * QT, col + c % 2 * CT * hd:col + (c % 2 + 1) * CT * hd]
                    nc.vector.tensor_tensor(dst.rearrange("p q (n e) -> p q n e", e=hd),
                                            parts[:, :, :, 0, :], parts[:, :, :, 1, :], ALU.add)

            for n in range(AHEAD * UP):
                maxima(n)
                if n % UP == UP - 1:
                    negated(n // UP)
            for n in range(PAIRS + TURN_LAG + 1):
                if n + AHEAD * UP < PAIRS:
                    maxima(n + AHEAD * UP)
                    if n % UP == UP - 1:
                        negated(n // UP + AHEAD)
                if turn_at(n) is not None:
                    normalise(turn_at(n))

        @block.scalar
        def _(act):
            def maxima_rows(u):
                act.wait_ge(negT_ps, u + 1)
                if u >= 2:
                    act.wait_ge(shifted[(u - 2) % NBUF], 32 * SH * RT * ((u - 2) // NBUF + 1))
                nc.scalar.copy(negT[:, u % 2, :], ps[0:2 * SH * G, 7, 384:512].bitcast(BF16)
                               ).then_inc(negT_ready, 1)

            def exponentials(n):
                act.wait_ge(t_ps, n + 1)
                if n >= PROBS:
                    act.wait_ge(weighed, 2 * (n - PROBS) // CT + 1)
                nc.scalar.activation(prob[:, n % PROBS, :, :, :].rearrange("p h k q -> p (h k q)"),
                                     ps[:, 2 + 2 * (n % 2):4 + 2 * (n % 2), :].rearrange("p b n -> p (b n)"),
                                     ACT.Exp, scale=lay.scale).then_inc(t_exp, 1)

            def copied_sums(gi):
                act.wait_ge(weighed, 2 * (gi + 1))
                if gi >= 2:
                    act.wait_ge(tok_ps, 2 * (gi - 1))
                nc.scalar.copy(sumsT[:, gi % 2, :], ps[:, 6, :]).then_inc(sums_copied, 1)

            maxima_rows(0)
            for n in range(PAIRS + 1):
                if n < PAIRS:
                    exponentials(n)
                    if n % UP == 0 and n // UP + 1 < U:
                        maxima_rows(n // UP + 1)
                if n >= CT and n % CT == 0:
                    copied_sums(n // CT - 1)


def attention_output(nc, m, name, w_dram, b_dram):
    with ExitStack() as ctx:
        def sem(n):
            return m.sem(name + n, ctx)
        w = m.sb(name + "w", [P, KD, D], ctx=ctx)
        b = m.sb(name + "b", [1, D], ctx=ctx)
        ld, at_ps, at_ready, out_ps, out_used = (sem(n) for n in ("ld", "at_ps", "at_ready", "out_ps", "out_used"))
        block = ctx.enter_context(nc.Block())

        @block.sync
        def _(sp):
            sp.dma_start(w[:], w_dram.rearrange("(c p) n -> p c n", p=P)).then_inc(ld, 16)
            sp.dma_start(b[:], b_dram.rearrange("(a n) -> a n", a=1)).then_inc(ld, 16)

        @block.tensor
        def _(pe):
            for i in range(NT + 1):
                if i < NT:
                    if i >= 2:
                        pe.wait_ge(at_ready, i - 1)
                    transpose_tile(nc, m, i % 2, m.attn[:, i, :]).then_inc(at_ps, 1)
                if i == 1:
                    pe.wait_ge(ld, 32)
                if i >= 1:
                    t = i - 1
                    pe.wait_ge(at_ready, t + 1)
                    if t >= 2:
                        pe.wait_ge(out_used, t - 1)
                    matmul_tile(nc, m.ps[:, 2 + t % 2, 0:D], m.xT, t, w, b[:], m.ones_row[:]).then_inc(out_ps, 1)

        @block.scalar
        def _(act):
            for i in range(NT):
                act.wait_ge(at_ps, i + 1)
                transposed_copy(nc, m, i, i % 2, m.xT).then_inc(at_ready, 1)

        @block.vector
        def _(dve):
            for i in range(NT):
                dve.wait_ge(out_ps, i + 1)
                nc.vector.tensor_tensor(m.xs[:, i, :], m.xs[:, i, :], m.ps[:, 2 + i % 2, 0:D],
                                        ALU.add).then_inc(out_used, 1)


def rounds(eng, n, body):
    body(0, True, n == 1)
    if n == 3:
        body(1, False, False)
    elif n > 3:
        with eng.Fori(1, n - 1) as g:
            body(g, False, False)
    if n > 1:
        body(n - 1, False, True)


E0, I0 = 16, 128
SH0 = 512 // I0
X0 = E0 + SH0
GRP, GSZ = 4, 4


def route_l0(nc, m, io):
    with ExitStack() as ctx:
        def sem(n):
            return m.sem("r0_" + n, ctx)

        def sb(n, shape, dt=F32):
            return m.sb("r0_" + n, [P] + shape, dt, ctx)
        rw, bias, iota = sb("rw", [KD, E0]), sb("bias", [E0]), sb("iota", [E0])
        score, biased = sb("score", [NT, E0]), sb("biased", [NT, E0])
        hi, lo = sb("hi", [NT * GRP, 2]), sb("lo", [NT * GRP, 2])
        top, second, t0, gsum = (sb(n, [NT * GRP]) for n in ("top", "second", "t0", "gsum"))
        later = sb("later", [GRP, GRP])
        more, same = sb("more", [NT, GRP, GRP]), sb("same", [NT, GRP, GRP])
        rank, masked = sb("rank", [NT, GRP]), sb("masked", [NT, E0])
        top8, idx8, idxf = sb("top8", [NT, 8]), sb("idx8", [NT, 8], U32), sb("idxf", [NT, 8])
        hot, den = sb("hot", [2, NT, E0]), sb("den", [NT])
        ld, step, root_in, root_out, xn_ready, xt_ps, xt_ready, logit_ps, score_ready = (sem(n) for n in (
            "ld", "step", "root_in", "root_out", "xn_ready", "xt_ps", "xt_ready", "logit_ps", "score_ready"))
        block = ctx.enter_context(nc.Block())

        @block.sync
        def _(sp):
            sp.dma_start(rw[:], io["L0_router_T"].rearrange("(c p) n -> p c n", p=P)).then_inc(ld, 16)
            sp.dma_start(bias[:], io["L0_ffn_e_bias"].partition_broadcast(P)).then_inc(ld, 16)
            sp.dma_start(iota[:], io["iota"][0:E0].partition_broadcast(P)).then_inc(ld, 16)
            sp.dma_start(later[:], io["later"].partition_broadcast(P)).then_inc(ld, 16)
            for q in range(PAIRS):
                load_weights(sp, m, io, 2 * q, 2, q)

        @block.tensor
        def _(pe):
            pe.wait_ge(ld, 64)
            transpose_and_project(nc, pe, m, xn_ready, xt_ps, xt_ready, rw, E0, logit_ps)

        @block.scalar
        def _(act):
            layernorm_scalar(nc, act, m, root_in, root_out)
            for i in range(NT):
                act.wait_ge(xt_ps, i + 1)
                transposed_copy(nc, m, i, i % 2, m.xT).then_inc(xt_ready, 1)
            act.wait_ge(logit_ps, 1)
            nc.scalar.activation(score[:].rearrange("p i e -> p (i e)"), m.ps[:, 2, 0:NT * E0], ACT.Sigmoid
                                 ).then_inc(score_ready, 1)

        @block.vector
        def _(dve):
            chain = Chain(dve, step)
            link, v = chain.link, nc.vector
            layernorm_vector(nc, dve, chain, m, 1e-5, root_in, root_out, xn_ready)
            v.memset(m.comb[:, :, E0:X0], 1.0)
            dve.wait_ge(ld, 64)
            dve.wait_ge(score_ready, 1)
            link(v.tensor_tensor(biased[:], score[:], bcast(bias[:], 1, NT), ALU.add))
            pairs = biased[:].rearrange("p i (g a b) -> p (i g) a b", g=GRP, b=2)
            v.tensor_tensor(hi[:], pairs[:, :, :, 0], pairs[:, :, :, 1], ALU.max)
            link(v.tensor_tensor(lo[:], pairs[:, :, :, 0], pairs[:, :, :, 1], ALU.min))
            v.tensor_tensor(top[:], hi[:, :, 0], hi[:, :, 1], ALU.max)
            v.tensor_tensor(second[:], hi[:, :, 0], hi[:, :, 1], ALU.min)
            link(v.tensor_tensor(t0[:], lo[:, :, 0], lo[:, :, 1], ALU.max))
            link(v.tensor_tensor(gsum[:], second[:], t0[:], ALU.max))
            link(v.tensor_tensor(second[:], gsum[:], top[:], ALU.add))
            gs = second[:].rearrange("p (i g) -> p i g", g=GRP)
            mine, other = bcast(gs, 3, GRP), bcast(gs, 2, GRP)
            v.tensor_tensor(more[:], other, mine, ALU.is_gt)
            link(v.tensor_tensor(same[:], other, mine, ALU.is_equal))
            same_earlier = hot[:, 0, :, :].rearrange("p i (g h) -> p i g h", g=GRP)
            link(v.tensor_tensor(same_earlier, same[:], bcast(later[:], 1, NT), ALU.mult))
            link(v.tensor_tensor(same[:], more[:], same_earlier, ALU.add))
            link(v.tensor_reduce(rank[:], same[:], AX_X, ALU.add))
            link(v.tensor_scalar(gsum[:].rearrange("p (i g) -> p i g", g=GRP), rank[:], 1.5, None, ALU.is_lt))
            link(v.tensor_tensor(hot[:, 0, :, :].rearrange("p i (g h) -> p (i g) h", g=GRP),
                                 biased[:].rearrange("p i (g h) -> p (i g) h", g=GRP),
                                 bcast(gsum[:], 2, GSZ), ALU.mult))
            link(v.tensor_scalar(masked[:], hot[:, 0, :, :], 0.0, None, ALU.add))
            top_indices(nc, link, masked, top8, idx8, idxf)
            for j in range(2):
                ins = v.tensor_tensor(hot[:, j, :, :], bcast(iota[:], 1, NT), bcast(idxf[:, :, j], 2, E0), ALU.is_equal)
            link(ins)
            link(v.tensor_tensor(masked[:], hot[:, 0, :, :], hot[:, 1, :, :], ALU.add))
            link(v.tensor_tensor(biased[:], masked[:], score[:], ALU.mult))
            link(v.tensor_reduce(den[:], biased[:], AX_X, ALU.add))
            link(v.tensor_scalar(m.rstd[:, 0, :], den[:], 1e-20, None, ALU.add))
            link(v.reciprocal(den[:], m.rstd[:, 0, :]))
            v.tensor_tensor(m.comb[:, :, 0:E0], biased[:], bcast(den[:], 2, E0), ALU.mult)


def transpose_and_project(nc, pe, m, xn_ready, xt_ps, xt_ready, w, n, logit_ps):
    for i in range(NT):
        pe.wait_ge(xn_ready, i + 1)
        if i >= 2:
            pe.wait_ge(xt_ready, i - 1)
        transpose_tile(nc, m, i % 2, m.xn[:, i, :]).then_inc(xt_ps, 1)
    pe.wait_ge(xt_ready, NT)
    for i in range(NT):
        ins = matmul_tile(nc, m.ps[:, 2, i * n:(i + 1) * n], m.xT, i, w)
    ins.then_inc(logit_ps, 1)


def top_indices(nc, link, values, top8, idx8, idxf):
    for i in range(NT):
        ins = nc.vector.max(top8[:, i, :], values[:, i, :])
    link(ins)
    for i in range(NT):
        ins = nc.vector.max_index(idx8[:, i, :], top8[:, i, :], values[:, i, :])
    link(ins)
    link(nc.vector.tensor_copy(idxf[:], idx8[:]))


def experts_l0(nc, m, io):
    with ExitStack() as ctx:
        def sem(n):
            return m.sem("f0_" + n, ctx)
        HT = T // 2
        up = m.sb("f0_up", [P, 2, KD, I0], ctx=ctx)
        down = m.sb("f0_down", [P, 2, D], ctx=ctx)
        relu = m.sb("f0_relu", [P, 2, HT], ctx=ctx)
        hid = m.sb("f0_hid", [P, 2, HT], ctx=ctx)
        loaded = [sem("loaded0"), sem("loaded1")]
        up_ps, relu_done, hid_done, down_ps, added = (sem(n) for n in (
            "up_ps", "relu_done", "hid_done", "down_ps", "added"))
        block = ctx.enter_context(nc.Block())
        NG = X0 // 2

        @block.sync
        def _(sp):
            def body(g, first, last):
                for j in range(2):
                    e = 2 * g + j
                    if not first:
                        sp.wait_ge(down_ps, 8 * (e - 1))
                    sp.dma_start(up[:, j, :, :],
                                 io["L0_up"][bass.ds(e, 1), :, :].rearrange("a (c p) n -> p (a c) n", p=P)
                                 ).then_inc(loaded[j], 16)
                    sp.dma_start(down[:, j, :], io["L0_down"][bass.ds(e, 1), :, :].rearrange("a p n -> p (a n)")
                                 ).then_inc(loaded[j], 16)
            rounds(sp, NG, body)

        @block.tensor
        def _(pe):
            def hidden(n, slot, half, loads, first):
                if half == 0:
                    pe.wait_ge(loaded[slot], 32 * loads)
                if not first:
                    pe.wait_ge(relu_done, n - 1)
                for c in range(KD):
                    ins = nc.tensor.matmul(m.ps[:, half, :], up[:, slot, c, :], m.xT[:, c, half * HT:(half + 1) * HT],
                                           start=(c == 0), stop=(c == KD - 1))
                ins.then_inc(up_ps, 1)

            def outputs(n, slot, half, first):
                pe.wait_ge(hid_done, n + 1)
                for t in range(4):
                    if not first:
                        pe.wait_ge(added, 4 * n + t - 3)
                    nc.tensor.matmul(m.ps[:, 2 + t, 0:D], hid[:, half, t * P:(t + 1) * P], down[:, slot, :],
                                     start=True, stop=True).then_inc(down_ps, 1)

            hidden(0, 0, 0, 1, True)

            def body(g, first, last):
                for k in range(4):
                    n = 4 * g + k
                    if not (last and k == 3):
                        hidden(n + 1, ((k + 1) // 2) % 2, (k + 1) % 2, g + 1 + (k == 3), first and k == 0)
                    outputs(n, k // 2, k % 2, first and k == 0)
            rounds(pe, NG, body)

        @block.scalar
        def _(act):
            def body(g, first, last):
                for k in range(4):
                    n = 4 * g + k
                    act.wait_ge(up_ps, n + 1)
                    if not (first and k < 2):
                        act.wait_ge(hid_done, n - 1)
                    nc.scalar.activation(relu[:, k % 2, :], m.ps[:, k % 2, :], ACT.Relu).then_inc(relu_done, 1)
            rounds(act, NG, body)

        @block.gpsimd
        def _(pool):
            def body(g, first, last):
                for k in range(4):
                    n = 4 * g + k
                    pool.wait_ge(relu_done, n + 1)
                    if not (first and k < 2):
                        pool.wait_ge(down_ps, 4 * (n - 1))
                    nc.gpsimd.tensor_tensor(hid[:, k % 2, :], relu[:, k % 2, :], relu[:, k % 2, :], ALU.mult
                                            ).then_inc(hid_done, 1)
            rounds(pool, NG, body)

        @block.vector
        def _(dve):
            def body(g, first, last):
                for k in range(4):
                    for t in range(4):
                        i = 4 * (k % 2) + t
                        dve.wait_ge(down_ps, 16 * g + 4 * k + t + 1)
                        nc.vector.scalar_tensor_tensor(
                            m.xs[:, i, :], m.ps[:, 2 + t, 0:D], m.comb[:, i, bass.ds(2 * g + k // 2, 1)], m.xs[:, i, :],
                            ALU.mult, ALU.add).then_inc(added, 1)
            rounds(dve, NG, body)


def prep_l1(nc, m, io):
    lay, H, hd = L1, L1.heads, L1.hd
    with ExitStack() as ctx:
        def sem(n):
            return m.sem("p1_" + n, ctx)

        def sb(n, shape, parts=P):
            return m.sb("p1_" + n, [parts] + shape, F32, ctx)
        wq, wmain, wdca = sb("wq", [KD, D]), sb("wmain", [2 * D]), sb("wdca", [2 * D])
        bq, bmain, bdca = sb("bq", [D], 1), sb("bmain", [2 * D], 1), sb("bdca", [2 * D], 1)
        tmask = sb("tmask", [2, S], 1)
        pmask = sb("pmask", [QT, 2])
        ctxT_dca = sb("ctxT_dca", [B, P])
        nw, nb = sb("nw", [3, hd]), sb("nb", [3, hd])
        hmean, hvar = sb("hmean", [2, NT, H]), sb("hvar", [2, NT, H])
        hwork = sb("hwork", [4, 2 * NT * H])
        sq = sb("sq", [2, D])
        scaled = sb("scaled", [2, 2, D])
        ld, ld_norm, step, root_in, root_out, xn_ready, xt_ps, xt_ready = (sem(n) for n in (
            "ld", "ld_norm", "step", "root_in", "root_out", "xn_ready", "xt_ps", "xt_ready"))
        ctx_ready, v_set, k_ps, v_copied, q_ps, cent, squared, hroot_in, hroot_out, scaled_done, tm_done = (
            sem(n) for n in ("ctx_ready", "v_set", "k_ps", "v_copied", "q_ps", "cent", "squared", "hroot_in",
                             "hroot_out", "scaled_done", "tm_done"))
        pool_step, squares_summed = sem("pool_step"), sem("squares_summed")
        split_ps, hi_ready, rest_ready, mid_ready, lo_ready = (sem(n) for n in (
            "split_ps", "hi_ready", "rest_ready", "mid_ready", "lo_ready"))
        part_dma = [sem("part_dma0"), sem("part_dma1")]
        ps = m.ps
        block = ctx.enter_context(nc.Block())

        @block.sync
        def _(sp):
            loads = [(wq[:], io["L1_xattn_Wq"].rearrange("(c p) n -> p c n", p=P)),
                     (wmain[:], io["L1_wmain"]), (wdca[:], io["L1_xattn_Wkv_dca"]),
                     (bq[:], io["L1_xattn_bq"].rearrange("(a n) -> a n", a=1)),
                     (bmain[:], io["L1_bmain"]), (bdca[:], io["L1_xattn_bkv_dca"].rearrange("(a n) -> a n", a=1)),
                     (tmask[:], io["tmask"]), (pmask[:], io["pmask"])]
            for dst, src in loads:
                sp.dma_start(dst, src).then_inc(ld, 16)
            for dst, which in ((nw, "w"), (nb, "b")):
                sp.dma_start(dst[:, 0, :], io["L1_xattn_qn_" + which].partition_broadcast(P)).then_inc(ld_norm, 16)
                for j in (1, 2):
                    sp.dma_start(dst[0:P - DCA * (j - 1), j, :],
                                 io["L1_xattn_kn_" + which].partition_broadcast(P - DCA * (j - 1))).then_inc(ld_norm, 16)
                sp.dma_start(dst[P - DCA:P, 2, :],
                             io["L1_xattn_kn_dca_" + which].partition_broadcast(DCA)).then_inc(ld_norm, 16)
            for s in range(len(SPLITS)):
                sp.wait_ge(lo_ready, s + 1)
                sp.wait_ge(mid_ready, s + 1)
                split_writes(sp, m, s, part_dma)
            for b in range(2):
                sp.wait_ge(part_dma[b], 16 * WRITES * len(SPLITS) // 2)

        @block.tensor
        def _(pe):
            pe.wait_ge(ld, 8 * 16)
            pe.wait_ge(ctx_ready, 1)
            for i in range(NT):
                odd = i % 2
                if i >= 2:
                    pe.wait_ge(cent, i - 1)
                if i >= 2:
                    pe.wait_ge(v_copied, i - 1)
                main = m.ctxT[:, i * P:(i + 1) * P]
                dca = ctxT_dca[:, i // 2, :]
                mmask, dmask = (tmask[:, a, odd * P:(odd + 1) * P] for a in range(2))
                k_out, v_out, vd_out = ps[:, odd, 0:D], ps[:, 2 + odd, 0:D], ps[:, 2 + odd, D:2 * D]
                for out, col in ((k_out, 0), (v_out, D)):
                    both = odd and col == 0
                    nc.tensor.matmul(out, main, wmain[:, col:col + D], start=True, stop=False)
                    ins = nc.tensor.matmul(out, mmask, bmain[:, col:col + D], start=False, stop=not both)
                    if both:
                        nc.tensor.matmul(out, dca, wdca[:, 0:D], start=False, stop=False)
                        ins = nc.tensor.matmul(out, dmask, bdca[:, 0:D], start=False, stop=True)
                if odd:
                    nc.tensor.matmul(vd_out, dca, wdca[:, D:2 * D], start=True, stop=False)
                    ins = nc.tensor.matmul(vd_out, dmask, bdca[:, D:2 * D], start=False, stop=True)
                ins.then_inc(k_ps, 1)
            pe.wait_ge(v_copied, NT)
            for i in range(NT + 1):
                if i < NT:
                    pe.wait_ge(xn_ready, i + 1)
                    if i >= 2:
                        pe.wait_ge(xt_ready, i - 1)
                    transpose_tile(nc, m, 2 + i % 2, m.xn[:, i, :]).then_inc(xt_ps, 1)
                if i >= 1:
                    t = i - 1
                    pe.wait_ge(xt_ready, t + 1)
                    if t >= 2:
                        pe.wait_ge(cent, NT + t - 1)
                    matmul_tile(nc, ps[:, 4 + t % 2, 0:D], m.xT, t, wq, bq[:], m.ones_row[:]).then_inc(q_ps, 1)
            for s in range(len(SPLITS)):
                split_tensor(nc, pe, m, s, tm_done, rest_ready).then_inc(split_ps, 1)

        def token_major(n):
            return (m.k_tm if n < NT else m.q_tm)[:, n % NT, :]

        @block.vector
        def _(dve):
            chain = Chain(dve, step)
            link, v = chain.link, nc.vector
            def sum_squares(n):
                dve.wait_ge(squared, n + 1)
                nc.vector.tensor_reduce(hvar[:, n // NT, n % NT, :], sq[:, n % 2, :].rearrange("p (h e) -> p h e", h=H),
                                        AX_X, ALU.add).then_inc(squares_summed, 1)

            layernorm_vector(nc, dve, chain, m, 1e-5, root_in, root_out, xn_ready)
            v.memset(ctxT_dca[:], 0.0)
            link(v.memset(m.v1[:], 0.0))
            dve.wait_ge(ld, 8 * 16)
            tail = m.ctxT[:].rearrange("p (b s) -> p b s", b=B)[:, :, MAIN:S]
            link(v.tensor_copy(ctxT_dca[:, :, P - DCA:P], tail))
            v.memset(tail, 0.0).then_inc(ctx_ready, 1)
            for i in range(NT):
                for a in range(2):
                    col = (a + 1) * (hd + 1) - 1
                    ins = v.tensor_copy(m.v1[:, i, :, col], pmask[:, i % 2, a:a + 1].broadcast_to([P, H]))
            ins.then_inc(v_set, 1)
            for n in range(2 * NT):
                i = n % NT
                dve.wait_ge(k_ps if n < NT else q_ps, i + 1)
                src = ps[:, (0 if n < NT else 4) + i % 2, 0:D].rearrange("p (h e) -> p h e", h=H)
                side = n // NT
                link(v.tensor_reduce(hvar[:, side, i, :], src, AX_X, ALU.add))
                link(v.tensor_scalar(hmean[:, side, i, :], hvar[:, side, i, :], 1.0 / hd, None, ALU.mult))
                v.tensor_tensor(token_major(n).rearrange("p (h e) -> p h e", h=H), src,
                                bcast(hmean[:, side, i, :], 2, hd), ALU.subtract).then_inc(cent, 1)
                if n >= 1:
                    sum_squares(n - 1)
            sum_squares(2 * NT - 1)
            dve.wait_ge(squares_summed, 2 * NT)
            flat = hvar[:].rearrange("p a i h -> p (a i h)")
            link(v.tensor_scalar(hwork[:, 0, :], flat, 1.0 / hd, 1e-6, ALU.mult, ALU.add))
            rsqrt_vector(nc, dve, chain, hwork[:, 0, :], None, [hwork[:, j, :] for j in range(4)], hroot_in, hroot_out)
            for n in range(2 * NT):
                if n >= 2:
                    dve.wait_ge(tm_done, n - 1)
                r = hwork[:, 2, n * H:(n + 1) * H]
                v.tensor_tensor(scaled[:, n % 2, 0, :].rearrange("p (h e) -> p h e", h=H),
                                token_major(n).rearrange("p (h e) -> p h e", h=H), bcast(r, 2, hd),
                                ALU.mult).then_inc(scaled_done, 1)
            for s in range(len(SPLITS)):
                dve.wait_ge(hi_ready, s + 1)
                if s >= 2:
                    dve.wait_ge(lo_ready, s - 1)
                v.tensor_tensor(m.rest[:, s % 2, :], ps[:, 6 + s % 2, :], m.part[:, s % 2, 0, :],
                                ALU.subtract).then_inc(rest_ready, 1)

        @block.scalar
        def _(act):
            layernorm_scalar(nc, act, m, root_in, root_out)
            act.wait_ge(v_set, 1)

            def square(n):
                act.wait_ge(cent, n + 1)
                if n >= 2:
                    act.wait_ge(squares_summed, n - 1)
                nc.scalar.activation(sq[:, n % 2, :], token_major(n), ACT.Square).then_inc(squared, 1)

            for i in range(NT):
                act.wait_ge(k_ps, i + 1)
                for a in range(1 + i % 2):
                    ins = nc.scalar.copy(m.v1[:, i, :, a * (hd + 1):a * (hd + 1) + hd],
                                         ps[:, 2 + i % 2, a * D:(a + 1) * D].rearrange("p (h e) -> p h e", h=H))
                ins.then_inc(v_copied, 1)
                square(i)
            for i in range(NT + 1):
                if i < NT:
                    act.wait_ge(xt_ps, i + 1)
                    transposed_copy(nc, m, i, 2 + i % 2, m.xT).then_inc(xt_ready, 1)
                if i >= 1:
                    square(NT + i - 1)
            act.wait_ge(hroot_in, 1)
            nc.scalar.activation(hwork[:, 1, :], hwork[:, 3, :], ACT.Sqrt).then_inc(hroot_out, 1)
            split_scalar(nc, act, m, split_ps, part_dma, hi_ready, rest_ready, mid_ready)

        @block.gpsimd
        def _(pool):
            pool.wait_ge(ld_norm, 8 * 16)
            for n in range(2 * NT):
                pool.wait_ge(scaled_done, n + 1)
                row = 0 if n >= NT else 1 + n % 2

                def heads(ap):
                    return ap.rearrange("p (h e) -> p h e", h=H)
                nc.gpsimd.tensor_tensor(heads(scaled[:, n % 2, 1, :]), heads(scaled[:, n % 2, 0, :]),
                                        bcast(nw[:, row, :], 1, H), ALU.mult).then_inc(pool_step, 1)
                pool.wait_ge(pool_step, n + 1)
                nc.gpsimd.tensor_tensor(heads(token_major(n)), heads(scaled[:, n % 2, 1, :]),
                                        bcast(nb[:, row, :], 1, H), ALU.add).then_inc(tm_done, 1)
            split_gpsimd(nc, pool, m, mid_ready, rest_ready, part_dma, lo_ready)


E1, I1, TOP1 = 60, 176, 4
SH1 = 704 // I1
HC = I1 // 2
ROUND = 12
OVER = -(-(T * TOP1 // P) // ROUND) * ROUND
BLOCKS = E1 + OVER
RING = ROUND
PAIRS = ROUND // 2
ZEROED = (BLOCKS + OVER) // ROUND


def route_l1(nc, m, io):
    with ExitStack() as ctx:
        def sem(n):
            return m.sem("r1_" + n, ctx)

        def sb(n, shape, dt=F32):
            return m.sb("r1_" + n, [P] + shape, dt, ctx)
        NC = E1 + 1
        gw, iota = sb("gw", [KD, NC]), sb("iota", [P])
        logit, prob = sb("logit", [NT, NC]), sb("prob", [NT, E1])
        top, total = sb("top", [NT]), sb("total", [NT])
        top8, idx8, idxf = m.topw, sb("idx8", [NT, 8], U32), sb("idxf", [NT, 8])
        hot = sb("hot", [TOP1, NT, E1])
        mask_bf = sb("mask_bf", [NT, E1], BF16)
        upper, upper_bf, ones_bf = sb("upper", [P]), sb("upper_bf", [P], BF16), sb("ones_bf", [P], BF16)
        count, marks, extra, incl = sb("count", [E1]), sb("marks", [NT]), sb("extra", [E1]), sb("incl", [E1])
        shift, slot_of, picked = sb("shift", [E1]), sb("slot_of", [NT, E1]), sb("picked", [TOP1, NT])
        over_cmp, over_f, ones_e = sb("over_cmp", [OVER, E1]), sb("over_f", [1 + OVER]), sb("ones_e", [E1])
        mask_ready, rank_ps = sem("mask_ready"), sem("rank_ps")
        ld, step, root_in, root_out, xn_ready, xt_ps, xt_ready, logit_ps, logit_ready, exp_in, exp_out = (
            sem(n) for n in ("ld", "step", "root_in", "root_out", "xn_ready", "xt_ps", "xt_ready", "logit_ps",
                             "logit_ready", "exp_in", "exp_out"))
        block = ctx.enter_context(nc.Block())

        @block.sync
        def _(sp):
            sp.dma_start(gw[:], io["L1_gates_T"].rearrange("(c p) n -> p c n", p=P)).then_inc(ld, 16)
            sp.dma_start(iota[:], io["iota"].partition_broadcast(P)).then_inc(ld, 16)
            sp.dma_start(upper[:], io["upper"]).then_inc(ld, 16)

        @block.tensor
        def _(pe):
            pe.wait_ge(ld, 48)
            transpose_and_project(nc, pe, m, xn_ready, xt_ps, xt_ready, gw, NC, logit_ps)
            pe.wait_ge(mask_ready, 1)
            for i in range(NT):
                for j in range(i + 1):
                    nc.tensor.matmul(m.ps[:, 3, i * E1:(i + 1) * E1], (upper_bf if j == i else ones_bf)[:],
                                     mask_bf[:, j, :], start=(j == 0), stop=(j == i))
            for j in range(NT):
                ins = nc.tensor.matmul(m.ps[:, 4, 0:E1], ones_bf[:], mask_bf[:, j, :],
                                       start=(j == 0), stop=(j == NT - 1))
            ins.then_inc(rank_ps, 1)

        @block.scalar
        def _(act):
            layernorm_scalar(nc, act, m, root_in, root_out)
            for i in range(NT):
                act.wait_ge(xt_ps, i + 1)
                transposed_copy(nc, m, i, i % 2, m.xT).then_inc(xt_ready, 1)
            act.wait_ge(logit_ready, 1)
            nc.scalar.activation(m.gate[:], logit[:, :, E1], ACT.Sigmoid)
            act.wait_ge(exp_in, 1)
            nc.scalar.activation(hot[:, 1, :, :], hot[:, 0, :, :], ACT.Exp).then_inc(exp_out, 1)

        @block.vector
        def _(dve):
            chain = Chain(dve, step)
            link, v = chain.link, nc.vector
            layernorm_vector(nc, dve, chain, m, 1e-5, root_in, root_out, xn_ready)
            dve.wait_ge(ld, 48)
            dve.wait_ge(logit_ps, 1)
            v.tensor_copy(logit[:].rearrange("p i e -> p (i e)"), m.ps[:, 2, 0:NT * NC]).then_inc(logit_ready, 1)
            dve.wait_ge(logit_ready, 1)
            lg = logit[:, :, 0:E1]
            link(v.tensor_reduce(top[:], lg, AX_X, ALU.max))
            v.tensor_tensor(hot[:, 0, :, :], lg, bcast(top[:], 2, E1), ALU.subtract).then_inc(exp_in, 1)
            dve.wait_ge(exp_out, 1)
            link(v.tensor_reduce(total[:], hot[:, 1, :, :], AX_X, ALU.add))
            link(v.reciprocal(top[:], total[:]))
            link(v.tensor_tensor(prob[:], hot[:, 1, :, :], bcast(top[:], 2, E1), ALU.mult))
            top_indices(nc, link, prob, top8, idx8, idxf)
            for j in range(TOP1):
                ins = v.tensor_tensor(hot[:, j, :, :], bcast(iota[:, 0:E1], 1, NT), bcast(idxf[:, :, j], 2, E1), ALU.is_equal)
            link(ins)
            v.tensor_copy(upper_bf[:], upper[:])
            v.memset(ones_bf[:], 1.0)
            v.memset(ones_e[:], 1.0)
            v.tensor_scalar(marks[:], iota[:, 1:1 + NT], float(P), None, ALU.mult)
            v.tensor_tensor(slot_of[:], hot[:, 0, :, :], hot[:, 1, :, :], ALU.add)
            link(v.tensor_tensor(prob[:], hot[:, 2, :, :], hot[:, 3, :, :], ALU.add))
            v.tensor_tensor(mask_bf[:], slot_of[:], prob[:], ALU.add).then_inc(mask_ready, 1)
            dve.wait_ge(rank_ps, 1)
            link(v.tensor_copy(count[:], m.ps[:, 4, 0:E1]))
            many = over_cmp[:].rearrange("p o e -> p (o e)")[:, 0:E1 * (NT - 1)].rearrange("p (e k) -> p e k", e=E1)
            link(v.tensor_tensor(many, bcast(count[:], 2, NT - 1), bcast(marks[:, 0:NT - 1], 1, E1), ALU.is_gt))
            link(v.tensor_reduce(extra[:], many, AX_X, ALU.add))
            link(v.tensor_tensor_scan(incl[:], ones_e[:], extra[:], 0.0, ALU.mult, ALU.add))
            link(v.tensor_tensor(count[:], incl[:], extra[:], ALU.subtract))
            link(v.tensor_tensor(extra[:], count[:], iota[:, 0:E1], ALU.subtract))
            link(v.tensor_scalar(shift[:], extra[:], float(E1 - 1), float(P), ALU.add, ALU.mult))
            rank = m.ps[:, 3, 0:NT * E1].rearrange("p (i e) -> p i e", i=NT)
            link(v.tensor_scalar(prob[:], rank, float(P), None, ALU.is_ge))
            link(v.tensor_tensor(slot_of[:], prob[:], bcast(shift[:], 1, NT), ALU.mult))
            link(v.tensor_tensor(prob[:], slot_of[:], rank, ALU.add))
            link(v.scalar_tensor_tensor(slot_of[:], bcast(iota[:, 0:E1], 1, NT), float(P), prob[:], ALU.mult, ALU.add))
            link(v.tensor_tensor(hot[:], hot[:], bcast(slot_of[:], 1, TOP1), ALU.mult))
            link(v.tensor_reduce(picked[:], hot[:], AX_X, ALU.add))
            link(v.tensor_copy(m.slot[:], picked[:]))
            link(v.tensor_tensor(over_cmp[:], bcast(incl[:], 1, OVER), bcast(iota[:, 0:OVER], 2, E1), ALU.is_le))
            link(v.tensor_reduce(over_f[:, 1:1 + OVER], over_cmp[:], AX_X, ALU.add))
            v.tensor_copy(over_f[:, 0:1], incl[:, E1 - 1:E1])
            link(v.tensor_scalar(over_cmp[:, 0, 0:OVER], over_f[:, 1:1 + OVER], float(E1 - 1), None, ALU.min))
            v.tensor_copy(m.over[:, 0:1], over_f[0:1, 0:1])
            v.tensor_copy(m.over[:, 1:1 + OVER], over_cmp[0:1, 0, 0:OVER])


def load_weights(eng, m, io, e, n, pair):
    eng.dma_start(m.ew13[:, 2 * pair:2 * pair + n, :, :],
                  io["L1_w13"][bass.ds(e, n), :, :].rearrange("a (c p) n -> p a c n", p=P)
                  ).then_inc(m.ew_loaded[pair], 16)
    eng.dma_start(m.ew2[:, 2 * pair:2 * pair + n, :, :],
                  io["L1_w2"][bass.ds(e, n), :, :].rearrange("a (c p) n -> p a c n", p=HC)
                  ).then_inc(m.ew_loaded[pair], 16)


def dispatch_l1(nc, pool, m, sent):
    pool.wait_ge(m.zeroed, 16 * ZEROED)
    for i in range(NT):
        for j in range(TOP1):
            nc.gpsimd.indirect_dma_start(m.x_slots, bass.IndirectOffsetOnAxis(m.slot[:, j, i:i + 1], 0),
                                         m.xn[:, i, :], None).then_inc(sent, 16)
    pool.wait_ge(sent, 16 * NT * TOP1)


FETCHES = 8
PICKS = [(i, j) for i in range(NT) for j in range(TOP1)]


def fetch_outputs(nc, pool, m, yg, fetched, combined):
    for n, (i, j) in enumerate(PICKS):
        if n >= FETCHES:
            pool.wait_ge(combined, n - FETCHES + 1)
        nc.gpsimd.indirect_dma_start(yg[:, n % FETCHES, :], None, m.y_slots,
                                     bass.IndirectOffsetOnAxis(m.slot[:, j, i:i + 1], 0)
                                     ).then_inc(fetched[n % FETCHES], 16)


def shared_l1(nc, m, io, half):
    with ExitStack() as ctx:
        def sem(n):
            return m.sem(f"f{half + 3}_{n}", ctx)
        name = f"f{half + 3}_"
        w13 = m.sb(name + "w13", [P, 2, KD, 2 * I1], ctx=ctx)
        w2 = m.sb(name + "w2", [HC, 2, 2, D], ctx=ctx)
        act_g = m.sb(name + "act_g", [P, 2, I1], ctx=ctx)
        hid = m.sb(name + "hid", [P, 2, I1], ctx=ctx)
        hidT = m.sb(name + "hidT", [HC, 2, 2 * P], ctx=ctx)
        loaded = [sem("loaded0"), sem("loaded1")]
        gu_ps, silu_done, hid_done, ht_ps, ht_done, y_ps, added = (sem(n) for n in (
            "gu_ps", "silu_done", "hid_done", "ht_ps", "ht_done", "y_ps", "added"))
        if half == 0:
            sent = sem("sent")
        else:
            yg = m.sb("yg", [P, FETCHES, D], ctx=ctx)
            fetched = [sem(f"fetched{b}") for b in range(FETCHES)]
            combined = sem("combined")
        STEPS = SH1 // 2 * NT
        ps = m.ps
        block = ctx.enter_context(nc.Block())

        @block.gpsimd
        def _(pool):
            if half == 0:
                dispatch_l1(nc, pool, m, sent)
            else:
                fetch_outputs(nc, pool, m, yg, fetched, combined)

        @block.sync
        def _(sp):
            for j in range(2):
                e = 2 * half + j
                sp.dma_start(w13[:, j, :, :], io["L1_shared_w13"][e].rearrange("(c p) n -> p c n", p=P)
                             ).then_inc(loaded[j], 16)
                sp.dma_start(w2[:, j, :, :], io["L1_shared_w2"][e].rearrange("(c p) n -> p c n", p=HC)
                             ).then_inc(loaded[j], 16)

        @block.tensor
        def _(pe):
            def gate_up(k):
                part, i = k // NT, k % NT
                if i == 0:
                    pe.wait_ge(loaded[part], 32)
                if k >= 2:
                    pe.wait_ge(hid_done, k - 1)
                for c in range(KD):
                    ins = nc.tensor.matmul(ps[:, k % 2, 0:2 * I1], m.xT[:, c, i * P:(i + 1) * P], w13[:, part, c, :],
                                           start=(c == 0), stop=(c == KD - 1))
                ins.then_inc(gu_ps, 1)

            def turn(k):
                pe.wait_ge(hid_done, k + 1)
                if k >= 2:
                    pe.wait_ge(ht_done, k - 1)
                for c in range(2):
                    ins = nc.tensor.transpose(ps[0:HC, 2 + k % 2, c * P:(c + 1) * P],
                                              hid[:, k % 2, c * HC:(c + 1) * HC], m.ident[:])
                ins.then_inc(ht_ps, 1)

            def outputs(k):
                pe.wait_ge(ht_done, k + 1)
                if k >= 2:
                    pe.wait_ge(added, k - 1)
                for c in range(2):
                    ins = nc.tensor.matmul(ps[:, 4 + k % 2, 0:D], hidT[:, k % 2, c * P:(c + 1) * P],
                                           w2[:, k // NT, c, :], start=(c == 0), stop=(c == 1))
                ins.then_inc(y_ps, 1)

            gate_up(0)
            gate_up(1)
            turn(0)
            for k in range(STEPS):
                if k + 2 < STEPS:
                    gate_up(k + 2)
                if k + 1 < STEPS:
                    turn(k + 1)
                outputs(k)

        @block.scalar
        def _(act):
            def silu(k):
                act.wait_ge(gu_ps, k + 1)
                if k >= 2:
                    act.wait_ge(hid_done, k - 1)
                nc.scalar.activation(act_g[:, k % 2, :], ps[:, k % 2, 0:I1], ACT.Silu).then_inc(silu_done, 1)

            silu(0)
            silu(1)
            for k in range(STEPS):
                act.wait_ge(ht_ps, k + 1)
                if k >= 2:
                    act.wait_ge(y_ps, k - 1)
                nc.scalar.copy(hidT[:, k % 2, :], ps[0:HC, 2 + k % 2, 0:2 * P]).then_inc(ht_done, 1)
                if k + 2 < STEPS:
                    silu(k + 2)

        @block.vector
        def _(dve):
            def multiply(k):
                dve.wait_ge(silu_done, k + 1)
                if k >= 2:
                    dve.wait_ge(ht_ps, k - 1)
                nc.vector.tensor_tensor(hid[:, k % 2, :], act_g[:, k % 2, :], ps[:, k % 2, I1:2 * I1], ALU.mult
                                        ).then_inc(hid_done, 1)

            def combine(n, steps):
                i, j = PICKS[n]
                dve.wait_ge(fetched[n % FETCHES], 16 * (n // FETCHES + 1))
                dve.wait_ge(added, steps)
                if n >= 1:
                    dve.wait_ge(combined, n)
                nc.vector.scalar_tensor_tensor(m.xs[:, i, :], yg[:, n % FETCHES, :], m.topw[:, i, j:j + 1],
                                               m.xs[:, i, :], ALU.mult, ALU.add).then_inc(combined, 1)

            per_step = len(PICKS) // STEPS
            multiply(0)
            multiply(1)
            for k in range(STEPS):
                if k + 2 < STEPS:
                    multiply(k + 2)
                if half == 1 and k >= 1:
                    for n in range(per_step * (k - 1), per_step * k):
                        combine(n, k)
                i = k % NT
                dve.wait_ge(y_ps, k + 1)
                if half == 1 and k >= 1:
                    dve.wait_ge(combined, per_step * k)
                nc.vector.scalar_tensor_tensor(m.xs[:, i, :], ps[:, 4 + k % 2, 0:D], m.gate[:, i:i + 1],
                                               m.xs[:, i, :], ALU.mult, ALU.add).then_inc(added, 1)
            if half == 1:
                for n in range(per_step * (STEPS - 1), len(PICKS)):
                    combine(n, STEPS)


def routed_l1(nc, m, io):
    with ExitStack() as ctx:
        def sem(n):
            return m.sem("f2_" + n, ctx)
        xg = m.sb("f2_xg", [P, 6, D], ctx=ctx)
        xgT = m.sb("f2_xgT", [P, 4, D], ctx=ctx)
        act_g = m.sb("f2_act_g", [P, 2, I1], ctx=ctx)
        hid = m.sb("f2_hid", [P, 2, I1], ctx=ctx)
        hidT = m.sb("f2_hidT", [HC, 2, 2 * P], ctx=ctx)
        yb = m.sb("f2_yb", [P, 4, D], ctx=ctx)
        x_loaded = [sem(f"x_loaded{j}") for j in range(3)]
        y_stored = [sem("y_stored0"), sem("y_stored1")]
        over_loaded = [sem(f"over_loaded{j}") for j in range(PAIRS)]
        xt_ps, xt_done, gu_ps, silu_done, hid_done, ht_ps, ht_done, y_ps, y_done = (sem(n) for n in (
            "xt_ps", "xt_done", "gu_ps", "silu_done", "hid_done", "ht_ps", "ht_done", "y_ps", "y_done"))
        block = ctx.enter_context(nc.Block())
        ps = m.ps
        FIXED, FURTHER = E1 // ROUND, OVER // ROUND

        def all_rounds(eng, prologue, body):
            prologue(0)
            rounds(eng, FIXED, body)
            blocks = eng.value_load(m.over[0:1, 0:1], min_val=0, max_val=OVER)
            for r in range(FURTHER):
                with eng.If(blocks > r * ROUND):
                    prologue(FIXED + r)
                    body(FIXED + r, False, True)

        @block.sync
        def _(sp):
            def load_x(g, h):
                rows = m.x_slots[bass.ds((ROUND * g + 2 * h) * P, 2 * P), :]
                sp.dma_start(xg[:, 2 * (h % 3):2 * (h % 3) + 2, :], rows.rearrange("(b p) d -> p b d", p=P)
                             ).then_inc(x_loaded[h % 3], 16)

            def store_y(g, h):
                sp.wait_ge(y_done, ROUND * g + 2 * h + 2)
                rows = m.y_slots[bass.ds((ROUND * g + 2 * h) * P, 2 * P), :]
                sp.dma_start(rows.rearrange("(b p) d -> p b d", p=P), yb[:, 2 * (h % 2):2 * (h % 2) + 2, :]
                             ).then_inc(y_stored[h % 2], 16)

            def prologue(g):
                load_x(g, 0)
                load_x(g, 1)
                if g >= FIXED:
                    for h in range(PAIRS):
                        sp.wait_ge(y_ps, ROUND * (g - 1) + 2 * h + 2)
                        for b in range(2):
                            o = ROUND * (g - FIXED) + 2 * h + b
                            e = sp.value_load(m.over[0:1, 1 + o:2 + o], min_val=0, max_val=E1 - 1)
                            for w, dram, pp in ((m.ew13, "L1_w13", P), (m.ew2, "L1_w2", HC)):
                                sp.dma_start(w[:, 2 * h + b, :, :],
                                             io[dram][bass.ds(e, 1), :, :].rearrange("a (c p) n -> p (a c) n", p=pp)
                                             ).then_inc(over_loaded[h], 16)

            def body(g, first, last):
                for h in range(PAIRS):
                    if not (first and h == 0):
                        sp.wait_ge(xt_ps, ROUND * g + 2 * h)
                    if h < PAIRS - 2:
                        load_x(g, h + 2)
                    elif not last:
                        load_x(g + 1, h + 2 - PAIRS)
                    if not (first and h == 0):
                        sp.wait_ge(y_ps, ROUND * g + 2 * h)
                    if not isinstance(g, int) or g < FIXED:
                        if h >= 1:
                            if not last:
                                load_weights(sp, m, io, ROUND * (g + 1) + 2 * (h - 1), 2, h - 1)
                        elif not first:
                            load_weights(sp, m, io, ROUND * g + 2 * (PAIRS - 1), 2, PAIRS - 1)
                    if h >= 1:
                        store_y(g, h - 1)
                    elif not first and not (isinstance(g, int) and g >= FIXED):
                        store_y(g - 1, PAIRS - 1)
                if last:
                    store_y(g, PAIRS - 1)
                    for a in range(2):
                        sp.wait_ge(y_stored[a], 16 * (PAIRS // 2) * (g + 1))
            all_rounds(sp, prologue, body)

        @block.tensor
        def _(pe):
            def turn_x(g, k, first):
                n, h = ROUND * g + k, (k // 2) % PAIRS
                gg, kk = (g, k) if k < ROUND else (g + 1, k - ROUND)
                if kk % 2 == 0:
                    pe.wait_ge(x_loaded[h % 3], 16 * ((PAIRS // 3) * gg + kk // 6 + 1))
                if not (first and k < 2):
                    pe.wait_ge(xt_done, n - 1)
                for c in range(KD):
                    ins = nc.tensor.transpose(ps[:, 6 + k % 2, c * P:(c + 1) * P], xg[:, k % 6, c * P:(c + 1) * P],
                                              m.ident[:])
                ins.then_inc(xt_ps, 1)

            def gate_up(g, k, first):
                n, slot = ROUND * g + k, k % ROUND
                gg, kk = (g, k) if k < ROUND else (g + 1, k - ROUND)
                if kk % 2 == 0:
                    if isinstance(gg, int) and gg >= FIXED:
                        pe.wait_ge(over_loaded[slot // 2], 64 * (gg - FIXED + 1))
                    else:
                        pe.wait_ge(m.ew_loaded[slot // 2], 32 * (gg + 1))
                pe.wait_ge(xt_done, n + 1)
                if not (first and k < 2):
                    pe.wait_ge(hid_done, n - 1)
                for c in range(KD):
                    ins = nc.tensor.matmul(ps[:, k % 2, 0:2 * I1], xgT[:, k % 4, c * P:(c + 1) * P],
                                           m.ew13[:, slot, c, :], start=(c == 0), stop=(c == KD - 1))
                ins.then_inc(gu_ps, 1)

            def turn_hid(g, k, first):
                n = ROUND * g + k
                pe.wait_ge(hid_done, n + 1)
                if not (first and k < 2):
                    pe.wait_ge(ht_done, n - 1)
                for c in range(2):
                    ins = nc.tensor.transpose(ps[0:HC, 2 + k % 2, c * P:(c + 1) * P],
                                              hid[:, k % 2, c * HC:(c + 1) * HC], m.ident[:])
                ins.then_inc(ht_ps, 1)

            def outputs(g, k, first):
                n = ROUND * g + k
                pe.wait_ge(ht_done, n + 1)
                if not (first and k < 2):
                    pe.wait_ge(y_done, n - 1)
                for c in range(2):
                    ins = nc.tensor.matmul(ps[:, 4 + k % 2, 0:D], hidT[:, k % 2, c * P:(c + 1) * P],
                                           m.ew2[:, k, c, :], start=(c == 0), stop=(c == 1))
                ins.then_inc(y_ps, 1)

            def prologue(g):
                first = g == 0
                for k in range(3):
                    turn_x(g, k, first)
                gate_up(g, 0, first)
                gate_up(g, 1, first)
                turn_hid(g, 0, first)

            def body(g, first, last):
                for k in range(ROUND):
                    if not (last and k + 3 >= ROUND):
                        turn_x(g, k + 3, first)
                    if not (last and k + 2 >= ROUND):
                        gate_up(g, k + 2, first)
                    if not (last and k + 1 >= ROUND):
                        turn_hid(g, k + 1, first)
                    outputs(g, k, first)
            all_rounds(pe, prologue, body)

        @block.scalar
        def _(act):
            def copy_x(g, k, first):
                n = ROUND * g + k
                act.wait_ge(xt_ps, n + 1)
                if not (first and k < 4):
                    act.wait_ge(gu_ps, n - 3)
                nc.scalar.copy(xgT[:, k % 4, :], ps[:, 6 + k % 2, 0:D]).then_inc(xt_done, 1)

            def silu(g, k, first):
                n = ROUND * g + k
                act.wait_ge(gu_ps, n + 1)
                if not (first and k < 2):
                    act.wait_ge(hid_done, n - 1)
                nc.scalar.activation(act_g[:, k % 2, :], ps[:, k % 2, 0:I1], ACT.Silu).then_inc(silu_done, 1)

            def prologue(g):
                first = g == 0
                for k in range(3):
                    copy_x(g, k, first)
                silu(g, 0, first)
                silu(g, 1, first)

            def body(g, first, last):
                for k in range(ROUND):
                    n = ROUND * g + k
                    act.wait_ge(ht_ps, n + 1)
                    if not (first and k < 2):
                        act.wait_ge(y_ps, n - 1)
                    nc.scalar.copy(hidT[:, k % 2, :], ps[0:HC, 2 + k % 2, 0:2 * P]).then_inc(ht_done, 1)
                    if not (last and k + 3 >= ROUND):
                        copy_x(g, k + 3, first)
                    if not (last and k + 2 >= ROUND):
                        silu(g, k + 2, first)
            all_rounds(act, prologue, body)

        @block.vector
        def _(dve):
            def multiply(g, k, first):
                n = ROUND * g + k
                dve.wait_ge(silu_done, n + 1)
                if not (first and k < 2):
                    dve.wait_ge(ht_ps, n - 1)
                nc.vector.tensor_tensor(hid[:, k % 2, :], act_g[:, k % 2, :], ps[:, k % 2, I1:2 * I1], ALU.mult
                                        ).then_inc(hid_done, 1)

            def prologue(g):
                multiply(g, 0, g == 0)
                multiply(g, 1, g == 0)

            def body(g, first, last):
                for k in range(ROUND):
                    if not (last and k + 2 >= ROUND):
                        multiply(g, k + 2, first)
                    dve.wait_ge(y_ps, ROUND * g + k + 1)
                    if k % 2 == 0 and not (first and k < 4):
                        dve.wait_ge(y_stored[(k // 2) % 2], 16 * ((PAIRS // 2) * g + k // 4))
                    nc.vector.tensor_copy(yb[:, k % 4, :], ps[:, 4 + k % 2, 0:D]).then_inc(y_done, 1)
            all_rounds(dve, prologue, body)


def store(nc, m, out):
    with ExitStack() as ctx:
        stored = m.sem("stored", ctx)
        block = ctx.enter_context(nc.Block())

        @block.sync
        def _(sp):
            sp.dma_start(out.rearrange("b (i p) d -> p (b i) d", p=P), m.xs[:]).then_inc(stored, 16)
            sp.wait_ge(stored, 16)


def build(nc, io, out):
    with ExitStack() as ctx:
        m = Mem(nc, ctx)
        m.xs = m.sb("xs", [P, NT, D])
        m.xn = m.sb("xn", [P, NT, D])
        m.xT = m.sb("xT", [P, KD, T])
        m.bn = m.sb("bn", [P, NT, 6])
        m.mv = m.sb("mv", [P, NT, 2])
        m.rstd = m.sb("rstd", [P, 4, NT])
        m.ident = m.sb("ident", [P, P])
        m.ident_bf = m.sb("ident_bf", [P, P], BF16)
        m.ones_row = m.sb("ones_row", [1, P])
        m.comb = m.sb("comb", [P, NT, X0])
        m.gate = m.sb("gate", [P, NT])
        m.ew13 = m.sb("ew13", [P, RING, KD, 2 * I1])
        m.ew2 = m.sb("ew2", [HC, RING, 2, D])
        m.ew_loaded = [m.sem(f"ew_loaded{j}") for j in range(RING // 2)]
        m.zeroed = m.sem("zeroed")
        m.slot = m.sb("slot", [P, TOP1, NT], U32)
        m.topw = m.sb("topw", [P, NT, 8])
        m.over = m.sb("over", [1, 1 + OVER], U32)
        m.x_slots = nc.dram_tensor("x_slots", [BLOCKS * P, D], F32, kind="Internal").ap()
        m.y_slots = nc.dram_tensor("y_slots", [BLOCKS * P, D], F32, kind="Internal").ap()
        m.ps = ctx.enter_context(nc.psum_tensor("ps", [P, 8, 512], F32))
        m.stacks = {n: nc.dram_tensor(n + "_stacks", [D, PARTS, T], BF16, kind="Internal").ap() for n in ("q", "k")}
        with ExitStack() as scope:
            m.ctxT = m.sb("ctxT_sb", [CD, T], ctx=scope)
            m.k_tm = m.sb("k_tm", [P, NT, D], ctx=scope)
            m.q_tm = m.sb("q_tm", [P, NT, D], ctx=scope)
            m.attn = m.sb("attn", [P, NT, D], ctx=scope)
            m.rest = m.sb("rest", [P, 2, SW], ctx=scope)
            m.part = m.sb("part", [P, 2, 3, SW], BF16, ctx=scope)
            with ExitStack() as layer:
                m.v0 = m.sb("v0", [P, NT, L0.heads, L0.hd + 1], ctx=layer)
                prep_l0(nc, m, io)
                m.old_sems, m.stage_sems = m.stage_sems, []
                attention(nc, m, L0, io)
                m.old_sems, m.stage_sems = m.stage_sems, []
            attention_output(nc, m, "o0_", io["L0_xattn_Wout"], io["L0_xattn_bout"])
            route_l0(nc, m, io)
            experts_l0(nc, m, io)
            with ExitStack() as layer:
                m.v1 = m.sb("v1", [P, NT, L1.heads, L1.vw], ctx=layer)
                prep_l1(nc, m, io)
                attention(nc, m, L1, io)
            attention_output(nc, m, "o1_", io["L1_xattn_Wo"], io["L1_xattn_bo"])
        route_l1(nc, m, io)
        shared_l1(nc, m, io, 0)
        routed_l1(nc, m, io)
        shared_l1(nc, m, io, 1)
        store(nc, m, out)


def host_layout(inputs):
    io = {n: np.ascontiguousarray(a) for n, a in inputs.items()}
    io["ctxT"] = np.ascontiguousarray(np.asarray(io.pop("ctx_1024")).reshape(T, CD).T)
    io["ident"] = np.eye(P, dtype=np.float32)
    io["ones_row"] = np.ones((1, P), np.float32)
    io["l0_ones"] = np.ones((2, G, S), np.float32)
    keys = np.arange(S) < MAIN
    io["l1_ones"] = np.broadcast_to(np.stack([keys, keys, ~keys, ~keys])[:, None, :], (4, G, S)).astype(np.float32)
    io["tmask"] = np.stack([keys, ~keys]).astype(np.float32)[None]
    io["pmask"] = np.ascontiguousarray(io["tmask"].reshape(2, QT, P).transpose(2, 1, 0))
    io["iota"] = np.arange(P, dtype=np.float32)
    io["later"] = np.tril(np.ones((GRP, GRP), np.float32), -1)
    io["L0_router_T"] = np.ascontiguousarray(io["L0_ffn_router_weight"].T)
    up, down = io.pop("L0_ffn_shared_up"), io.pop("L0_ffn_shared_down")
    io["L0_up"] = np.concatenate([io.pop("L0_ffn_w_up"), up.reshape(D, SH0, I0).transpose(1, 0, 2)])
    io["L0_down"] = np.concatenate([io.pop("L0_ffn_w_down"), down.reshape(SH0, I0, D)])
    wmain = np.concatenate([io.pop("L1_xattn_Wk"), io.pop("L1_xattn_Wv")], axis=1)
    bmain = np.concatenate([io.pop("L1_xattn_bk"), io.pop("L1_xattn_bv")])[None]
    io["L1_wmain"], io["L1_bmain"] = (
        np.ascontiguousarray(a.reshape(-1, L1.heads, 2, L1.hd).transpose(0, 2, 1, 3).reshape(-1, 2 * D))
        for a in (wmain, bmain))
    io["L1_gates_T"] = np.concatenate([io.pop("L1_ffn_gate_w"), io.pop("L1_ffn_shared_gate_w")]).T.copy()
    gate_up, down = io.pop("L1_ffn_se_gate_up_w"), io.pop("L1_ffn_se_down_w")
    w13 = gate_up.reshape(2, SH1, I1, D).transpose(1, 0, 2, 3).reshape(SH1, 2 * I1, D)
    io["L1_shared_w13"] = w13.transpose(0, 2, 1).copy()
    io["L1_shared_w2"] = down.T.reshape(SH1, I1, D).copy()
    io["L1_w13"] = io.pop("L1_ffn_w13").transpose(0, 2, 1).copy()
    io["L1_w2"] = io.pop("L1_ffn_w2").transpose(0, 2, 1).copy()
    io["upper"] = np.triu(np.ones((P, P), np.float32), 1)
    return io


def kernel(**inputs):
    import concourse.bacc as bacc
    from concourse.bass_utils import run_bass_kernel_spmd

    arrays = host_layout(inputs)
    nc = bacc.Bacc("TRN2", target_bir_lowering=False, num_devices=1)
    io = {n: nc.dram_tensor("in_" + n, a.shape, mybir.dt.from_np(a.dtype), kind="ExternalInput").ap()
          for n, a in arrays.items()}
    out = nc.dram_tensor("out_x", (B, S, D), F32, kind="ExternalOutput").ap()
    build(nc, io, out)
    r = run_bass_kernel_spmd(nc, [{"in_" + n: a for n, a in arrays.items()}], core_ids=[0])
    return r.results[0]["out_x"]
```

```python
from contextlib import ExitStack

import numpy as np

import concourse.bass as bass
from concourse import mybir
from concourse.alu_op_type import AluOpType as ALU

ACT = mybir.ActivationFunctionType
F32 = mybir.dt.float32
BF16 = mybir.dt.bfloat16
U32 = mybir.dt.uint32
AX_X = mybir.AxisListType.X

P = 128
D = 256
KD = D // P
B = 4
S = 256
T = B * S
NT = T // P
QT = S // P
CD = 128
G = 8
PARTS = 6
Q_ROWS = (slice(0, 3), slice(3, 6, 2), slice(4, 5))
K_ROWS = (slice(2, 5), slice(0, 6, 5), slice(1, 2))
DCA = 16
MAIN = S - DCA
ROUNDER = 1.5 * 2.0 ** 23
PI_BELOW = 3.1415925


def bcast(ap, axis, n):
    a = ap.unsqueeze(axis)
    shape = list(a.shape)
    shape[axis] = n
    return a.broadcast_to(shape)


class Layer:

    def __init__(self, name, heads, shifts, scale):
        self.name = name
        self.heads = heads
        self.hd = D // heads
        self.rows = PARTS * self.hd
        self.shifts = shifts
        self.krows = self.rows + 2 * shifts
        self.vw = shifts * (self.hd + 1)
        self.scale = scale
        self.groups = heads // G
        self.units = B * self.groups
        self.row_tiles = 2 if self.krows <= P // 2 else 1

    def place(self, i, k):
        return (i + k * G // 2, k * P // 2, i) if self.row_tiles == 2 else (2 * i + k, 0, 2 * i + k)


L0 = Layer("l0", 32, 1, float(1.0 / np.sqrt(np.float32(8))))
L1 = Layer("l1", 16, 2, 0.25)


class Chain:

    def __init__(self, eng, sem, base=0):
        self.eng, self.sem, self.base, self.n = eng, sem, base, 0

    def link(self, ins):
        self.n += 1
        ins.then_inc(self.sem, 1)
        self.eng.wait_ge(self.sem, self.base + self.n)


class Mem:

    def __init__(self, nc, ctx):
        self.nc, self.ctx = nc, ctx
        self.stage_sems, self.old_sems = [], []

    def sb(self, name, shape, dt=F32, ctx=None):
        return (ctx or self.ctx).enter_context(self.nc.sbuf_tensor(name, shape, dt))

    def sem(self, name, ctx=None):
        s = (ctx or self.ctx).enter_context(self.nc.semaphore(name))
        if ctx is not None:
            self.stage_sems.append(s)
        return s

    def clear_sems(self, dve):
        for s in self.old_sems:
            dve.sem_clear(s)
        self.old_sems = []


def rsqrt_vector(nc, dve, chain, var, eps, work, root_in, root_out, turn=1):
    v, y, r, t = work
    if eps is not None:
        chain.link(nc.vector.tensor_scalar(v, var, eps, None, ALU.add))
    nc.vector.reciprocal(t, v).then_inc(root_in, 1)
    dve.wait_ge(root_out, turn)
    chain.link(nc.vector.tensor_tensor(t, y, y, ALU.mult))
    chain.link(nc.vector.tensor_tensor(r, t, v, ALU.mult))
    chain.link(nc.vector.tensor_scalar(t, r, -0.5, 1.5, ALU.mult, ALU.add))
    chain.link(nc.vector.tensor_tensor(r, y, t, ALU.mult))


def layernorm_vector(nc, dve, chain, m, eps, root_in, root_out, xn_ready):
    for i in range(NT):
        ins = nc.vector.bn_stats(m.bn[:, i, :], m.xs[:, i, :])
    chain.link(ins)
    for i in range(NT):
        ins = nc.vector.bn_aggr(m.mv[:, i, :], m.bn[:, i, :])
    chain.link(ins)
    rsqrt_vector(nc, dve, chain, m.mv[:, :, 1], eps, [m.rstd[:, j, :] for j in range(4)], root_in, root_out)
    for i in range(NT):
        nc.vector.tensor_scalar(m.xn[:, i, :], m.xs[:, i, :], m.mv[:, i, 0:1], m.rstd[:, 2, i:i + 1],
                                ALU.subtract, ALU.mult).then_inc(xn_ready, 1)


def layernorm_scalar(nc, act, m, root_in, root_out):
    act.wait_ge(root_in, 1)
    nc.scalar.activation(m.rstd[:, 1, :], m.rstd[:, 3, :], ACT.Sqrt).then_inc(root_out, 1)


def transpose_tile(nc, m, bank, src):
    for c in range(KD):
        ins = nc.tensor.transpose(m.ps[:, bank, c * P:(c + 1) * P], src[:, c * P:(c + 1) * P], m.ident[:])
    return ins


def transposed_copy(nc, m, i, bank, dst):
    return nc.scalar.copy(dst[:, :, i * P:(i + 1) * P],
                          m.ps[:, bank, 0:D].rearrange("p (c t) -> p c t", c=KD))


def matmul_tile(nc, out, xT, i, w, bias=None, ones=None):
    for c in range(KD):
        ins = nc.tensor.matmul(out, xT[:, c, i * P:(i + 1) * P], w[:, c, :], start=(c == 0),
                               stop=(c == KD - 1 and bias is None))
    if bias is not None:
        ins = nc.tensor.matmul(out, ones, bias, start=False, stop=True)
    return ins


SPLITS = [(src, half, th) for src in ("k", "q") for th in range(2) for half in range(KD)]
K_SPLITS, Q_SPLITS = range(4), range(4, 8)
SW = 4 * P
WRITES = 3
SB = 4
K_TURN = 6
SPLIT_BANKS = (6, 7, 0, 1)


def split_tensor(nc, pe, m, s, tiles_ready, parts_taken):
    src, half, th = SPLITS[s]
    tile = m.k_tm if src == "k" else m.q_tm
    pe.wait_ge(tiles_ready, (0 if src == "k" else NT) + 4 * th + 4)
    if s >= SB:
        pe.wait_ge(parts_taken, s - SB + 1)
    for j in range(4):
        ins = nc.tensor.transpose(m.ps[:, SPLIT_BANKS[s % SB], j * P:(j + 1) * P],
                                  tile[:, 4 * th + j, half * P:(half + 1) * P], m.ident[:])
    return ins


def split_writes(sp, m, s, part_dma):
    src, half, th = SPLITS[s]
    for part, rows in enumerate(Q_ROWS if src == "q" else K_ROWS):
        dst = m.stacks[src][half * P:(half + 1) * P, rows, th * SW:(th + 1) * SW]
        sp.dma_start(dst, bcast(m.part[:, s % SB, part, :], 1, dst.shape[1])
                     ).then_inc(part_dma[s % SB], 16)


def prep_l0(nc, m, io):
    lay = L0
    with ExitStack() as ctx:
        def sem(n):
            return m.sem("p0_" + n, ctx)
        wq = m.sb("p0_wq", [P, KD, D], ctx=ctx)
        wkv = m.sb("p0_wkv", [P, 2 * D], ctx=ctx)
        ang = m.sb("p0_ang", [P, 2, NT, 4], ctx=ctx)
        trig = m.sb("p0_trig", [P, 2, NT, 4], ctx=ctx)
        turns = m.sb("p0_turns", [P, 2, NT, 4], ctx=ctx)
        pos = m.sb("p0_pos", [P, NT, 2], ctx=ctx)
        rot = m.sb("p0_rot", [P, 2, 2, D], ctx=ctx)
        ld_const, ld_x, ld_ctx, ld_wkv, ld_wq, ld_pos = (sem(n) for n in (
            "ld_const", "ld_x", "ld_ctx", "ld_wkv", "ld_wq", "ld_pos"))
        step, xn_ready, xt_ps, xt_ready = sem("step"), sem("xn_ready"), sem("xt_ps"), sem("xt_ready")
        kv_ps, v_copied, q_ps, rot_ready, rot_done = (sem(n) for n in (
            "kv_ps", "v_copied", "q_ps", "rot_ready", "rot_done"))
        ang_ready, trig_ready, root_in, root_out = (sem(n) for n in ("ang_ready", "trig_ready", "root_in", "root_out"))
        split_ps, hi_ready, rest_ready, mid_ready, lo_ready, ones_set = (sem(n) for n in (
            "split_ps", "hi_ready", "rest_ready", "mid_ready", "lo_ready", "ones_set"))
        part_dma = m.part_dma[lay.name]
        ps = m.ps
        block = ctx.enter_context(nc.Block())

        @block.sync
        def _(sp):
            sp.dma_start(m.xs[:], io["x"].rearrange("b (i p) d -> p (b i) d", p=P)).then_inc(ld_x, 16)
            for dst, name in ((m.ident, "ident"), (m.ones_row, "ones_row")):
                sp.dma_start(dst[:], io[name]).then_inc(ld_const, 16)
            sp.dma_start(m.ctxT[:], io["ctxT"]).then_inc(ld_ctx, 16)
            sp.dma_start(wkv[:], io["L0_xattn_Wkv"]).then_inc(ld_wkv, 16)
            sp.dma_start(pos[:], io["fside_BxSx2_0"].rearrange("b (i p) c -> p (b i) c", p=P)).then_inc(ld_pos, 16)
            sp.dma_start(wq[:], io["L0_xattn_Wq"].rearrange("(c p) n -> p c n", p=P)).then_inc(ld_wq, 16)
            for s in range(len(SPLITS)):
                sp.wait_ge(lo_ready, s + 1)
                sp.wait_ge(mid_ready, s + 1)
                split_writes(sp, m, s, part_dma)

        @block.tensor
        def _(pe):
            pe.wait_ge(ld_ctx, 16)
            pe.wait_ge(ld_wkv, 16)
            for i in range(NT):
                if i >= 2:
                    pe.wait_ge(v_copied, i - 1)
                    pe.wait_ge(rot_ready, i - 1)
                for side in range(2):
                    ins = nc.tensor.matmul(ps[:, 2 * side + i % 2, 0:D], m.ctxT[:, i * P:(i + 1) * P],
                                           wkv[:, side * D:(side + 1) * D], start=True, stop=True)
                ins.then_inc(kv_ps, 1)
            pe.wait_ge(v_copied, NT)
            pe.wait_ge(ld_const, 32)
            pe.wait_ge(ld_wq, 16)
            for i in range(NT + 1):
                if i == 3:
                    for s in K_SPLITS:
                        split_tensor(nc, pe, m, s, rot_done, rest_ready).then_inc(split_ps, 1)
                if i < NT:
                    pe.wait_ge(xn_ready, i + 1)
                    if i >= 2:
                        pe.wait_ge(xt_ready, i - 1)
                    transpose_tile(nc, m, 2 + i % 2, m.xn[:, i, :]).then_inc(xt_ps, 1)
                if i >= 1:
                    t = i - 1
                    pe.wait_ge(xt_ready, t + 1)
                    if t >= 2:
                        pe.wait_ge(rot_ready, NT + t - 1)
                    matmul_tile(nc, ps[:, 4 + t % 2, 0:D], m.xT, t, wq).then_inc(q_ps, 1)
            for s in Q_SPLITS:
                split_tensor(nc, pe, m, s, rot_done, rest_ready).then_inc(split_ps, 1)

        @block.vector
        def _(dve):
            chain = Chain(dve, step)
            dve.wait_ge(ld_pos, 16)
            for f, freq in enumerate((1.0, 10000.0 ** -0.5)):
                for k, phase in enumerate((0.0, np.pi / 2)):
                    ins = nc.vector.tensor_scalar(ang[:, k, :, f::2], pos[:], float(np.float32(freq)),
                                                  float(phase), ALU.mult, ALU.add)
            chain.link(ins)
            chain.link(nc.vector.tensor_scalar(turns[:], ang[:], float(0.5 / np.pi), ROUNDER, ALU.mult, ALU.add))
            chain.link(nc.vector.tensor_scalar(trig[:], turns[:], ROUNDER, float(-2 * np.pi), ALU.subtract, ALU.mult))
            chain.link(nc.vector.tensor_tensor(turns[:], trig[:], ang[:], ALU.add))
            nc.vector.tensor_scalar(ang[:], turns[:], PI_BELOW, -PI_BELOW, ALU.min, ALU.max).then_inc(ang_ready, 1)
            nc.vector.memset(m.v0[:, :, :, lay.hd:lay.hd + 1], 1.0).then_inc(ones_set, 1)
            dve.wait_ge(ld_x, 16)
            layernorm_vector(nc, dve, chain, m, 1e-5, root_in, root_out, xn_ready)
            dve.wait_ge(trig_ready, 1)
            for n in range(2 * NT):
                if n == NT:
                    split_vector(nc, dve, m, K_SPLITS, hi_ready, lo_ready, rest_ready)
                i, k_side = n % NT, n < NT
                dve.wait_ge(kv_ps if k_side else q_ps, i + 1)
                if n >= 2:
                    dve.wait_ge(rot_done, n - 1)
                src = ps[:, (0 if k_side else 4) + i % 2, 0:D].rearrange("p (h a e) -> p h (a e)", h=32, a=4)
                src = src.rearrange("p h (a e) -> p h a e", a=4)
                for k in range(2):
                    w = trig[:, k, i, :]
                    wb = w.unsqueeze(1).unsqueeze(3).broadcast_to([P, 32, 4, 2])
                    ins = nc.vector.tensor_tensor(rot[:, n % 2, k, :].rearrange("p (h a e) -> p h a e", h=32, a=4),
                                                  src, wb, ALU.mult)
                chain.link(ins)
                dst, sin, cos = (tile.rearrange("p (a e) -> p a e", e=2) for tile in (
                    (m.k_tm if k_side else m.q_tm)[:, i, :], rot[:, n % 2, 0, :], rot[:, n % 2, 1, :]))
                nc.vector.tensor_tensor(dst[:, :, 0], cos[:, :, 0], sin[:, :, 1], ALU.subtract
                                        ).then_inc(rot_ready, 1)
            split_vector(nc, dve, m, Q_SPLITS, hi_ready, lo_ready, rest_ready)

        @block.scalar
        def _(act):
            act.wait_ge(ang_ready, 1)
            nc.scalar.activation(trig[:], ang[:], ACT.Sin).then_inc(trig_ready, 1)
            layernorm_scalar(nc, act, m, root_in, root_out)
            act.wait_ge(ones_set, 1)
            for i in range(NT):
                act.wait_ge(kv_ps, i + 1)
                nc.scalar.copy(m.v0[:, i, :, 0:lay.hd],
                               ps[:, 2 + i % 2, 0:D].rearrange("p (h e) -> p h e", h=32)).then_inc(v_copied, 1)
            for i in range(NT):
                if i == 3:
                    split_scalar(nc, act, m, K_SPLITS, split_ps, part_dma, hi_ready, rest_ready, mid_ready)
                act.wait_ge(xt_ps, i + 1)
                transposed_copy(nc, m, i, 2 + i % 2, m.xT).then_inc(xt_ready, 1)
            split_scalar(nc, act, m, Q_SPLITS, split_ps, part_dma, hi_ready, rest_ready, mid_ready)

        @block.gpsimd
        def _(pool):
            pool.wait_ge(ld_const, 32)
            nc.gpsimd.tensor_copy(m.ident_bf[:], m.ident[:])
            for n in range(2 * NT):
                if n == NT:
                    split_gpsimd(nc, pool, m, K_SPLITS, mid_ready, rest_ready, part_dma, lo_ready)
                i = n % NT
                dst = (m.k_tm if n < NT else m.q_tm)[:, i, :].rearrange("p (a e) -> p a e", e=2)
                sin = rot[:, n % 2, 0, :].rearrange("p (a e) -> p a e", e=2)
                cos = rot[:, n % 2, 1, :].rearrange("p (a e) -> p a e", e=2)
                pool.wait_ge(rot_ready, n + 1)
                nc.gpsimd.tensor_tensor(dst[:, :, 1], sin[:, :, 0], cos[:, :, 1], ALU.add).then_inc(rot_done, 1)
            split_gpsimd(nc, pool, m, Q_SPLITS, mid_ready, rest_ready, part_dma, lo_ready)


def split_scalar(nc, act, m, splits, split_ps, part_dma, hi_ready, rest_ready, mid_ready):
    def high(s):
        act.wait_ge(split_ps, s + 1)
        if s >= SB:
            act.wait_ge(part_dma[s % SB], 16 * WRITES * (s // SB))
        nc.scalar.copy(m.part[:, s % SB, 0, :], m.ps[:, SPLIT_BANKS[s % SB], :]).then_inc(hi_ready, 1)

    high(splits[0])
    for s in splits:
        if s + 1 in splits:
            high(s + 1)
        act.wait_ge(rest_ready, s + 1)
        nc.scalar.copy(m.part[:, s % SB, 1, :], m.rest[:, s % SB, :]).then_inc(mid_ready, 1)


def split_vector(nc, dve, m, splits, hi_ready, lo_ready, rest_ready):
    for s in splits:
        dve.wait_ge(hi_ready, s + 1)
        if s >= SB:
            dve.wait_ge(lo_ready, s - SB + 1)
        nc.vector.tensor_tensor(m.rest[:, s % SB, :], m.ps[:, SPLIT_BANKS[s % SB], :], m.part[:, s % SB, 0, :],
                                ALU.subtract).then_inc(rest_ready, 1)


def split_gpsimd(nc, pool, m, splits, mid_ready, rest_ready, part_dma, lo_ready):
    for s in splits:
        pool.wait_ge(rest_ready, s + 1)
        pool.wait_ge(mid_ready, s + 1)
        if s >= SB:
            pool.wait_ge(part_dma[s % SB], 16 * WRITES * (s // SB))
        nc.gpsimd.tensor_tensor(m.part[:, s % SB, 2, :], m.rest[:, s % SB, :], m.part[:, s % SB, 1, :],
                                ALU.subtract).then_inc(lo_ready, 1)


def zero_slots(nc, pool, m, zeros, zero_set, t_ps, unit):
    nc.gpsimd.memset(zeros[:], 0.0).then_inc(zero_set, 1)
    pool.wait_ge(zero_set, 1)
    writes = [(m.x_slots, r) for r in range(BLOCKS // ROUND)] + \
             [(m.y_slots, r) for r in range(E1 // ROUND, BLOCKS // ROUND)]
    for n, (slots, r) in enumerate(writes):
        pool.wait_ge(t_ps, unit * (n + 1))
        rows = slots[r * ROUND * P:(r + 1) * ROUND * P, :].rearrange("(b p) d -> p b d", p=P)
        pool.dma_start(rows, bcast(zeros[:], 1, ROUND)).then_inc(m.zeroed, 16)


NBUF = 4
AHEAD = 2
PROBS = 4
LAG = 1
TURN_LAG = 2


def attention(nc, m, lay, io):
    U, GR, R, SH, W, hd = lay.units, lay.groups, lay.rows, lay.shifts, lay.vw, lay.hd
    cuts = ((0, S),) if SH == 1 else ((0, MAIN), (MAIN, S))
    v = m.v0 if lay is L0 else m.v1
    ps = m.ps
    CT = 4 // SH
    HG = 2 * CT
    NG = G // HG
    UP = G // 2
    PAIRS = U * UP
    RT = lay.row_tiles
    tiles = [k * P // 2 for k in range(RT)]
    GT = G // RT
    with ExitStack() as ctx:
        def sem(n):
            return m.sem(lay.name + "a_" + n, ctx)
        qs = m.sb(lay.name + "_qs", [tiles[-1] + lay.krows, NBUF, GT, S], BF16, ctx)
        ks = m.sb(lay.name + "_ks", [tiles[-1] + lay.krows, NBUF, GT, S], BF16, ctx)
        prob = m.sb(lay.name + "_prob", [P, PROBS, 2, QT, S], ctx=ctx)
        mx = m.sb(lay.name + "_mx", [P, 2, QT, SH, G], ctx=ctx)
        neg = m.sb(lay.name + "_neg", [P, 2, QT, SH, 2, G], BF16, ctx)
        negT = m.sb(lay.name + "_negT", [2 * SH * G, 2, S], BF16, ctx)
        sumsT = m.sb(lay.name + "_sumsT", [P, 2, 2 * S], ctx=ctx)
        zero_row = m.sb(lay.name + "_zero_row", [1, 2 * S], ctx=ctx)
        rec = m.sb(lay.name + "_rec", [P, QT, CT * SH], ctx=ctx)
        ctxv = m.sb(lay.name + "_ctxv", [P, QT, CT * SH, hd], ctx=ctx)
        if lay is L0:
            zeros, zero_set = m.sb("zeros", [P, D], ctx=ctx), sem("zero_set")
        loaded = [sem(f"loaded{b}") for b in range(NBUF)]
        shifted = [sem(f"shifted{b}") for b in range(NBUF)]
        ones_ld, zero_row_set = m.ones_ld[lay.name], sem("zero_row_set")
        s_ps, s_max, step, neg_ready = sem("s_ps"), sem("s_max"), sem("step"), sem("neg_ready")
        negT_ps, negT_ready, t_ps, t_exp = sem("negT_ps"), sem("negT_ready"), sem("t_ps"), sem("t_exp")
        weighed, sums_copied, tok_ps, tok_used = sem("weighed"), sem("sums_copied"), sem("tok_ps"), sem("tok_used")
        block = ctx.enter_context(nc.Block())

        def score_bank(n):
            return n % 3 * 2 if n < AHEAD * UP else 0

        def turn_at(n):
            past = n - TURN_LAG - (CT - 1)
            return past // CT * 2 + past % CT if past >= 0 and past % CT < 2 and past // CT * CT < PAIRS else None

        @block.sync
        def _(sp):
            def load(u, b):
                bt, g = u // GR, u % GR
                if g == 0 and bt % 2 == 0:
                    for a in (bt, bt + 1):
                        sp.wait_ge(m.part_dma[lay.name][a], 16 * WRITES * len(SPLITS) // SB)
                for dst, src in ((qs, "q"), (ks, "k")):
                    for k, row in enumerate(tiles):
                        dims = (g * G + k * GT) * hd
                        stack = m.stacks[src][dims:dims + GT * hd, :, bt * S:(bt + 1) * S]
                        sp.dma_start(dst[row:row + R, b, :, :], stack.rearrange("(h d) j t -> (d j) h t", d=hd)
                                     ).then_inc(loaded[b], 16)

            def shift_rows(u, b):
                sp.wait_ge(negT_ready, u + 1)
                for k, row in enumerate(tiles):
                    for r in range(2 * SH):
                        sp.dma_start(qs[row + R + r:row + R + r + 1, b, :, :],
                                     negT[r * G + k * GT:r * G + (k + 1) * GT, b % 2, :]).then_inc(shifted[b], 16)

            for u in range(NBUF):
                load(u, u)
            for u in range(U):
                shift_rows(u, u % NBUF)
                if u >= AHEAD and u + NBUF - AHEAD < U:
                    n = u - AHEAD
                    sp.wait_ge(t_ps, UP * (n + 1))
                    load(n + NBUF, n % NBUF)

        @block.gpsimd
        def _(pool):
            nc.gpsimd.memset(zero_row[:], 0.0).then_inc(zero_row_set, 1)
            for b in range(NBUF):
                for row in tiles:
                    pool.dma_start(ks[row + R:row + lay.krows, b, :, :], io[lay.name + "_ones"][:, 0:GT, :]
                                   ).then_inc(ones_ld, 16)
            if lay is L0:
                zero_slots(nc, pool, m, zeros, zero_set, t_ps, UP)

        @block.tensor
        def _(pe):
            turned = [0]
            maxed = [0]

            def scores(n):
                u, i = n // UP, n % UP
                if i == 0:
                    pe.wait_ge(loaded[u % NBUF], 32 * RT * (u // NBUF + 1))
                if n >= AHEAD * UP:
                    pe.wait_ge(s_max, n)
                elif n >= 3:
                    pe.wait_ge(s_max, n - 2)
                for qt in range(QT):
                    for k in range(2):
                        _, row, col = lay.place(i, k)
                        ins = nc.tensor.matmul(ps[:, score_bank(n) + k, qt * S:(qt + 1) * S],
                                               qs[row:row + R, u % NBUF, col, qt * P:(qt + 1) * P],
                                               ks[row:row + R, u % NBUF, col, :], start=True, stop=True)
                ins.then_inc(s_ps, 1)

            def transposed_maxima(u):
                pe.wait_ge(neg_ready, u + 1)
                if u >= 1:
                    pe.wait_ge(negT_ready, u)
                if turned[0]:
                    pe.wait_ge(tok_used, turned[0])
                out = ps[0:2 * SH * G, 7, 384:512].bitcast(BF16)
                for qt in range(QT):
                    ins = nc.tensor.transpose(out[:, qt * P:(qt + 1) * P],
                                              neg[:, u % 2, qt, :, :, :].rearrange("p s k g -> p (s k g)"),
                                              m.ident_bf[:])
                ins.then_inc(negT_ps, 1)
                maxed[0] += 1

            def shifted_scores(n):
                u, i = n // UP, n % UP
                b = u % NBUF
                if i == 0:
                    pe.wait_ge(shifted[b], 32 * SH * RT * (u // NBUF + 1))
                if n >= 2:
                    pe.wait_ge(t_exp, n - 1)
                for kt in range(QT):
                    for k in range(2):
                        _, row, col = lay.place(i, k)
                        ins = nc.tensor.matmul(ps[:, 2 + 2 * (n % 2) + k, kt * S:(kt + 1) * S],
                                               ks[row:row + lay.krows, b, col, kt * P:(kt + 1) * P],
                                               qs[row:row + lay.krows, b, col, :], start=True, stop=True)
                ins.then_inc(t_ps, 1)

            def values(c):
                pe.wait_ge(t_exp, CT * (c + 1) // 2)
                if c % 2 == 0 and c >= 2:
                    pe.wait_ge(sums_copied, c // 2)
                for kt in range(QT):
                    for j in range(CT):
                        n, k = CT // 2 * c + j % (CT // 2), j // (CT // 2)
                        head = n // UP % GR * G + lay.place(n % UP, k)[0]
                        row = j * P // CT
                        ins = nc.tensor.matmul(ps[row:row + W, 6, (c % 2) * S:(c % 2 + 1) * S],
                                               v[:, n // UP // GR * QT + kt, head, :], prob[:, n % PROBS, k, kt, :],
                                               start=(kt == 0), stop=(kt == QT - 1))
                ins.then_inc(weighed, 1)

            def token_sums(c):
                gi = c // 2
                pe.wait_ge(sums_copied, gi + 1)
                if c >= 1:
                    pe.wait_ge(tok_used, c)
                pe.wait_ge(negT_ready, maxed[0])
                for q in range(QT):
                    ins = nc.tensor.transpose(ps[:, 7, q * P:(q + 1) * P],
                                              sumsT[:, gi % 2, (c % 2) * S + q * P:(c % 2) * S + (q + 1) * P],
                                              m.ident[:])
                ins.then_inc(tok_ps, 1)
                turned[0] += 1

            pe.wait_ge(zero_row_set, 1)
            nc.tensor.matmul(ps[:, 6, :], m.ones_row[:], zero_row[:], start=True, stop=True)
            for n in range(AHEAD * UP):
                scores(n)
                if n == UP:
                    transposed_maxima(0)
            pe.wait_ge(ones_ld, 16 * RT * NBUF)
            for n in range(PAIRS + TURN_LAG + 1):
                if n + AHEAD * UP < PAIRS:
                    scores(n + AHEAD * UP)
                if n < PAIRS:
                    shifted_scores(n)
                    if n % UP == 0 and n // UP + 1 < U:
                        transposed_maxima(n // UP + 1)
                if n >= LAG and (n - LAG + 1) % (CT // 2) == 0 and n - LAG < PAIRS:
                    values((n - LAG + 1) // (CT // 2) - 1)
                if turn_at(n) is not None:
                    token_sums(turn_at(n))

        @block.vector
        def _(dve):
            m.clear_sems(dve)
            chain = Chain(dve, step)

            def maxima(n):
                u, i = n // UP, n % UP
                first, second = (lay.place(i, k)[0] for k in range(2))
                dve.wait_ge(s_ps, n + 1)
                pair = ps[:, score_bank(n):score_bank(n) + 2, :].rearrange("p k (q t) -> p k q t", q=QT)
                for s, (lo, hi) in enumerate(cuts):
                    ins = nc.vector.reduce_max(
                        mx[:, u % 2, :, s, first:second + 1:second - first].rearrange("p q k -> p k q"),
                        pair[:, :, :, lo:hi], AX_X)
                ins.then_inc(s_max, 1)

            def negated(u):
                dve.wait_ge(s_max, UP * (u + 1))
                if u >= 2:
                    dve.wait_ge(negT_ps, u - 1)
                chain.link(nc.vector.tensor_scalar(neg[:, u % 2, :, :, 0, :], mx[:, u % 2, :, :, :],
                                                   -1.0, None, ALU.mult))
                for q in range(QT):
                    ins = nc.vector.scalar_tensor_tensor(neg[:, u % 2, q, :, 1, :], mx[:, u % 2, q, :, :], -1.0,
                                                         neg[:, u % 2, q, :, 0, :], ALU.mult, ALU.subtract)
                ins.then_inc(neg_ready, 1)

            def normalise(c):
                gi = c // 2
                u = gi // NG
                bt, col = u // GR, (u % GR * G + gi % NG * HG) * hd
                sums = ps[:, 7, 0:QT * P].rearrange("p (q n r) -> p q n r", q=QT, n=CT)[:, :, :, 0:W]
                sums = sums.rearrange("p q n (s e) -> p q n s e", s=SH)
                dve.wait_ge(tok_ps, c + 1)
                chain.link(nc.vector.reciprocal(rec[:].rearrange("p q (n s) -> p q n s", s=SH),
                                                sums[:, :, :, :, hd]))
                for q in range(QT):
                    dst = m.attn[:, bt * QT + q, col:col + HG * hd]
                    weight = bcast(rec[:, q, :], 2, hd)
                    if SH == 1:
                        out = dst.rearrange("p (k c n e) -> p k c n e", k=2, c=2, n=2)[:, :, c % 2, :, :]
                        src = sums[:, q, :, 0, 0:hd].rearrange("p (k n) e -> p k n e", k=2)
                        weight = weight.rearrange("p (k n) e -> p k n e", k=2)
                    else:
                        out = ctxv[:, q, :, :].rearrange("p (n s) e -> p n s e", s=SH)
                        src = sums[:, q, :, :, 0:hd]
                        weight = weight.rearrange("p (n s) e -> p n s e", s=SH)
                    ins = nc.vector.tensor_tensor(out, src, weight, ALU.mult)
                ins.then_inc(tok_used, 1)
                if SH == 2:
                    dve.wait_ge(tok_used, c + 1)
                    parts = ctxv[:].rearrange("p q (n s) e -> p q n s e", s=SH)
                    dst = m.attn[:, bt * QT:(bt + 1) * QT, col + c % 2 * CT * hd:col + (c % 2 + 1) * CT * hd]
                    nc.vector.tensor_tensor(dst.rearrange("p q (n e) -> p q n e", e=hd),
                                            parts[:, :, :, 0, :], parts[:, :, :, 1, :], ALU.add)

            for n in range(AHEAD * UP):
                maxima(n)
                if n % UP == UP - 1:
                    negated(n // UP)
            for n in range(PAIRS + TURN_LAG + 1):
                if n + AHEAD * UP < PAIRS:
                    maxima(n + AHEAD * UP)
                    if n % UP == UP - 1:
                        negated(n // UP + AHEAD)
                if turn_at(n) is not None:
                    normalise(turn_at(n))

        @block.scalar
        def _(act):
            def maxima_rows(u):
                act.wait_ge(negT_ps, u + 1)
                if u >= 2:
                    act.wait_ge(shifted[(u - 2) % NBUF], 32 * SH * RT * ((u - 2) // NBUF + 1))
                nc.scalar.copy(negT[:, u % 2, :], ps[0:2 * SH * G, 7, 384:512].bitcast(BF16)
                               ).then_inc(negT_ready, 1)

            def exponentials(n):
                act.wait_ge(t_ps, n + 1)
                if n >= PROBS:
                    act.wait_ge(weighed, 2 * (n - PROBS) // CT + 1)
                nc.scalar.activation(prob[:, n % PROBS, :, :, :].rearrange("p h k q -> p (h k q)"),
                                     ps[:, 2 + 2 * (n % 2):4 + 2 * (n % 2), :].rearrange("p b n -> p (b n)"),
                                     ACT.Exp, scale=lay.scale).then_inc(t_exp, 1)

            def copied_sums(gi):
                act.wait_ge(weighed, 2 * (gi + 1))
                if gi >= 2:
                    act.wait_ge(tok_ps, 2 * (gi - 1))
                nc.scalar.copy(sumsT[:, gi % 2, :], ps[:, 6, :]).then_inc(sums_copied, 1)

            maxima_rows(0)
            for n in range(PAIRS + 1):
                if n < PAIRS:
                    exponentials(n)
                    if n % UP == 0 and n // UP + 1 < U:
                        maxima_rows(n // UP + 1)
                if n >= CT and n % CT == 0:
                    copied_sums(n // CT - 1)


def attention_output(nc, m, name, w_dram, b_dram):
    with ExitStack() as ctx:
        def sem(n):
            return m.sem(name + n, ctx)
        w = m.sb(name + "w", [P, KD, D], ctx=ctx)
        b = m.sb(name + "b", [P, D], ctx=ctx)
        ld, bias_ld, bias_added = (sem(n) for n in ("ld", "bias_ld", "bias_added"))
        at_ps, at_ready, out_ps, out_used = (sem(n) for n in ("at_ps", "at_ready", "out_ps", "out_used"))
        block = ctx.enter_context(nc.Block())

        @block.sync
        def _(sp):
            sp.dma_start(w[:], w_dram.rearrange("(c p) n -> p c n", p=P)).then_inc(ld, 16)
            sp.dma_start(b[:], b_dram.partition_broadcast(P)).then_inc(bias_ld, 16)

        @block.tensor
        def _(pe):
            for i in range(NT + 1):
                if i < NT:
                    if i >= 2:
                        pe.wait_ge(at_ready, i - 1)
                    transpose_tile(nc, m, i % 2, m.attn[:, i, :]).then_inc(at_ps, 1)
                if i == 1:
                    pe.wait_ge(ld, 16)
                if i >= 1:
                    t = i - 1
                    pe.wait_ge(at_ready, t + 1)
                    if t >= 2:
                        pe.wait_ge(out_used, t - 1)
                    matmul_tile(nc, m.ps[:, 2 + t % 2, 0:D], m.xT, t, w).then_inc(out_ps, 1)

        @block.scalar
        def _(act):
            for i in range(NT):
                act.wait_ge(at_ps, i + 1)
                transposed_copy(nc, m, i, i % 2, m.xT).then_inc(at_ready, 1)

        @block.vector
        def _(dve):
            dve.wait_ge(bias_ld, 16)
            nc.vector.tensor_tensor(m.xs[:], m.xs[:], bcast(b[:], 1, NT), ALU.add).then_inc(bias_added, 1)
            dve.wait_ge(bias_added, 1)
            for i in range(NT):
                dve.wait_ge(out_ps, i + 1)
                nc.vector.tensor_tensor(m.xs[:, i, :], m.xs[:, i, :], m.ps[:, 2 + i % 2, 0:D],
                                        ALU.add).then_inc(out_used, 1)


def rounds(eng, n, body):
    body(0, True, n == 1)
    if n == 3:
        body(1, False, False)
    elif n > 3:
        with eng.Fori(1, n - 1) as g:
            body(g, False, False)
    if n > 1:
        body(n - 1, False, True)


E0, I0 = 16, 128
SH0 = 512 // I0
X0 = E0 + SH0
GRP, GSZ = 4, 4


def route_l0(nc, m, io):
    with ExitStack() as ctx:
        def sem(n):
            return m.sem("r0_" + n, ctx)

        def sb(n, shape, dt=F32):
            return m.sb("r0_" + n, [P] + shape, dt, ctx)
        rw, bias, iota = sb("rw", [KD, E0]), sb("bias", [E0]), sb("iota", [E0])
        score, biased = sb("score", [NT, E0]), sb("biased", [NT, E0])
        hi, lo = sb("hi", [NT * GRP, 2]), sb("lo", [NT * GRP, 2])
        top, second, t0, gsum = (sb(n, [NT * GRP]) for n in ("top", "second", "t0", "gsum"))
        later = sb("later", [GRP, GRP])
        more, same = sb("more", [NT, GRP, GRP]), sb("same", [NT, GRP, GRP])
        rank, masked = sb("rank", [NT, GRP]), sb("masked", [NT, E0])
        top8, idx8, idxf = sb("top8", [NT, 8]), sb("idx8", [NT, 8], U32), sb("idxf", [NT, 8])
        hot, den = sb("hot", [2, NT, E0]), sb("den", [NT])
        ld, step, root_in, root_out, xn_ready, xt_ps, xt_ready, logit_ps, score_ready = (sem(n) for n in (
            "ld", "step", "root_in", "root_out", "xn_ready", "xt_ps", "xt_ready", "logit_ps", "score_ready"))
        block = ctx.enter_context(nc.Block())

        @block.sync
        def _(sp):
            sp.dma_start(rw[:], io["L0_router_T"].rearrange("(c p) n -> p c n", p=P)).then_inc(ld, 16)
            sp.dma_start(bias[:], io["L0_ffn_e_bias"].partition_broadcast(P)).then_inc(ld, 16)
            sp.dma_start(iota[:], io["iota"][0:E0].partition_broadcast(P)).then_inc(ld, 16)
            sp.dma_start(later[:], io["later"].partition_broadcast(P)).then_inc(ld, 16)
            for j in range(2):
                load_expert_l0(sp, m, io, j, j)

        @block.tensor
        def _(pe):
            pe.wait_ge(ld, 64)
            transpose_and_project(nc, pe, m, xn_ready, xt_ps, xt_ready, rw, E0, logit_ps)

        @block.scalar
        def _(act):
            layernorm_scalar(nc, act, m, root_in, root_out)
            for i in range(NT):
                act.wait_ge(xt_ps, i + 1)
                transposed_copy(nc, m, i, i % 2, m.xT).then_inc(xt_ready, 1)
            act.wait_ge(logit_ps, 1)
            nc.scalar.activation(score[:].rearrange("p i e -> p (i e)"), m.ps[:, 2, 0:NT * E0], ACT.Sigmoid
                                 ).then_inc(score_ready, 1)

        @block.vector
        def _(dve):
            chain = Chain(dve, step)
            link, v = chain.link, nc.vector
            layernorm_vector(nc, dve, chain, m, 1e-5, root_in, root_out, xn_ready)
            v.memset(m.comb[:, :, E0:X0], 1.0)
            dve.wait_ge(ld, 64)
            dve.wait_ge(score_ready, 1)
            link(v.tensor_tensor(biased[:], score[:], bcast(bias[:], 1, NT), ALU.add))
            pairs = biased[:].rearrange("p i (g a b) -> p (i g) a b", g=GRP, b=2)
            v.tensor_tensor(hi[:], pairs[:, :, :, 0], pairs[:, :, :, 1], ALU.max)
            link(v.tensor_tensor(lo[:], pairs[:, :, :, 0], pairs[:, :, :, 1], ALU.min))
            v.tensor_tensor(top[:], hi[:, :, 0], hi[:, :, 1], ALU.max)
            v.tensor_tensor(second[:], hi[:, :, 0], hi[:, :, 1], ALU.min)
            link(v.tensor_tensor(t0[:], lo[:, :, 0], lo[:, :, 1], ALU.max))
            link(v.tensor_tensor(gsum[:], second[:], t0[:], ALU.max))
            link(v.tensor_tensor(second[:], gsum[:], top[:], ALU.add))
            gs = second[:].rearrange("p (i g) -> p i g", g=GRP)
            mine, other = bcast(gs, 3, GRP), bcast(gs, 2, GRP)
            v.tensor_tensor(more[:], other, mine, ALU.is_gt)
            link(v.tensor_tensor(same[:], other, mine, ALU.is_equal))
            same_earlier = hot[:, 0, :, :].rearrange("p i (g h) -> p i g h", g=GRP)
            link(v.tensor_tensor(same_earlier, same[:], bcast(later[:], 1, NT), ALU.mult))
            link(v.tensor_tensor(same[:], more[:], same_earlier, ALU.add))
            link(v.tensor_reduce(rank[:], same[:], AX_X, ALU.add))
            link(v.tensor_scalar(gsum[:].rearrange("p (i g) -> p i g", g=GRP), rank[:], 1.5, None, ALU.is_lt))
            link(v.tensor_tensor(hot[:, 0, :, :].rearrange("p i (g h) -> p (i g) h", g=GRP),
                                 biased[:].rearrange("p i (g h) -> p (i g) h", g=GRP),
                                 bcast(gsum[:], 2, GSZ), ALU.mult))
            link(v.tensor_scalar(masked[:], hot[:, 0, :, :], 0.0, None, ALU.add))
            top_indices(nc, link, masked, top8, idx8, idxf)
            for j in range(2):
                ins = v.tensor_tensor(hot[:, j, :, :], bcast(iota[:], 1, NT), bcast(idxf[:, :, j], 2, E0), ALU.is_equal)
            link(ins)
            link(v.tensor_tensor(masked[:], hot[:, 0, :, :], hot[:, 1, :, :], ALU.add))
            link(v.tensor_tensor(biased[:], masked[:], score[:], ALU.mult))
            link(v.tensor_reduce(den[:], biased[:], AX_X, ALU.add))
            link(v.tensor_scalar(m.rstd[:, 0, :], den[:], 1e-20, None, ALU.add))
            link(v.reciprocal(den[:], m.rstd[:, 0, :]))
            v.tensor_tensor(m.comb[:, :, 0:E0], biased[:], bcast(den[:], 2, E0), ALU.mult)


def transpose_and_project(nc, pe, m, xn_ready, xt_ps, xt_ready, w, n, logit_ps):
    for i in range(NT):
        pe.wait_ge(xn_ready, i + 1)
        if i >= 2:
            pe.wait_ge(xt_ready, i - 1)
        transpose_tile(nc, m, i % 2, m.xn[:, i, :]).then_inc(xt_ps, 1)
    pe.wait_ge(xt_ready, NT)
    for i in range(NT):
        ins = matmul_tile(nc, m.ps[:, 2, i * n:(i + 1) * n], m.xT, i, w)
    ins.then_inc(logit_ps, 1)


def top_indices(nc, link, values, top8, idx8, idxf):
    for i in range(NT):
        ins = nc.vector.max(top8[:, i, :], values[:, i, :])
    link(ins)
    for i in range(NT):
        ins = nc.vector.max_index(idx8[:, i, :], top8[:, i, :], values[:, i, :])
    link(ins)
    link(nc.vector.tensor_copy(idxf[:], idx8[:]))


def load_expert_l0(sp, m, io, e, j):
    sp.dma_start(m.f0_up[:, j, :, :], io["L0_up"][bass.ds(e, 1), :, :].rearrange("a (c p) n -> p (a c) n", p=P)
                 ).then_inc(m.f0_loaded[j], 16)
    sp.dma_start(m.f0_down[:, j, :], io["L0_down"][bass.ds(e, 1), :, :].rearrange("a p n -> p (a n)")
                 ).then_inc(m.f0_loaded[j], 16)


def experts_l0(nc, m, io):
    with ExitStack() as ctx:
        def sem(n):
            return m.sem("f0_" + n, ctx)
        HT = T // 2
        up, down, loaded = m.f0_up, m.f0_down, m.f0_loaded
        relu = m.sb("f0_relu", [P, 2, HT], ctx=ctx)
        hid = m.sb("f0_hid", [P, 2, HT], ctx=ctx)
        up_ps, relu_done, hid_done, down_ps, added = (sem(n) for n in (
            "up_ps", "relu_done", "hid_done", "down_ps", "added"))
        block = ctx.enter_context(nc.Block())
        NG = X0 // 2

        @block.sync
        def _(sp):
            def body(g, first, last):
                for j in range(2 if not first else 0):
                    e = 2 * g + j
                    sp.wait_ge(down_ps, 8 * (e - 1))
                    load_expert_l0(sp, m, io, e, j)
            rounds(sp, NG, body)

        @block.tensor
        def _(pe):
            def hidden(n, slot, half, loads, first):
                if half == 0:
                    pe.wait_ge(loaded[slot], 32 * loads)
                if not first:
                    pe.wait_ge(relu_done, n - 1)
                for c in range(KD):
                    ins = nc.tensor.matmul(m.ps[:, half, :], up[:, slot, c, :], m.xT[:, c, half * HT:(half + 1) * HT],
                                           start=(c == 0), stop=(c == KD - 1))
                ins.then_inc(up_ps, 1)

            def outputs(n, slot, half, first):
                pe.wait_ge(hid_done, n + 1)
                for t in range(4):
                    if not first:
                        pe.wait_ge(added, 4 * n + t - 3)
                    nc.tensor.matmul(m.ps[:, 2 + t, 0:D], hid[:, half, t * P:(t + 1) * P], down[:, slot, :],
                                     start=True, stop=True).then_inc(down_ps, 1)

            hidden(0, 0, 0, 1, True)

            def body(g, first, last):
                for k in range(4):
                    n = 4 * g + k
                    if not (last and k == 3):
                        hidden(n + 1, ((k + 1) // 2) % 2, (k + 1) % 2, g + 1 + (k == 3), first and k == 0)
                    outputs(n, k // 2, k % 2, first and k == 0)
            rounds(pe, NG, body)

        @block.scalar
        def _(act):
            def body(g, first, last):
                for k in range(4):
                    n = 4 * g + k
                    act.wait_ge(up_ps, n + 1)
                    if not (first and k < 2):
                        act.wait_ge(hid_done, n - 1)
                    nc.scalar.activation(relu[:, k % 2, :], m.ps[:, k % 2, :], ACT.Relu).then_inc(relu_done, 1)
            rounds(act, NG, body)

        @block.gpsimd
        def _(pool):
            def body(g, first, last):
                for k in range(4):
                    n = 4 * g + k
                    pool.wait_ge(relu_done, n + 1)
                    if not (first and k < 2):
                        pool.wait_ge(down_ps, 4 * (n - 1))
                    nc.gpsimd.tensor_tensor(hid[:, k % 2, :], relu[:, k % 2, :], relu[:, k % 2, :], ALU.mult
                                            ).then_inc(hid_done, 1)
            rounds(pool, NG, body)

        @block.vector
        def _(dve):
            def body(g, first, last):
                for k in range(4):
                    for t in range(4):
                        i = 4 * (k % 2) + t
                        dve.wait_ge(down_ps, 16 * g + 4 * k + t + 1)
                        nc.vector.scalar_tensor_tensor(
                            m.xs[:, i, :], m.ps[:, 2 + t, 0:D], m.comb[:, i, bass.ds(2 * g + k // 2, 1)], m.xs[:, i, :],
                            ALU.mult, ALU.add).then_inc(added, 1)
            rounds(dve, NG, body)


def prep_l1(nc, m, io):
    lay, H, hd = L1, L1.heads, L1.hd
    with ExitStack() as ctx:
        def sem(n):
            return m.sem("p1_" + n, ctx)

        def sb(n, shape, parts=P):
            return m.sb("p1_" + n, [parts] + shape, F32, ctx)
        wq, wmain, wdca = sb("wq", [KD, D]), sb("wmain", [2 * D]), sb("wdca", [2 * D])
        bq, bmain, bdca = sb("bq", [D], 1), sb("bmain", [2 * D], 1), sb("bdca", [2 * D], 1)
        tmask = sb("tmask", [2, S], 1)
        pmask = sb("pmask", [QT, 2])
        ctxT_dca = sb("ctxT_dca", [B, P])
        nw, nb = sb("nw", [3, hd]), sb("nb", [3, hd])
        hmean, hvar = sb("hmean", [2, NT, H]), sb("hvar", [2, NT, H])
        hwork = sb("hwork", [2, 4, NT * H])
        sq = sb("sq", [2, D])
        ld, ld_norm, step, root_in, root_out, xn_ready, xt_ps, xt_ready = (sem(n) for n in (
            "ld", "ld_norm", "step", "root_in", "root_out", "xn_ready", "xt_ps", "xt_ready"))
        ctx_ready, v_set, k_ps, v_copied, q_ps, cent, squared, hroot_in, hroot_out, scaled_done, tm_done = (
            sem(n) for n in ("ctx_ready", "v_set", "k_ps", "v_copied", "q_ps", "cent", "squared", "hroot_in",
                             "hroot_out", "scaled_done", "tm_done"))
        pool_step, squares_summed, v_zeroed = sem("pool_step"), sem("squares_summed"), sem("v_zeroed")
        split_ps, hi_ready, rest_ready, mid_ready, lo_ready = (sem(n) for n in (
            "split_ps", "hi_ready", "rest_ready", "mid_ready", "lo_ready"))
        part_dma = m.part_dma[lay.name]
        ps = m.ps
        block = ctx.enter_context(nc.Block())

        @block.sync
        def _(sp):
            loads = [(wq[:], io["L1_xattn_Wq"].rearrange("(c p) n -> p c n", p=P)),
                     (wmain[:], io["L1_wmain"]), (wdca[:], io["L1_xattn_Wkv_dca"]),
                     (bq[:], io["L1_xattn_bq"].rearrange("(a n) -> a n", a=1)),
                     (bmain[:], io["L1_bmain"]), (bdca[:], io["L1_xattn_bkv_dca"].rearrange("(a n) -> a n", a=1)),
                     (tmask[:], io["tmask"]), (pmask[:], io["pmask"])]
            for dst, src in loads:
                sp.dma_start(dst, src).then_inc(ld, 16)
            for dst, which in ((nw, "w"), (nb, "b")):
                sp.dma_start(dst[:, 0, :], io["L1_xattn_qn_" + which].partition_broadcast(P)).then_inc(ld_norm, 16)
                for j in (1, 2):
                    main = P - DCA * (j - 1)
                    sp.dma_start(dst[0:main, j, :], io["L1_xattn_kn_" + which].partition_broadcast(main)
                                 ).then_inc(ld_norm, 16)
                sp.dma_start(dst[P - DCA:P, 2, :],
                             io["L1_xattn_kn_dca_" + which].partition_broadcast(DCA)).then_inc(ld_norm, 16)
            for q in range(PAIRS):
                load_weights(sp, m, io, 2 * q, 2, q)
            for s in range(len(SPLITS)):
                sp.wait_ge(lo_ready, s + 1)
                sp.wait_ge(mid_ready, s + 1)
                split_writes(sp, m, s, part_dma)

        @block.tensor
        def _(pe):
            pe.wait_ge(ld, 8 * 16)
            pe.wait_ge(ctx_ready, 1)
            for i in range(NT):
                odd = i % 2
                if i >= 2:
                    pe.wait_ge(cent, i - 1)
                if i >= 2:
                    pe.wait_ge(v_copied, i - 1)
                main = m.ctxT[:, i * P:(i + 1) * P]
                dca = ctxT_dca[:, i // 2, :]
                mmask, dmask = (tmask[:, a, odd * P:(odd + 1) * P] for a in range(2))
                k_out, v_out, vd_out = ps[:, odd, 0:D], ps[:, 2 + odd, 0:D], ps[:, 2 + odd, D:2 * D]
                for out, col in ((k_out, 0), (v_out, D)):
                    both = odd and col == 0
                    nc.tensor.matmul(out, main, wmain[:, col:col + D], start=True, stop=False)
                    ins = nc.tensor.matmul(out, mmask, bmain[:, col:col + D], start=False, stop=not both)
                    if both:
                        nc.tensor.matmul(out, dca, wdca[:, 0:D], start=False, stop=False)
                        ins = nc.tensor.matmul(out, dmask, bdca[:, 0:D], start=False, stop=True)
                if odd:
                    nc.tensor.matmul(vd_out, dca, wdca[:, D:2 * D], start=True, stop=False)
                    ins = nc.tensor.matmul(vd_out, dmask, bdca[:, D:2 * D], start=False, stop=True)
                ins.then_inc(k_ps, 1)
            pe.wait_ge(v_copied, NT)
            for i in range(NT + 1):
                if i == K_TURN + 1:
                    for s in K_SPLITS:
                        split_tensor(nc, pe, m, s, tm_done, rest_ready).then_inc(split_ps, 1)
                if i < NT:
                    pe.wait_ge(xn_ready, i + 1)
                    if i >= 2:
                        pe.wait_ge(xt_ready, i - 1)
                    transpose_tile(nc, m, 2 + i % 2, m.xn[:, i, :]).then_inc(xt_ps, 1)
                if i >= 1:
                    t = i - 1
                    pe.wait_ge(xt_ready, t + 1)
                    if t >= 2:
                        pe.wait_ge(cent, NT + t - 1)
                    matmul_tile(nc, ps[:, 4 + t % 2, 0:D], m.xT, t, wq, bq[:], m.ones_row[:]).then_inc(q_ps, 1)
            for s in Q_SPLITS:
                split_tensor(nc, pe, m, s, tm_done, rest_ready).then_inc(split_ps, 1)

        HH = NT // 2 * H

        def half_heads(tiles, th):
            return tiles[:, 4 * th:4 * th + 4, :].rearrange("p i (h e) -> p (i h) e", h=H)

        def token_major(n):
            return (m.k_tm if n < NT else m.q_tm)[:, n % NT, :]

        @block.vector
        def _(dve):
            chain = Chain(dve, step)
            link, v = chain.link, nc.vector
            def sum_squares(n):
                dve.wait_ge(squared, n + 1)
                nc.vector.tensor_reduce(hvar[:, n // NT, n % NT, :], sq[:, n % 2, :].rearrange("p (h e) -> p h e", h=H),
                                        AX_X, ALU.add).then_inc(squares_summed, 1)

            link(v.memset(ctxT_dca[:], 0.0))
            tail = m.ctxT[:].rearrange("p (b s) -> p b s", b=B)[:, :, MAIN:S]
            link(v.tensor_copy(ctxT_dca[:, :, P - DCA:P], tail))
            v.memset(tail, 0.0).then_inc(ctx_ready, 1)
            layernorm_vector(nc, dve, chain, m, 1e-5, root_in, root_out, xn_ready)

            def heads(ap):
                return ap.rearrange("p (h e) -> p h e", h=H)

            for side in range(2):
                for n in range(side * NT, (side + 1) * NT):
                    if n == NT + K_TURN:
                        split_vector(nc, dve, m, K_SPLITS, hi_ready, lo_ready, rest_ready)
                    i = n % NT
                    dve.wait_ge(q_ps if side else k_ps, i + 1)
                    src = heads(ps[:, 4 * side + i % 2, 0:D])
                    link(v.tensor_reduce(hvar[:, side, i, :], src, AX_X, ALU.add))
                    link(v.tensor_scalar(hmean[:, side, i, :], hvar[:, side, i, :], 1.0 / hd, None, ALU.mult))
                    v.tensor_tensor(heads(token_major(n)), src, bcast(hmean[:, side, i, :], 2, hd), ALU.subtract
                                    ).then_inc(cent, 1)
                    if i >= 1:
                        sum_squares(n - 1)
                sum_squares((side + 1) * NT - 1)
                dve.wait_ge(squares_summed, NT * (side + 1))
                flat = hvar[:, side, :, :].rearrange("p i h -> p (i h)")
                link(v.tensor_scalar(hwork[:, side, 0, :], flat, 1.0 / hd, 1e-6, ALU.mult, ALU.add))
                rsqrt_vector(nc, dve, chain, hwork[:, side, 0, :], None, [hwork[:, side, j, :] for j in range(4)],
                             hroot_in, hroot_out, side + 1)
                for th in range(2):
                    r = bcast(hwork[:, side, 2, th * HH:(th + 1) * HH], 2, hd)
                    tiles = half_heads(m.q_tm if side else m.k_tm, th)
                    ins = v.tensor_tensor(tiles, tiles, r, ALU.mult)
                    if side:
                        link(ins)
                        ins = v.tensor_tensor(tiles, tiles, bcast(nw[:, 0, :], 1, HH), ALU.mult)
                    ins.then_inc(scaled_done, 1)
            split_vector(nc, dve, m, Q_SPLITS, hi_ready, lo_ready, rest_ready)

        @block.scalar
        def _(act):
            layernorm_scalar(nc, act, m, root_in, root_out)
            act.wait_ge(v_set, 1)

            def square(n):
                act.wait_ge(cent, n + 1)
                if n >= 2:
                    act.wait_ge(squares_summed, n - 1)
                nc.scalar.activation(sq[:, n % 2, :], token_major(n), ACT.Square).then_inc(squared, 1)

            def roots(side):
                act.wait_ge(hroot_in, side + 1)
                nc.scalar.activation(hwork[:, side, 1, :], hwork[:, side, 3, :], ACT.Sqrt).then_inc(hroot_out, 1)

            for i in range(NT):
                act.wait_ge(k_ps, i + 1)
                for a in range(1 + i % 2):
                    ins = nc.scalar.copy(m.v1[:, i, :, a * (hd + 1):a * (hd + 1) + hd],
                                         ps[:, 2 + i % 2, a * D:(a + 1) * D].rearrange("p (h e) -> p h e", h=H))
                ins.then_inc(v_copied, 1)
                square(i)
            roots(0)
            for i in range(NT + 1):
                if i == K_TURN + 1:
                    split_scalar(nc, act, m, K_SPLITS, split_ps, part_dma, hi_ready, rest_ready, mid_ready)
                if i < NT:
                    act.wait_ge(xt_ps, i + 1)
                    transposed_copy(nc, m, i, 2 + i % 2, m.xT).then_inc(xt_ready, 1)
                if i >= 1:
                    square(NT + i - 1)
            roots(1)
            split_scalar(nc, act, m, Q_SPLITS, split_ps, part_dma, hi_ready, rest_ready, mid_ready)

        @block.gpsimd
        def _(pool):
            nc.gpsimd.memset(m.v1[:], 0.0).then_inc(v_zeroed, 1)
            pool.wait_ge(v_zeroed, 1)
            pool.wait_ge(ld, 8 * 16)
            for i in range(NT):
                for a in range(2):
                    col = (a + 1) * (hd + 1) - 1
                    ins = nc.gpsimd.tensor_copy(m.v1[:, i, :, col], pmask[:, i % 2, a:a + 1].broadcast_to([P, H]))
            ins.then_inc(v_set, 1)
            pool.wait_ge(ld_norm, 8 * 16)

            def heads(ap):
                return ap.rearrange("p (h e) -> p h e", h=H)

            for n in range(NT):
                row = 1 + n % 2
                tile = heads(m.k_tm[:, n, :])
                pool.wait_ge(scaled_done, n // 4 + 1)
                nc.gpsimd.tensor_tensor(tile, tile, bcast(nw[:, row, :], 1, H), ALU.mult).then_inc(pool_step, 1)
                pool.wait_ge(pool_step, n + 1)
                nc.gpsimd.tensor_tensor(tile, tile, bcast(nb[:, row, :], 1, H), ALU.add).then_inc(tm_done, 1)
            split_gpsimd(nc, pool, m, K_SPLITS, mid_ready, rest_ready, part_dma, lo_ready)
            for th in range(2):
                tiles = half_heads(m.q_tm, th)
                pool.wait_ge(scaled_done, 2 + th + 1)
                nc.gpsimd.tensor_tensor(tiles, tiles, bcast(nb[:, 0, :], 1, HH), ALU.add).then_inc(tm_done, 4)
            split_gpsimd(nc, pool, m, Q_SPLITS, mid_ready, rest_ready, part_dma, lo_ready)


E1, I1, TOP1 = 60, 176, 4
SH1 = 704 // I1
HC = I1 // 2
ROUND = 12
OVER = -(-(T * TOP1 // P) // ROUND) * ROUND
BLOCKS = E1 + OVER
RING = ROUND
PAIRS = ROUND // 2
ZEROED = (BLOCKS + OVER) // ROUND


def route_l1(nc, m, io):
    with ExitStack() as ctx:
        def sem(n):
            return m.sem("r1_" + n, ctx)

        def sb(n, shape, dt=F32):
            return m.sb("r1_" + n, [P] + shape, dt, ctx)
        NC = E1 + 1
        gw, iota = sb("gw", [KD, NC]), m.iota
        logit, prob = sb("logit", [NT, NC]), sb("prob", [NT, E1])
        top, total = sb("top", [NT]), sb("total", [NT])
        top8, idx8, idxf = m.topw, sb("idx8", [NT, 8], U32), sb("idxf", [NT, 8])
        hot = sb("hot", [TOP1, NT, E1])
        mask_bf = sb("mask_bf", [NT, E1], BF16)
        upper, upper_bf, ones_bf = sb("upper", [P]), sb("upper_bf", [P], BF16), sb("ones_bf", [P], BF16)
        count, marks, extra, incl = sb("count", [E1]), sb("marks", [NT]), sb("extra", [E1]), m.incl
        shift, slot_of, picked = sb("shift", [E1]), sb("slot_of", [NT, E1]), sb("picked", [TOP1, NT])
        many, ones_e = sb("many", [E1, NT - 1]), sb("ones_e", [E1])
        mask_ready, rank_ps = sem("mask_ready"), sem("rank_ps")
        ld, step, root_in, root_out, xn_ready, xt_ps, xt_ready, logit_ps, logit_ready, exp_in, exp_out = (
            sem(n) for n in ("ld", "step", "root_in", "root_out", "xn_ready", "xt_ps", "xt_ready", "logit_ps",
                             "logit_ready", "exp_in", "exp_out"))
        block = ctx.enter_context(nc.Block())

        @block.sync
        def _(sp):
            sp.dma_start(gw[:], io["L1_gates_T"].rearrange("(c p) n -> p c n", p=P)).then_inc(ld, 16)
            sp.dma_start(m.iota[:], io["iota"].partition_broadcast(P)).then_inc(ld, 16)
            sp.dma_start(upper[:], io["upper"]).then_inc(ld, 16)
            load_shared(sp, m, io, 0)

        @block.tensor
        def _(pe):
            pe.wait_ge(ld, 48)
            transpose_and_project(nc, pe, m, xn_ready, xt_ps, xt_ready, gw, NC, logit_ps)
            pe.wait_ge(mask_ready, 1)
            for i in range(NT):
                for j in range(i + 1):
                    nc.tensor.matmul(m.ps[:, 3, i * E1:(i + 1) * E1], (upper_bf if j == i else ones_bf)[:],
                                     mask_bf[:, j, :], start=(j == 0), stop=(j == i))
            for j in range(NT):
                ins = nc.tensor.matmul(m.ps[:, 4, 0:E1], ones_bf[:], mask_bf[:, j, :],
                                       start=(j == 0), stop=(j == NT - 1))
            ins.then_inc(rank_ps, 1)

        @block.scalar
        def _(act):
            layernorm_scalar(nc, act, m, root_in, root_out)
            for i in range(NT):
                act.wait_ge(xt_ps, i + 1)
                transposed_copy(nc, m, i, i % 2, m.xT).then_inc(xt_ready, 1)
            act.wait_ge(logit_ready, 1)
            nc.scalar.activation(m.gate[:], logit[:, :, E1], ACT.Sigmoid)
            act.wait_ge(exp_in, 1)
            nc.scalar.activation(hot[:, 1, :, :], hot[:, 0, :, :], ACT.Exp).then_inc(exp_out, 1)

        @block.vector
        def _(dve):
            chain = Chain(dve, step)
            link, v = chain.link, nc.vector
            layernorm_vector(nc, dve, chain, m, 1e-5, root_in, root_out, xn_ready)
            dve.wait_ge(ld, 48)
            v.tensor_copy(upper_bf[:], upper[:])
            v.memset(ones_bf[:], 1.0)
            v.memset(ones_e[:], 1.0)
            v.tensor_scalar(marks[:], iota[:, 1:1 + NT], float(P), None, ALU.mult)
            dve.wait_ge(logit_ps, 1)
            v.tensor_copy(logit[:].rearrange("p i e -> p (i e)"), m.ps[:, 2, 0:NT * NC]).then_inc(logit_ready, 1)
            dve.wait_ge(logit_ready, 1)
            lg = logit[:, :, 0:E1]
            link(v.tensor_reduce(top[:], lg, AX_X, ALU.max))
            v.tensor_tensor(hot[:, 0, :, :], lg, bcast(top[:], 2, E1), ALU.subtract).then_inc(exp_in, 1)
            dve.wait_ge(exp_out, 1)
            link(v.tensor_reduce(total[:], hot[:, 1, :, :], AX_X, ALU.add))
            link(v.reciprocal(top[:], total[:]))
            link(v.tensor_tensor(prob[:], hot[:, 1, :, :], bcast(top[:], 2, E1), ALU.mult))
            top_indices(nc, link, prob, top8, idx8, idxf)
            for j in range(TOP1):
                ins = v.tensor_tensor(hot[:, j, :, :], bcast(iota[:, 0:E1], 1, NT), bcast(idxf[:, :, j], 2, E1),
                                      ALU.is_equal)
            link(ins)
            v.tensor_tensor(slot_of[:], hot[:, 0, :, :], hot[:, 1, :, :], ALU.add)
            link(v.tensor_tensor(prob[:], hot[:, 2, :, :], hot[:, 3, :, :], ALU.add))
            v.tensor_tensor(mask_bf[:], slot_of[:], prob[:], ALU.add).then_inc(mask_ready, 1)
            dve.wait_ge(rank_ps, 1)
            link(v.tensor_copy(count[:], m.ps[:, 4, 0:E1]))
            link(v.tensor_tensor(many[:], bcast(count[:], 2, NT - 1), bcast(marks[:, 0:NT - 1], 1, E1), ALU.is_gt))
            link(v.tensor_reduce(extra[:], many[:], AX_X, ALU.add))
            link(v.tensor_tensor_scan(incl[:], ones_e[:], extra[:], 0.0, ALU.mult, ALU.add))
            link(v.tensor_tensor(count[:], incl[:], extra[:], ALU.subtract))
            link(v.tensor_tensor(extra[:], count[:], iota[:, 0:E1], ALU.subtract))
            link(v.tensor_scalar(shift[:], extra[:], float(E1 - 1), float(P), ALU.add, ALU.mult))
            rank = m.ps[:, 3, 0:NT * E1].rearrange("p (i e) -> p i e", i=NT)
            link(v.tensor_scalar(prob[:], rank, float(P), None, ALU.is_ge))
            link(v.tensor_tensor(slot_of[:], prob[:], bcast(shift[:], 1, NT), ALU.mult))
            link(v.tensor_tensor(prob[:], slot_of[:], rank, ALU.add))
            link(v.scalar_tensor_tensor(slot_of[:], bcast(iota[:, 0:E1], 1, NT), float(P), prob[:], ALU.mult, ALU.add))
            link(v.tensor_tensor(hot[:], hot[:], bcast(slot_of[:], 1, TOP1), ALU.mult))
            link(v.tensor_reduce(picked[:], hot[:], AX_X, ALU.add))
            link(v.tensor_copy(m.slot[:], picked[:]))


def further_blocks(nc, link, m):
    v, iota, incl, over_cmp, over_f = nc.vector, m.iota, m.incl, m.over_cmp, m.over_f
    link(v.tensor_tensor(over_cmp[:], bcast(incl[:], 1, OVER), bcast(iota[:, 0:OVER], 2, E1), ALU.is_le))
    link(v.tensor_reduce(over_f[:, 1:1 + OVER], over_cmp[:], AX_X, ALU.add))
    v.tensor_copy(over_f[:, 0:1], incl[:, E1 - 1:E1])
    link(v.tensor_scalar(over_cmp[:, 0, 0:OVER], over_f[:, 1:1 + OVER], float(E1 - 1), None, ALU.min))
    v.tensor_copy(m.over[:, 0:1], over_f[0:1, 0:1])
    v.tensor_copy(m.over[:, 1:1 + OVER], over_cmp[0:1, 0, 0:OVER])


def load_weights(eng, m, io, e, n, pair):
    eng.dma_start(m.ew13[:, 2 * pair:2 * pair + n, :, :],
                  io["L1_w13"][bass.ds(e, n), :, :].rearrange("a (c p) n -> p a c n", p=P)
                  ).then_inc(m.ew_loaded[pair], 16)
    eng.dma_start(m.ew2[:, 2 * pair:2 * pair + n, :, :],
                  io["L1_w2"][bass.ds(e, n), :, :].rearrange("a (c p) n -> p a c n", p=HC)
                  ).then_inc(m.ew_loaded[pair], 16)


def dispatch_l1(nc, pool, m, sent):
    pool.wait_ge(m.zeroed, 16 * ZEROED)
    for i in range(NT):
        for j in range(TOP1):
            nc.gpsimd.indirect_dma_start(m.x_slots, bass.IndirectOffsetOnAxis(m.slot[:, j, i:i + 1], 0),
                                         m.xn[:, i, :], None).then_inc(sent, 16)
    pool.wait_ge(sent, 16 * NT * TOP1)


FETCHES = 8
PICKS = [(i, j) for i in range(NT) for j in range(TOP1)]


def fetch_outputs(nc, pool, m, yg, fetched, combined):
    for n, (i, j) in enumerate(PICKS):
        if n >= FETCHES:
            pool.wait_ge(combined, n - FETCHES + 1)
        nc.gpsimd.indirect_dma_start(yg[:, n % FETCHES, :], None, m.y_slots,
                                     bass.IndirectOffsetOnAxis(m.slot[:, j, i:i + 1], 0)
                                     ).then_inc(fetched[n % FETCHES], 16)


def load_shared(sp, m, io, half):
    for j in range(2):
        e = 2 * half + j
        sp.dma_start(m.sw13[:, j, :, :], io["L1_shared_w13"][e].rearrange("(c p) n -> p c n", p=P)
                     ).then_inc(m.sw_loaded[j], 16)
        sp.dma_start(m.sw2[:, j, :, :], io["L1_shared_w2"][e].rearrange("(c p) n -> p c n", p=HC)
                     ).then_inc(m.sw_loaded[j], 16)


def shared_l1(nc, m, half):
    with ExitStack() as ctx:
        def sem(n):
            return m.sem(f"f{half + 3}_{n}", ctx)
        name = f"f{half + 3}_"
        w13, w2 = m.sw13, m.sw2
        act_g = m.sb(name + "act_g", [P, 2, I1], ctx=ctx)
        hid = m.sb(name + "hid", [P, 2, I1], ctx=ctx)
        hidT = m.sb(name + "hidT", [HC, 2, 2 * P], ctx=ctx)
        gu_ps, silu_done, hid_done, ht_ps, ht_done, y_ps, added = (sem(n) for n in (
            "gu_ps", "silu_done", "hid_done", "ht_ps", "ht_done", "y_ps", "added"))
        if half == 0:
            sent, step = sem("sent"), sem("step")
        else:
            yg = m.sb("yg", [P, FETCHES, D], ctx=ctx)
            fetched = [sem(f"fetched{b}") for b in range(FETCHES)]
            combined = sem("combined")
        STEPS = SH1 // 2 * NT
        ps = m.ps
        block = ctx.enter_context(nc.Block())

        @block.gpsimd
        def _(pool):
            if half == 0:
                dispatch_l1(nc, pool, m, sent)
            else:
                fetch_outputs(nc, pool, m, yg, fetched, combined)

        @block.tensor
        def _(pe):
            def gate_up(k):
                part, i = k // NT, k % NT
                if i == 0:
                    pe.wait_ge(m.sw_loaded[part], 32 * (half + 1))
                if k >= 2:
                    pe.wait_ge(hid_done, k - 1)
                for c in range(KD):
                    ins = nc.tensor.matmul(ps[:, k % 2, 0:2 * I1], m.xT[:, c, i * P:(i + 1) * P], w13[:, part, c, :],
                                           start=(c == 0), stop=(c == KD - 1))
                ins.then_inc(gu_ps, 1)

            def turn(k):
                pe.wait_ge(hid_done, k + 1)
                if k >= 2:
                    pe.wait_ge(ht_done, k - 1)
                for c in range(2):
                    ins = nc.tensor.transpose(ps[0:HC, 2 + k % 2, c * P:(c + 1) * P],
                                              hid[:, k % 2, c * HC:(c + 1) * HC], m.ident[:])
                ins.then_inc(ht_ps, 1)

            def outputs(k):
                pe.wait_ge(ht_done, k + 1)
                if k >= 2:
                    pe.wait_ge(added, k - 1)
                for c in range(2):
                    ins = nc.tensor.matmul(ps[:, 4 + k % 2, 0:D], hidT[:, k % 2, c * P:(c + 1) * P],
                                           w2[:, k // NT, c, :], start=(c == 0), stop=(c == 1))
                ins.then_inc(y_ps, 1)

            gate_up(0)
            gate_up(1)
            turn(0)
            for k in range(STEPS):
                if k + 2 < STEPS:
                    gate_up(k + 2)
                if k + 1 < STEPS:
                    turn(k + 1)
                outputs(k)

        @block.scalar
        def _(act):
            def silu(k):
                act.wait_ge(gu_ps, k + 1)
                if k >= 2:
                    act.wait_ge(hid_done, k - 1)
                nc.scalar.activation(act_g[:, k % 2, :], ps[:, k % 2, 0:I1], ACT.Silu).then_inc(silu_done, 1)

            silu(0)
            silu(1)
            for k in range(STEPS):
                act.wait_ge(ht_ps, k + 1)
                if k >= 2:
                    act.wait_ge(y_ps, k - 1)
                nc.scalar.copy(hidT[:, k % 2, :], ps[0:HC, 2 + k % 2, 0:2 * P]).then_inc(ht_done, 1)
                if k + 2 < STEPS:
                    silu(k + 2)

        @block.vector
        def _(dve):
            def multiply(k):
                dve.wait_ge(silu_done, k + 1)
                if k >= 2:
                    dve.wait_ge(ht_ps, k - 1)
                nc.vector.tensor_tensor(hid[:, k % 2, :], act_g[:, k % 2, :], ps[:, k % 2, I1:2 * I1], ALU.mult
                                        ).then_inc(hid_done, 1)

            def combine(n, steps):
                i, j = PICKS[n]
                dve.wait_ge(fetched[n % FETCHES], 16 * (n // FETCHES + 1))
                dve.wait_ge(added, steps)
                if n >= 1:
                    dve.wait_ge(combined, n)
                nc.vector.scalar_tensor_tensor(m.xs[:, i, :], yg[:, n % FETCHES, :], m.topw[:, i, j:j + 1],
                                               m.xs[:, i, :], ALU.mult, ALU.add).then_inc(combined, 1)

            per_step = len(PICKS) // STEPS
            multiply(0)
            multiply(1)
            for k in range(STEPS):
                if k + 2 < STEPS:
                    multiply(k + 2)
                if half == 1 and k >= 1:
                    for n in range(per_step * (k - 1), per_step * k):
                        combine(n, k)
                i = k % NT
                dve.wait_ge(y_ps, k + 1)
                if half == 1 and k >= 1:
                    dve.wait_ge(combined, per_step * k)
                nc.vector.scalar_tensor_tensor(m.xs[:, i, :], ps[:, 4 + k % 2, 0:D], m.gate[:, i:i + 1],
                                               m.xs[:, i, :], ALU.mult, ALU.add).then_inc(added, 1)
                if half == 0 and k == NT:
                    further_blocks(nc, Chain(dve, step).link, m)
            if half == 1:
                for n in range(per_step * (STEPS - 1), len(PICKS)):
                    combine(n, STEPS)


def routed_l1(nc, m, io):
    with ExitStack() as ctx:
        def sem(n):
            return m.sem("f2_" + n, ctx)
        xg = m.sb("f2_xg", [P, 6, D], ctx=ctx)
        xgT = m.sb("f2_xgT", [P, 4, D], ctx=ctx)
        act_g = m.sb("f2_act_g", [P, 2, I1], ctx=ctx)
        hid = m.sb("f2_hid", [P, 2, I1], ctx=ctx)
        hidT = m.sb("f2_hidT", [HC, 2, 2 * P], ctx=ctx)
        yb = m.sb("f2_yb", [P, 4, D], ctx=ctx)
        x_loaded = [sem(f"x_loaded{j}") for j in range(3)]
        y_stored = [sem("y_stored0"), sem("y_stored1")]
        over_loaded = [sem(f"over_loaded{j}") for j in range(PAIRS)]
        xt_ps, xt_done, gu_ps, silu_done, hid_done, ht_ps, ht_done, y_ps, y_done = (sem(n) for n in (
            "xt_ps", "xt_done", "gu_ps", "silu_done", "hid_done", "ht_ps", "ht_done", "y_ps", "y_done"))
        block = ctx.enter_context(nc.Block())
        ps = m.ps
        FIXED, FURTHER = E1 // ROUND, OVER // ROUND
        further = []

        def all_rounds(eng, prologue, body):
            blocks = eng.value_load(m.over[0:1, 0:1], min_val=0, max_val=OVER)
            further.append(blocks)
            prologue(0)
            rounds(eng, FIXED, body)
            for r in range(FURTHER):
                with eng.If(blocks > r * ROUND):
                    prologue(FIXED + r)
                    body(FIXED + r, False, True)

        @block.sync
        def _(sp):
            def load_x(g, h):
                rows = m.x_slots[bass.ds((ROUND * g + 2 * h) * P, 2 * P), :]
                sp.dma_start(xg[:, 2 * (h % 3):2 * (h % 3) + 2, :], rows.rearrange("(b p) d -> p b d", p=P)
                             ).then_inc(x_loaded[h % 3], 16)

            def store_y(g, h):
                sp.wait_ge(y_done, ROUND * g + 2 * h + 2)
                rows = m.y_slots[bass.ds((ROUND * g + 2 * h) * P, 2 * P), :]
                sp.dma_start(rows.rearrange("(b p) d -> p b d", p=P), yb[:, 2 * (h % 2):2 * (h % 2) + 2, :]
                             ).then_inc(y_stored[h % 2], 16)

            def load_further(r, h):
                sp.wait_ge(y_ps, ROUND * (FIXED + r - 1) + 2 * h + 2)
                for b in range(2):
                    o = ROUND * r + 2 * h + b
                    e = sp.value_load(m.over[0:1, 1 + o:2 + o], min_val=0, max_val=E1 - 1)
                    for w, dram, pp in ((m.ew13, "L1_w13", P), (m.ew2, "L1_w2", HC)):
                        sp.dma_start(w[:, 2 * h + b, :, :],
                                     io[dram][bass.ds(e, 1), :, :].rearrange("a (c p) n -> p (a c) n", p=pp)
                                     ).then_inc(over_loaded[h], 16)

            def prologue(g):
                load_x(g, 0)
                load_x(g, 1)
                if g > FIXED:
                    for h in range(PAIRS):
                        load_further(g - FIXED, h)

            def body(g, first, last):
                for h in range(PAIRS):
                    if not (first and h == 0):
                        sp.wait_ge(xt_ps, ROUND * g + 2 * h)
                    if h < PAIRS - 2:
                        load_x(g, h + 2)
                    elif not last:
                        load_x(g + 1, h + 2 - PAIRS)
                    if not (first and h == 0):
                        sp.wait_ge(y_ps, ROUND * g + 2 * h)
                    if not isinstance(g, int) or g < FIXED:
                        if h >= 1:
                            if not last:
                                load_weights(sp, m, io, ROUND * (g + 1) + 2 * (h - 1), 2, h - 1)
                            else:
                                with sp.If(further[-1] > 0):
                                    load_further(0, h - 1)
                        elif not first:
                            load_weights(sp, m, io, ROUND * g + 2 * (PAIRS - 1), 2, PAIRS - 1)
                    if h >= 1:
                        store_y(g, h - 1)
                    elif not first and not (isinstance(g, int) and g >= FIXED):
                        store_y(g - 1, PAIRS - 1)
                if last:
                    store_y(g, PAIRS - 1)
                    if g == FIXED - 1:
                        with sp.If(further[-1] > 0):
                            load_further(0, PAIRS - 1)
                    for a in range(2):
                        sp.wait_ge(y_stored[a], 16 * (PAIRS // 2) * (g + 1))
            load_shared(sp, m, io, 1)
            all_rounds(sp, prologue, body)

        @block.tensor
        def _(pe):
            def turn_x(g, k, first):
                n, h = ROUND * g + k, (k // 2) % PAIRS
                gg, kk = (g, k) if k < ROUND else (g + 1, k - ROUND)
                if kk % 2 == 0:
                    pe.wait_ge(x_loaded[h % 3], 16 * ((PAIRS // 3) * gg + kk // 6 + 1))
                if not (first and k < 2):
                    pe.wait_ge(xt_done, n - 1)
                for c in range(KD):
                    ins = nc.tensor.transpose(ps[:, 6 + k % 2, c * P:(c + 1) * P], xg[:, k % 6, c * P:(c + 1) * P],
                                              m.ident[:])
                ins.then_inc(xt_ps, 1)

            def gate_up(g, k, first):
                n, slot = ROUND * g + k, k % ROUND
                gg, kk = (g, k) if k < ROUND else (g + 1, k - ROUND)
                if kk % 2 == 0:
                    if isinstance(gg, int) and gg >= FIXED:
                        pe.wait_ge(over_loaded[slot // 2], 64 * (gg - FIXED + 1))
                    else:
                        pe.wait_ge(m.ew_loaded[slot // 2], 32 * (gg + 1))
                pe.wait_ge(xt_done, n + 1)
                if not (first and k < 2):
                    pe.wait_ge(hid_done, n - 1)
                for c in range(KD):
                    ins = nc.tensor.matmul(ps[:, k % 2, 0:2 * I1], xgT[:, k % 4, c * P:(c + 1) * P],
                                           m.ew13[:, slot, c, :], start=(c == 0), stop=(c == KD - 1))
                ins.then_inc(gu_ps, 1)

            def turn_hid(g, k, first):
                n = ROUND * g + k
                pe.wait_ge(hid_done, n + 1)
                if not (first and k < 2):
                    pe.wait_ge(ht_done, n - 1)
                for c in range(2):
                    ins = nc.tensor.transpose(ps[0:HC, 2 + k % 2, c * P:(c + 1) * P],
                                              hid[:, k % 2, c * HC:(c + 1) * HC], m.ident[:])
                ins.then_inc(ht_ps, 1)

            def outputs(g, k, first):
                n = ROUND * g + k
                pe.wait_ge(ht_done, n + 1)
                if not (first and k < 2):
                    pe.wait_ge(y_done, n - 1)
                for c in range(2):
                    ins = nc.tensor.matmul(ps[:, 4 + k % 2, 0:D], hidT[:, k % 2, c * P:(c + 1) * P],
                                           m.ew2[:, k, c, :], start=(c == 0), stop=(c == 1))
                ins.then_inc(y_ps, 1)

            def prologue(g):
                first = g == 0
                for k in range(3):
                    turn_x(g, k, first)
                gate_up(g, 0, first)
                gate_up(g, 1, first)
                turn_hid(g, 0, first)

            def body(g, first, last):
                for k in range(ROUND):
                    if not (last and k + 3 >= ROUND):
                        turn_x(g, k + 3, first)
                    if not (last and k + 2 >= ROUND):
                        gate_up(g, k + 2, first)
                    if not (last and k + 1 >= ROUND):
                        turn_hid(g, k + 1, first)
                    outputs(g, k, first)
            all_rounds(pe, prologue, body)

        @block.scalar
        def _(act):
            def copy_x(g, k, first):
                n = ROUND * g + k
                act.wait_ge(xt_ps, n + 1)
                if not (first and k < 4):
                    act.wait_ge(gu_ps, n - 3)
                nc.scalar.copy(xgT[:, k % 4, :], ps[:, 6 + k % 2, 0:D]).then_inc(xt_done, 1)

            def silu(g, k, first):
                n = ROUND * g + k
                act.wait_ge(gu_ps, n + 1)
                if not (first and k < 2):
                    act.wait_ge(hid_done, n - 1)
                nc.scalar.activation(act_g[:, k % 2, :], ps[:, k % 2, 0:I1], ACT.Silu).then_inc(silu_done, 1)

            def prologue(g):
                first = g == 0
                for k in range(3):
                    copy_x(g, k, first)
                silu(g, 0, first)
                silu(g, 1, first)

            def body(g, first, last):
                for k in range(ROUND):
                    n = ROUND * g + k
                    act.wait_ge(ht_ps, n + 1)
                    if not (first and k < 2):
                        act.wait_ge(y_ps, n - 1)
                    nc.scalar.copy(hidT[:, k % 2, :], ps[0:HC, 2 + k % 2, 0:2 * P]).then_inc(ht_done, 1)
                    if not (last and k + 3 >= ROUND):
                        copy_x(g, k + 3, first)
                    if not (last and k + 2 >= ROUND):
                        silu(g, k + 2, first)
            all_rounds(act, prologue, body)

        @block.vector
        def _(dve):
            def multiply(g, k, first):
                n = ROUND * g + k
                dve.wait_ge(silu_done, n + 1)
                if not (first and k < 2):
                    dve.wait_ge(ht_ps, n - 1)
                nc.vector.tensor_tensor(hid[:, k % 2, :], act_g[:, k % 2, :], ps[:, k % 2, I1:2 * I1], ALU.mult
                                        ).then_inc(hid_done, 1)

            def prologue(g):
                multiply(g, 0, g == 0)
                multiply(g, 1, g == 0)

            def body(g, first, last):
                for k in range(ROUND):
                    if not (last and k + 2 >= ROUND):
                        multiply(g, k + 2, first)
                    dve.wait_ge(y_ps, ROUND * g + k + 1)
                    if k % 2 == 0 and not (first and k < 4):
                        dve.wait_ge(y_stored[(k // 2) % 2], 16 * ((PAIRS // 2) * g + k // 4))
                    nc.vector.tensor_copy(yb[:, k % 4, :], ps[:, 4 + k % 2, 0:D]).then_inc(y_done, 1)
            all_rounds(dve, prologue, body)


def store(nc, m, out):
    with ExitStack() as ctx:
        block = ctx.enter_context(nc.Block())

        @block.sync
        def _(sp):
            sp.dma_start(out.rearrange("b (i p) d -> p (b i) d", p=P), m.xs[:]).then_inc(m.stored, 16)
            sp.wait_ge(m.stored, 16)


def build(nc, io, out):
    with ExitStack() as ctx:
        m = Mem(nc, ctx)
        m.xs = m.sb("xs", [P, NT, D])
        m.xn = m.sb("xn", [P, NT, D])
        m.xT = m.sb("xT", [P, KD, T])
        m.bn = m.sb("bn", [P, NT, 6])
        m.mv = m.sb("mv", [P, NT, 2])
        m.rstd = m.sb("rstd", [P, 4, NT])
        m.ident = m.sb("ident", [P, P])
        m.ident_bf = m.sb("ident_bf", [P, P], BF16)
        m.ones_row = m.sb("ones_row", [1, P])
        m.comb = m.sb("comb", [P, NT, X0])
        m.gate = m.sb("gate", [P, NT])
        m.ew13 = m.sb("ew13", [P, RING, KD, 2 * I1])
        m.ew2 = m.sb("ew2", [HC, RING, 2, D])
        m.ew_loaded = [m.sem(f"ew_loaded{j}") for j in range(RING // 2)]
        m.zeroed, m.stored = m.sem("zeroed"), m.sem("stored")
        m.sw_loaded = [m.sem(f"sw_loaded{j}") for j in range(2)]
        m.part_dma = {lay.name: [m.sem(f"{lay.name}_part_dma{b}") for b in range(SB)] for lay in (L0, L1)}
        m.ones_ld = {lay.name: m.sem(lay.name + "_ones_ld") for lay in (L0, L1)}
        m.slot = m.sb("slot", [P, TOP1, NT], U32)
        m.topw = m.sb("topw", [P, NT, 8])
        m.over = m.sb("over", [1, 1 + OVER], U32)
        m.x_slots = nc.dram_tensor("x_slots", [BLOCKS * P, D], F32, kind="Internal").ap()
        m.y_slots = nc.dram_tensor("y_slots", [BLOCKS * P, D], F32, kind="Internal").ap()
        m.ps = ctx.enter_context(nc.psum_tensor("ps", [P, 8, 512], F32))
        m.stacks = {n: nc.dram_tensor(n + "_stacks", [D, PARTS, T], BF16, kind="Internal").ap() for n in ("q", "k")}
        with ExitStack() as scope:
            m.ctxT = m.sb("ctxT_sb", [CD, T], ctx=scope)
            m.k_tm = m.sb("k_tm", [P, NT, D], ctx=scope)
            m.q_tm = m.sb("q_tm", [P, NT, D], ctx=scope)
            m.attn = m.sb("attn", [P, NT, D], ctx=scope)
            m.rest = m.sb("rest", [P, SB, SW], ctx=scope)
            m.part = m.sb("part", [P, SB, 3, SW], BF16, ctx=scope)
            with ExitStack() as layer:
                m.v0 = m.sb("v0", [P, NT, L0.heads, L0.hd + 1], ctx=layer)
                prep_l0(nc, m, io)
                m.old_sems, m.stage_sems = m.stage_sems, []
                attention(nc, m, L0, io)
            attention_output(nc, m, "o0_", io["L0_xattn_Wout"], io["L0_xattn_bout"])
            m.old_sems, m.stage_sems = m.stage_sems, []
            with ExitStack() as layer:
                m.f0_up = m.sb("f0_up", [P, 2, KD, I0], ctx=layer)
                m.f0_down = m.sb("f0_down", [P, 2, D], ctx=layer)
                m.f0_loaded = [m.sem(f"f0_loaded{j}", layer) for j in range(2)]
                route_l0(nc, m, io)
                experts_l0(nc, m, io)
            with ExitStack() as layer:
                m.v1 = m.sb("v1", [P, NT, L1.heads, L1.vw], ctx=layer)
                prep_l1(nc, m, io)
                attention(nc, m, L1, io)
            attention_output(nc, m, "o1_", io["L1_xattn_Wo"], io["L1_xattn_bo"])
        m.sw13, m.sw2 = m.sb("sw13", [P, 2, KD, 2 * I1]), m.sb("sw2", [HC, 2, 2, D])
        with ExitStack() as scope:
            m.iota, m.incl = m.sb("iota", [P, P], ctx=scope), m.sb("incl", [P, E1], ctx=scope)
            m.over_cmp, m.over_f = (m.sb(n, [P] + shape, ctx=scope) for n, shape in (
                ("over_cmp", [OVER, E1]), ("over_f", [1 + OVER])))
            route_l1(nc, m, io)
            shared_l1(nc, m, 0)
        routed_l1(nc, m, io)
        shared_l1(nc, m, 1)
        store(nc, m, out)


def host_layout(inputs):
    io = {n: np.ascontiguousarray(a) for n, a in inputs.items()}
    io["ctxT"] = np.ascontiguousarray(np.asarray(io.pop("ctx_1024")).reshape(T, CD).T)
    io["ident"] = np.eye(P, dtype=np.float32)
    io["ones_row"] = np.ones((1, P), np.float32)
    io["l0_ones"] = np.ones((2, G, S), np.float32)
    keys = np.arange(S) < MAIN
    io["l1_ones"] = np.broadcast_to(np.stack([keys, keys, ~keys, ~keys])[:, None, :], (4, G, S)).astype(np.float32)
    io["tmask"] = np.stack([keys, ~keys]).astype(np.float32)[None]
    io["pmask"] = np.ascontiguousarray(io["tmask"].reshape(2, QT, P).transpose(2, 1, 0))
    io["iota"] = np.arange(P, dtype=np.float32)
    io["later"] = np.tril(np.ones((GRP, GRP), np.float32), -1)
    io["L0_router_T"] = np.ascontiguousarray(io["L0_ffn_router_weight"].T)
    up, down = io.pop("L0_ffn_shared_up"), io.pop("L0_ffn_shared_down")
    io["L0_up"] = np.concatenate([io.pop("L0_ffn_w_up"), up.reshape(D, SH0, I0).transpose(1, 0, 2)])
    io["L0_down"] = np.concatenate([io.pop("L0_ffn_w_down"), down.reshape(SH0, I0, D)])
    wmain = np.concatenate([io.pop("L1_xattn_Wk"), io.pop("L1_xattn_Wv")], axis=1)
    bmain = np.concatenate([io.pop("L1_xattn_bk"), io.pop("L1_xattn_bv")])[None]
    io["L1_wmain"], io["L1_bmain"] = (
        np.ascontiguousarray(a.reshape(-1, L1.heads, 2, L1.hd).transpose(0, 2, 1, 3).reshape(-1, 2 * D))
        for a in (wmain, bmain))
    io["L1_gates_T"] = np.concatenate([io.pop("L1_ffn_gate_w"), io.pop("L1_ffn_shared_gate_w")]).T.copy()
    gate_up, down = io.pop("L1_ffn_se_gate_up_w"), io.pop("L1_ffn_se_down_w")
    w13 = gate_up.reshape(2, SH1, I1, D).transpose(1, 0, 2, 3).reshape(SH1, 2 * I1, D)
    io["L1_shared_w13"] = w13.transpose(0, 2, 1).copy()
    io["L1_shared_w2"] = down.T.reshape(SH1, I1, D).copy()
    io["L1_w13"] = io.pop("L1_ffn_w13").transpose(0, 2, 1).copy()
    io["L1_w2"] = io.pop("L1_ffn_w2").transpose(0, 2, 1).copy()
    io["upper"] = np.triu(np.ones((P, P), np.float32), 1)
    return io


def kernel(**inputs):
    import concourse.bacc as bacc
    from concourse.bass_utils import run_bass_kernel_spmd

    arrays = host_layout(inputs)
    nc = bacc.Bacc("TRN2", target_bir_lowering=False, num_devices=1)
    io = {n: nc.dram_tensor("in_" + n, a.shape, mybir.dt.from_np(a.dtype), kind="ExternalInput").ap()
          for n, a in arrays.items()}
    out = nc.dram_tensor("out_x", (B, S, D), F32, kind="ExternalOutput").ap()
    build(nc, io, out)
    r = run_bass_kernel_spmd(nc, [{"in_" + n: a for n, a in arrays.items()}], core_ids=[0])
    return r.results[0]["out_x"]
```
